# Optimizing a Trainium2 kernel written in Bass

```python
import numpy as np
import jax
import jax.numpy as jnp

def _softmax(x, axis=-1):
    return jax.nn.softmax(x, axis=axis)

def _gelu(x):
    return jax.nn.gelu(x, approximate=True)

def _silu(x):
    return jax.nn.silu(x)

def _sigmoid(x):
    return jax.nn.sigmoid(x)

def _layernorm(x, axis=-1, eps=1e-05):
    m = jnp.mean(x, axis=axis, keepdims=True)
    v = jnp.var(x, axis=axis, keepdims=True)
    return (x - m) / jnp.sqrt(v + eps)

def _scatter_add(tgt, idx, src, axis=0):
    return tgt.at[idx].add(src)

def _segment_sum(src, seg, n):
    return jax.ops.segment_sum(src, seg, n)
kernel_name = 'mk_gps_d1_gnn_r8_08c565'

def setup_inputs(seed: int=0):
    np.random.seed(seed)
    _w = jnp.asarray

    def _rec_inputs():
        import jax
        import jax.numpy as jnp
        _gk = jax.random.key(seed)
        x = -0.0006008 + 1.001 * jax.random.normal(jax.random.fold_in(_gk, 1), (6250, 256), jnp.float32)
        src = jax.random.randint(jax.random.fold_in(_gk, 2), (100000,), 0, 6250, jnp.int32)
        dst = jax.random.randint(jax.random.fold_in(_gk, 3), (100000,), 0, 6250, jnp.int32)
        _o = jnp.argsort(dst, stable=True)
        src = src[_o]
        dst = dst[_o]
        edge_attr_64 = 5.96457e-05 + 0.999887 * jax.random.normal(jax.random.fold_in(_gk, 12), (100000, 64), jnp.float32)
        node_vec1 = jax.random.uniform(jax.random.fold_in(_gk, 13), (6250, 1), jnp.float32, 0.0, 0.999943)
        return (x, src, dst, edge_attr_64, node_vec1)
    x, src, dst, edge_attr_64, node_vec1 = _rec_inputs()

    def _L0_gnn_setup():
        import jax, jax.numpy as jnp
        import numpy as np
        N_NODES = 1250
        N_EDGES = 20000
        IN_FEATS = 256
        E_DIMS = 64
        NEG_SLOPE = 0.01
        key = jax.random.key(seed)
        ks = jax.random.split(key, 8)
        h = jax.random.normal(ks[0], (N_NODES, IN_FEATS), dtype=jnp.float32)
        w = jax.random.normal(ks[1], (N_EDGES, E_DIMS), dtype=jnp.float32)
        snorm_n = jax.random.uniform(ks[2], (N_NODES, 1), dtype=jnp.float32)
        edge_src = jax.random.randint(ks[3], (N_EDGES,), 0, N_NODES, dtype=jnp.int64)
        edge_dst = jax.random.randint(ks[4], (N_EDGES,), 0, N_NODES, dtype=jnp.int64)
        W_self = jax.random.normal(ks[5], (IN_FEATS, IN_FEATS), dtype=jnp.float32) * np.sqrt(2.0 / IN_FEATS)
        W_func = jax.random.normal(ks[6], (IN_FEATS, IN_FEATS), dtype=jnp.float32) * np.sqrt(2.0 / IN_FEATS)
        W_att = jax.random.normal(ks[7], (1, 2 * IN_FEATS + E_DIMS), dtype=jnp.float32) * np.sqrt(2.0 / (2 * IN_FEATS + E_DIMS))
        return {'h': h, 'w': w, 'snorm_n': snorm_n, 'edge_src': edge_src, 'edge_dst': edge_dst, 'W_self': W_self, 'W_func': W_func, 'W_att': W_att}
    _L0_gnn_all = _L0_gnn_setup()
    _L0_gnn_in = {k: v for k, v in _L0_gnn_all.items() if k in ('W_self', 'W_func', 'W_att')}
    del _L0_gnn_all

    def _L0_mix_setup():
        import jax, jax.numpy as jnp
        import numpy as np
        D_MODEL = 256
        NHEAD = 8
        D_HEAD = D_MODEL // NHEAD
        DIM_FF = 1024
        B, L = (4, 2048)
        LN_EPS = 1e-05

        def _layernorm(x, g, b):
            mu = jnp.mean(x, axis=-1, keepdims=True)
            var = jnp.mean((x - mu) ** 2, axis=-1, keepdims=True)
            return (x - mu) * jax.lax.rsqrt(var + LN_EPS) * g + b

        def _phi(x):
            return jnp.where(x > 0, x + 1.0, jnp.exp(x))
        key = jax.random.key(seed)
        ks = jax.random.split(key, 16)
        s_in = 1.0 / np.sqrt(D_MODEL)
        s_ff = 1.0 / np.sqrt(DIM_FF)
        inp = {'x': jax.random.normal(ks[0], (B, L, D_MODEL), dtype=jnp.float32), 'Wq': jax.random.normal(ks[1], (D_MODEL, D_MODEL), dtype=jnp.float32) * s_in, 'bq': jnp.zeros((D_MODEL,), jnp.float32), 'Wk': jax.random.normal(ks[2], (D_MODEL, D_MODEL), dtype=jnp.float32) * s_in, 'bk': jnp.zeros((D_MODEL,), jnp.float32), 'Wv': jax.random.normal(ks[3], (D_MODEL, D_MODEL), dtype=jnp.float32) * s_in, 'bv': jnp.zeros((D_MODEL,), jnp.float32), 'Wo': jax.random.normal(ks[4], (D_MODEL, D_MODEL), dtype=jnp.float32) * s_in, 'bo': jnp.zeros((D_MODEL,), jnp.float32), 'W1': jax.random.normal(ks[5], (D_MODEL, DIM_FF), dtype=jnp.float32) * s_in, 'b1': jnp.zeros((DIM_FF,), jnp.float32), 'W2': jax.random.normal(ks[6], (DIM_FF, D_MODEL), dtype=jnp.float32) * s_ff, 'b2': jnp.zeros((D_MODEL,), jnp.float32), 'ln1_g': jnp.ones((D_MODEL,), jnp.float32), 'ln1_b': jnp.zeros((D_MODEL,), jnp.float32), 'ln2_g': jnp.ones((D_MODEL,), jnp.float32), 'ln2_b': jnp.zeros((D_MODEL,), jnp.float32)}
        return inp
    _L0_mix_all = _L0_mix_setup()
    _L0_mix_in = {k: v for k, v in _L0_mix_all.items() if k in ('Wq', 'bq', 'Wk', 'bk', 'Wv', 'bv', 'Wo', 'bo', 'W1', 'b1', 'W2', 'b2', 'ln1_g', 'ln1_b', 'ln2_g', 'ln2_b')}
    del _L0_mix_all

    def _L0_ffn_setup():
        import jax, jax.numpy as jnp
        import numpy as np
        E, D, H, TOP_K = (6, 256, 256, 2)
        ROUTER_H = D // 2
        key = jax.random.key(seed)
        ks = jax.random.split(key, 12)
        s = 1.0 / np.sqrt(D)
        sh = 1.0 / np.sqrt(H)
        sr = 1.0 / np.sqrt(ROUTER_H)
        return {'features': jax.random.normal(ks[0], (8, 512, D), dtype=jnp.float32), 'router_w1': jax.random.uniform(ks[1], (D, ROUTER_H), jnp.float32, -s, s), 'router_b1': jnp.zeros((ROUTER_H,), jnp.float32), 'router_w2': jax.random.uniform(ks[2], (ROUTER_H, E), jnp.float32, -sr, sr), 'router_b2': jnp.zeros((E,), jnp.float32), 'expert_w1': jax.random.uniform(ks[3], (E, D, H), jnp.float32, -s, s), 'expert_b1': jnp.zeros((E, H), jnp.float32), 'expert_w2': jax.random.uniform(ks[4], (E, H, H), jnp.float32, -sh, sh), 'expert_b2': jnp.zeros((E, H), jnp.float32), 'expert_w3': jax.random.uniform(ks[5], (E, H, D), jnp.float32, -sh, sh), 'expert_b3': jnp.zeros((E, D), jnp.float32)}
    _L0_ffn_all = _L0_ffn_setup()
    _L0_ffn_in = {k: v for k, v in _L0_ffn_all.items() if k in ('router_w1', 'router_b1', 'router_w2', 'router_b2', 'expert_w1', 'expert_b1', 'expert_w2', 'expert_b2', 'expert_w3', 'expert_b3')}
    del _L0_ffn_all
    return {'x': x, 'src': src, 'dst': dst, 'edge_attr_64': edge_attr_64, 'node_vec1': node_vec1, 'L0_gnn_W_self': _L0_gnn_in['W_self'], 'L0_gnn_W_func': _L0_gnn_in['W_func'], 'L0_gnn_W_att': _L0_gnn_in['W_att'], 'L0_mix_Wq': _L0_mix_in['Wq'], 'L0_mix_bq': _L0_mix_in['bq'], 'L0_mix_Wk': _L0_mix_in['Wk'], 'L0_mix_bk': _L0_mix_in['bk'], 'L0_mix_Wv': _L0_mix_in['Wv'], 'L0_mix_bv': _L0_mix_in['bv'], 'L0_mix_Wo': _L0_mix_in['Wo'], 'L0_mix_bo': _L0_mix_in['bo'], 'L0_mix_W1': _L0_mix_in['W1'], 'L0_mix_b1': _L0_mix_in['b1'], 'L0_mix_W2': _L0_mix_in['W2'], 'L0_mix_b2': _L0_mix_in['b2'], 'L0_mix_ln1_g': _L0_mix_in['ln1_g'], 'L0_mix_ln1_b': _L0_mix_in['ln1_b'], 'L0_mix_ln2_g': _L0_mix_in['ln2_g'], 'L0_mix_ln2_b': _L0_mix_in['ln2_b'], 'L0_ffn_router_w1': _L0_ffn_in['router_w1'], 'L0_ffn_router_b1': _L0_ffn_in['router_b1'], 'L0_ffn_router_w2': _L0_ffn_in['router_w2'], 'L0_ffn_router_b2': _L0_ffn_in['router_b2'], 'L0_ffn_expert_w1': _L0_ffn_in['expert_w1'], 'L0_ffn_expert_b1': _L0_ffn_in['expert_b1'], 'L0_ffn_expert_w2': _L0_ffn_in['expert_w2'], 'L0_ffn_expert_b2': _L0_ffn_in['expert_b2'], 'L0_ffn_expert_w3': _L0_ffn_in['expert_w3'], 'L0_ffn_expert_b3': _L0_ffn_in['expert_b3']}

def reference(x, src, dst, edge_attr_64, node_vec1, L0_gnn_W_self, L0_gnn_W_func, L0_gnn_W_att, L0_mix_Wq, L0_mix_bq, L0_mix_Wk, L0_mix_bk, L0_mix_Wv, L0_mix_bv, L0_mix_Wo, L0_mix_bo, L0_mix_W1, L0_mix_b1, L0_mix_W2, L0_mix_b2, L0_mix_ln1_g, L0_mix_ln1_b, L0_mix_ln2_g, L0_mix_ln2_b, L0_ffn_router_w1, L0_ffn_router_b1, L0_ffn_router_w2, L0_ffn_router_b2, L0_ffn_expert_w1, L0_ffn_expert_b1, L0_ffn_expert_w2, L0_ffn_expert_b2, L0_ffn_expert_w3, L0_ffn_expert_b3):
    import jax
    import jax.numpy as jnp

    def _L0_gnn_ref(h, w, snorm_n, edge_src, edge_dst, W_self, W_func, W_att):
        import jax, jax.numpy as jnp
        import numpy as np
        N_NODES = 1250
        N_EDGES = 20000
        IN_FEATS = 256
        E_DIMS = 64
        NEG_SLOPE = 0.01
        N = h.shape[0]
        h_s = h @ W_self.T
        z = h @ W_func.T
        concat_z = jnp.concatenate([z[edge_src], z[edge_dst], w], axis=-1)
        e = jax.nn.leaky_relu(concat_z @ W_att.T, negative_slope=NEG_SLOPE)[:, 0]
        m = jax.ops.segment_max(e, edge_dst, num_segments=N)
        e_exp = jnp.exp(e - m[edge_dst])
        denom = jax.ops.segment_sum(e_exp, edge_dst, num_segments=N)
        alpha = e_exp / denom[edge_dst]
        agg = jax.ops.segment_sum(alpha[:, None] * z[edge_src], edge_dst, num_segments=N)
        h_new = h_s + agg
        deg = jax.ops.segment_sum(jnp.ones_like(e), edge_dst, num_segments=N)
        h_new = jnp.where(deg[:, None] > 0, h_new, h)
        h_new = jax.nn.relu(h_new)
        return h + h_new

    def _L0_mix_ref(x, Wq, bq, Wk, bk, Wv, bv, Wo, bo, W1, b1, W2, b2, ln1_g, ln1_b, ln2_g, ln2_b):
        import jax, jax.numpy as jnp
        import numpy as np
        D_MODEL = 256
        NHEAD = 8
        D_HEAD = D_MODEL // NHEAD
        DIM_FF = 1024
        B, L = (4, 2048)
        LN_EPS = 1e-05

        def _layernorm(x, g, b):
            mu = jnp.mean(x, axis=-1, keepdims=True)
            var = jnp.mean((x - mu) ** 2, axis=-1, keepdims=True)
            return (x - mu) * jax.lax.rsqrt(var + LN_EPS) * g + b

        def _phi(x):
            return jnp.where(x > 0, x + 1.0, jnp.exp(x))
        Bq, Lq, _ = x.shape
        q = (x @ Wq + bq).reshape(Bq, Lq, NHEAD, D_HEAD)
        k = (x @ Wk + bk).reshape(Bq, Lq, NHEAD, D_HEAD)
        v = (x @ Wv + bv).reshape(Bq, Lq, NHEAD, D_HEAD)
        q_phi = _phi(q)
        k_phi = _phi(k)
        kv = jnp.einsum('blhd,blhe->bhde', k_phi, v)
        k_sum = k_phi.sum(axis=1)
        z = 1.0 / (jnp.einsum('blhd,bhd->blh', q_phi, k_sum) + 1e-06)
        out = jnp.einsum('blhd,bhde,blh->blhe', q_phi, kv, z)
        out = out.reshape(Bq, Lq, D_MODEL) @ Wo + bo
        x = _layernorm(x + out, ln1_g, ln1_b)
        ff = jax.nn.relu(x @ W1 + b1) @ W2 + b2
        x = _layernorm(x + ff, ln2_g, ln2_b)
        return x

    def _L0_ffn_ref(features, router_w1, router_b1, router_w2, router_b2, expert_w1, expert_b1, expert_w2, expert_b2, expert_w3, expert_b3):
        import jax, jax.numpy as jnp
        import numpy as np
        E, D, H, TOP_K = (6, 256, 256, 2)
        ROUTER_H = D // 2
        rh = jax.nn.relu(features @ router_w1 + router_b1)
        expert_logits = jax.nn.softmax(rh @ router_w2 + router_b2, axis=-1)
        top_w, top_i = jax.lax.top_k(expert_logits, TOP_K)
        routing_weights = jax.nn.softmax(top_w, axis=-1)
        h1 = jax.nn.relu(jnp.einsum('bsd,edh->bseh', features, expert_w1) + expert_b1)
        h2 = jax.nn.relu(jnp.einsum('bseh,ehf->bsef', h1, expert_w2) + expert_b2)
        expert_out = jnp.einsum('bsef,efo->bseo', h2, expert_w3) + expert_b3
        sel = jnp.take_along_axis(expert_out, top_i[:, :, :, None], axis=2)
        combined = jnp.sum(sel * routing_weights[..., None], axis=2)
        return combined
    xn = _layernorm(x, axis=-1)
    x = x + _L0_gnn_ref(xn, edge_attr_64, node_vec1, src, dst, L0_gnn_W_self, L0_gnn_W_func, L0_gnn_W_att) + _L0_mix_ref(xn[None], L0_mix_Wq, L0_mix_bq, L0_mix_Wk, L0_mix_bk, L0_mix_Wv, L0_mix_bv, L0_mix_Wo, L0_mix_bo, L0_mix_W1, L0_mix_b1, L0_mix_W2, L0_mix_b2, L0_mix_ln1_g, L0_mix_ln1_b, L0_mix_ln2_g, L0_mix_ln2_b)[0]
    x = x + _L0_ffn_ref(_layernorm(x, axis=-1)[None], L0_ffn_router_w1, L0_ffn_router_b1, L0_ffn_router_w2, L0_ffn_router_b2, L0_ffn_expert_w1, L0_ffn_expert_b1, L0_ffn_expert_w2, L0_ffn_expert_b2, L0_ffn_expert_w3, L0_ffn_expert_b3)[0]
    return x

_drawn_inputs = setup_inputs


def setup_inputs(seed=0):
    import zlib

    import numpy as np

    out = dict(_drawn_inputs(seed))
    spreads = {'L0_mix_bq': (0.0, 0.8),
     'L0_mix_bk': (0.0, 0.8),
     'L0_mix_bv': (0.0, 0.1),
     'L0_mix_bo': (0.0, 0.1),
     'L0_mix_b1': (0.0, 0.402),
     'L0_mix_b2': (0.0, 0.292),
     'L0_mix_ln1_g': (1.0, 0.2),
     'L0_mix_ln1_b': (0.0, 0.1),
     'L0_mix_ln2_g': (1.0, 0.2),
     'L0_mix_ln2_b': (0.0, 0.1),
     'L0_ffn_router_b1': (0.0, 0.637),
     'L0_ffn_router_b2': (0.0, 0.421),
     'L0_ffn_expert_b1': (0.0, 0.8),
     'L0_ffn_expert_b2': (0.0, 0.8),
     'L0_ffn_expert_b3': (0.0, 0.337)}
    factors = {'L0_mix_Wq': 8.0,
     'L0_mix_Wk': 8.0,
     'L0_mix_Wv': 8.0,
     'L0_ffn_expert_w1': 3.442,
     'L0_ffn_expert_w2': 2.944}
    for name, (base, spread) in spreads.items():
        noise = np.random.default_rng([zlib.crc32(name.encode()), seed]).standard_normal(out[name].shape)
        drawn = base * np.exp(spread * noise) if base else spread * noise
        out[name] = jnp.asarray(drawn.astype(out[name].dtype))
    for name, factor in factors.items():
        out[name] = (out[name] * factor).astype(out[name].dtype)
    return out
```

```python
from contextlib import ExitStack

import concourse.bass as bass
from concourse import mybir

F32 = mybir.dt.float32
I32 = mybir.dt.int32
U32 = mybir.dt.uint32
ALU = mybir.AluOpType
ACT = mybir.ActivationFunctionType
AX = mybir.AxisListType

N, D = 6250, 256
E, ED = 100000, 64
R = 125
GROUP = 2 * R
GROUPS = N // GROUP
BLOCKS = N // R
PAIRS = E // (2 * R)
STEPS = 450
QS, CS = 90, 5
JS = 2 * CS
LROW = CS * 2 * R
FF = 1024
FC = FF // 128
HEAD = 32
EXPERTS = 6
CHUNK = 40
CHUNKS = E // R // CHUNK
SLOTS = 10
BIG = 1e30
EPS = 1e-5
ROUND = 12582912.0


class Own:

    def __init__(self, eng, sem, per, group):
        self.eng, self.sem, self.per, self.group, self.k = eng, sem, per, group, 0

    def did(self, ins):
        ins.then_inc(self.sem, 1)
        self.k += 1

    def settle(self):
        self.eng.wait_ge(self.sem, self.group * self.per + self.k)

    def end(self):
        assert self.k == self.per, (self.k, self.per)


def freed(eng, sem, count):
    if not (isinstance(count, int) and count <= 0):
        eng.wait_ge(sem, count)


def repeated(eng, n, body):
    body(0)
    with eng.Fori(1, n) as i:
        body(i)


def build(nc, x, src, dst, attr, wselfT, wfuncT, wfunc, att_nodes, att_edge, wq, wk, wv, wo, w1, w2,
          bq, b1, bkv, rowvecs, rw1, rb1, rw2, rb2, ew1, ew2, ew3, eb1, eb2, eb3, out):
    assert STEPS >= PAIRS + BLOCKS - 1 and QS * CS == STEPS
    ctx = ExitStack()
    with ctx:
        def sb(name, shape, dt=F32):
            return ctx.enter_context(nc.sbuf_tensor(name, shape, dt))

        sems = {}

        def s(name):
            if name not in sems:
                sems[name] = ctx.enter_context(nc.semaphore(name))
            return sems[name]

        xn_rows = nc.dram_tensor("xn_rows", (N, D), F32).ap()
        xnT_d = nc.dram_tensor("xnT_d", (GROUPS, 128, 2 * GROUP), F32).ap()
        mix_rows = nc.dram_tensor("mix_rows", (N, D), F32).ap()
        s1_d = nc.dram_tensor("s1_d", (N, 1), F32).ap()
        s2_d = nc.dram_tensor("s2_d", (1, N), F32).ap()
        ew_d = nc.dram_tensor("ew_d", (PAIRS, 2 * R), F32).ap()
        blk_d = nc.dram_tensor("blk_d", (STEPS,), I32).ap()

        def rows_of(t, g):
            v = t.rearrange("(g j p) d -> g p j d", j=2, p=R)
            return v[bass.ds(g, 1)].rearrange("g p j d -> (g p) j d")

        ident = sb("ident", [128, 128])
        bmask = sb("bmask", [128, 128])
        iota_r = sb("iota_r", [R, R])
        iota_e = sb("iota_e", [R, EXPERTS])
        iota_s = sb("iota_s", [QS, CS])
        iota_t = sb("iota_t", [1, PAIRS])
        ones_row = sb("ones_row", [1, 128])
        rv = sb("rv", [R, 6, D])
        rb2_bc = sb("rb2_bc", [R, EXPERTS])
        awe = sb("awe", [R, ED])
        bq_c = sb("bq_c", [128, 2])
        b1_c = sb("b1_c", [128, FC])
        rb1_c = sb("rb1_c", [128, 1])
        eb_c = sb("eb_c", [128, 2, EXPERTS, 2])
        eb3_s = sb("eb3_s", [EXPERTS, D])
        wq_s = sb("wq_s", [128, 2, D])
        wo_s = sb("wo_s", [128, 2, D])
        w1_s = sb("w1_s", [128, 2, FF])
        w2_s = sb("w2_s", [128, FC, D])
        wself_s = sb("wself_s", [128, 2, D])
        wfunc_s = sb("wfunc_s", [128, 2, D])
        wfuncT_s = sb("wfuncT_s", [128, 2, D])
        rw1_s = sb("rw1_s", [128, 2, 128])
        rw2_s = sb("rw2_s", [128, EXPERTS])
        attn_c = sb("attn_c", [128, 2, 2])
        u_s = sb("u_s", [128, 2, 2])
        kvbd = sb("kvbd", [128, 2, 128])
        ksbd = sb("ksbd", [128, 2, 128])
        a_src = sb("a_src", [R, QS, JS], I32)
        a_rel = sb("a_rel", [R, QS, JS])
        a_s1 = sb("a_s1", [R, QS, JS])
        a_s2 = sb("a_s2", [R, QS, JS])
        a_p = a_s1
        blk_row = sb("blk_row", [1, STEPS], I32)
        acc = sb("acc", [R, BLOCKS * (D + 1)])
        accv = acc[:].rearrange("p (b n) -> p b n", n=D + 1)
        s2_bc = acc[:, 0:N]

        def tail(k):
            o = N + k * (LROW + 2)
            return acc[0:QS, o:o + LROW]

        valid, e_l, t_l = tail(0), tail(1), tail(2)
        wexp = sb("wexp", [128, 3 * EXPERTS * 2 * D])
        wexpv = wexp[:].rearrange("p (l e c n) -> p l e c n", l=3, e=EXPERTS, c=2)

        def early(k, n=LROW):
            return wexp[0:QS, k * (LROW + 4):k * (LROW + 4) + n]

        src_i, dst_i, src_f, dst_f = early(0).bitcast(I32), early(1).bitcast(I32), early(2), early(3)
        rel_l, ew_l = early(4), early(5)
        reset, f_l, b_l = early(0, LROW + 1), early(1), early(2)
        ew_n = wexp[0:R, 6 * (LROW + 4):6 * (LROW + 4) + E // R]
        ring = sb("ring", [R, SLOTS * 2, D + 1])
        attr_s = ring[:].rearrange("p a b -> p (a b)")[:, 0:2 * CHUNK * ED].rearrange(
            "p (h k f) -> p h k f", h=2, f=ED)
        onehot = sb("onehot", [R, 4, R])
        junk = onehot[:].rearrange("p a b -> p (a b)")
        tabs = sb("tabs", [QS, 8, CS])
        tab_i = sb("tab_i", [QS, 2, CS], I32)
        dlast = sb("dlast", [1, PAIRS], I32)
        idx_slot = sb("idx_slot", [R, 2, JS], I32)
        s1_slot = sb("s1_slot", [R, 2, JS])
        mark = sb("mark", [1, 1])
        sm = sb("sm", [QS, 8])
        smr = sb("smr", [1, 12, 92])
        work = sb("work", [128, 16 * 512])

        def w(k, shape, n=1):
            v = work[0:shape[0], 512 * k:512 * (k + n)]
            size = 1
            for a in shape[1:]:
                size *= a
            v = v[:, 0:size]
            if len(shape) == 3:
                v = v.rearrange("p (a b) -> p a b", a=shape[1])
            return v

        xn_in, xnT_in = w(0, [R, 2, D]), w(1, [128, 2, GROUP])
        p_x, p_xn, p_xnT = w(2, [R, 2, D]), w(3, [R, 2, D]), w(4, [128, 2, GROUP])
        p_s = w(5, [2, GROUP])
        p_k, p_min, p_exp, p_phi = w(6, [R, 2, D]), w(7, [R, 2, D]), w(8, [R, 2, D]), w(9, [R, 2, D])
        p_v = [w(10, [R, 2, 129]), w(11, [R, 2, 129])]
        wkv_s, bkv_bc, zeros = w(12, [128, 2, 2 * D], 2), w(14, [R, 2 * D]), w(15, [128, 260])
        tab_t = w(10, [1, 2, PAIRS], 2)
        m_q, m_e, m_r, m_n = w(2, [128, 2, GROUP]), w(3, [128, 2, GROUP]), w(4, [128, 2, GROUP]), w(5, [128, 2, GROUP])
        m_z, m_y, m_yb, m_yT = w(6, [R, 2, D]), w(7, [R, 2, D]), w(8, [R, 2, D]), w(9, [128, 2, GROUP])
        m_h = w(10, [128, FC, GROUP], 4)
        m_z2, m_o = w(14, [R, 2, D]), w(15, [R, 2, D])
        f_x, f_mix, f_an, f_aT = w(2, [R, 2, D]), w(3, [R, 2, D]), w(4, [R, 2, D]), w(5, [128, 2, GROUP])
        f_t, f_x1, f_xT, f_x2 = w(6, [R, 2, D]), w(7, [R, 2, D]), w(8, [128, 2, GROUP]), w(9, [R, 2, D])
        f_h1 = [w(10, [128, 2, GROUP]), w(11, [128, 2, GROUP])]
        f_h2 = [w(12, [128, 2, GROUP]), w(13, [128, 2, GROUP])]
        f_rh, f_wT = w(14, [128, GROUP]), w(15, [EXPERTS, GROUP])
        st = sb("st", [R, 2, 6])
        mv = sb("mv", [R, 2, 2])
        lnv = sb("lnv", [R, 2])
        rstd = sb("rstd", [R, 2])
        st2, mv2 = sb("st2", [R, 2, 6]), sb("mv2", [R, 2, 2])
        lnv2, rstd2 = sb("lnv2", [R, 2]), sb("rstd2", [R, 2])
        dn = sb("dn", [R, 3, 2])
        lg = sb("lg", [R, 2, 8])
        pr = sb("pr", [R, 2, 8])
        top = sb("top", [R, 2, 8])
        topi = sb("topi", [R, 2, 8], U32)
        topf = sb("topf", [R, 2, 2])
        rt = sb("rt", [R, 8, 2])
        wt1, wt2, wt = sb("wt1", [R, 2, EXPERTS]), sb("wt2", [R, 2, EXPERTS]), sb("wt", [R, 2, EXPERTS])

        bank = [ctx.enter_context(nc.psum_tensor(f"bank{i}", [128, 512], F32)) for i in range(8)]

        def pt(b):
            return bank[b][:, 0:2 * GROUP].rearrange("p (c n) -> p c n", c=2)

        def pr_(b):
            return bank[b][0:R, :].rearrange("p (j n) -> p j n", j=2)

        def apart(eng, name):
            eng.sem_inc(s(name), 1)

        block = ctx.enter_context(nc.Block())
        LOADS_EARLY, LOADS_LATE = 27, 3 * EXPERTS

        @block.sync
        def _(sp):
            def load(sem, dst_, src_):
                sp.dma_start(dst_, src_).then_inc(s(sem), 16)

            with nc.allow_non_contiguous_dma(reason="one index of each pair of edge tiles"):
                load("dlast_in", dlast[:], dst.rearrange("(t e) -> t e", e=2 * R)[:, 2 * R - 1:2 * R]
                     .rearrange("t e -> e t"))
            cols = lambda t: t.rearrange("(c p) n -> p c n", p=128)
            load("w_in", wfunc_s[:], cols(wfunc))
            load("w_in", attn_c[:], att_nodes)
            load("p1_x", p_x, rows_of(x, 0))
            load("w_in", wkv_s[:, :, 0:D], cols(wk))
            load("w_in", wkv_s[:, :, D:2 * D], cols(wv))
            load("w_in", bkv_bc, bkv.to_broadcast([R, 2 * D]))
            load("w_in", wq_s[:], cols(wq))
            load("w_in", wo_s[:], cols(wo))
            load("w_in", w1_s[:], cols(w1))
            load("w_in", w2_s[:], cols(w2))
            load("w_in", bq_c[:], bq)
            load("w_in", b1_c[:], b1)
            load("w_in", awe[:], att_edge.to_broadcast([R, ED]))
            load("w_in", rb2_bc[:], rb2.to_broadcast([R, EXPERTS]))
            load("w_in", rb1_c[:], rb1)
            for k in range(6):
                load("w_in", rv[:, k, :], rowvecs[k:k + 1, :].to_broadcast([R, D]))
            load("w_in", eb_c[:, 0], eb1)
            load("w_in", eb_c[:, 1], eb2)
            load("w_in", eb3_s[:], eb3)
            load("w_in", wself_s[:], cols(wselfT))
            load("w_in", wfuncT_s[:], cols(wfuncT))
            load("w_in", rw1_s[:], cols(rw1))
            load("w_in", rw2_s[:], rw2)
            sp.wait_ge(s("tab_done"), 1)
            load("blk_out", blk_d.rearrange("(q c) -> q c", c=CS), tab_i[:, 1, :])
            sp.wait_ge(s("blk_out"), 16)
            load("blk_in", blk_row[:], blk_d[None, :])

            def pass1(g, more):
                sp.wait_ge(s("p1_xn"), g + 1)
                if more:
                    load("p1_x", p_x, rows_of(x, g + 1))
                load("p1_xn_out", rows_of(xn_rows, g), p_xn)
                sp.wait_ge(s("p1_xnT"), g + 1)
                load("p1_xnT_out", xnT_d[bass.ds(g, 1)].rearrange("g p n -> (g p) n"),
                     p_xnT.rearrange("p c n -> p (c n)"))
                sp.wait_ge(s("p1_s"), g + 1)
                load("p1_s_out", s1_d.rearrange("(g n) a -> a g n", n=GROUP)[:, bass.ds(g, 1), :]
                     .rearrange("a g n -> a (g n)"), p_s[0:1, :])
                load("p1_s_out", s2_d.rearrange("a (g n) -> a g n", n=GROUP)[:, bass.ds(g, 1), :]
                     .rearrange("a g n -> a (g n)"), p_s[1:2, :])

            def body(i):
                pass1(i, True)

            repeated(sp, GROUPS - 1, body)
            pass1(GROUPS - 1, False)
            sp.wait_ge(s("p1_s_out"), 32 * GROUPS)
            load("s2_in", s2_bc, s2_d.to_broadcast([R, N]))
            attr_v = attr.rearrange("(p c k) f -> c p k f", p=R, k=CHUNK)
            def body(i):
                for h in range(2):
                    freed(sp, s(f"attr_used{h}"), i)
                    load(f"attr_in{h}", attr_s[:, h], attr_v[bass.ds(i * 2 + h, 1)].rearrange("c p k f -> (c p) k f"))

            repeated(sp, CHUNKS // 2, body)
            sp.wait_ge(s("ew_done"), 1)
            load("ew_out", ew_d.rearrange("t e -> (t e)").rearrange("(p k) -> p k", p=R), ew_n)
            sp.wait_ge(s("p1_xn_out"), 16 * GROUPS)
            sp.wait_ge(s("p1_xnT_out"), 16 * GROUPS)

            def mix_in(g):
                freed(sp, s("m_q"), g)
                load("m_xnT", xnT_in.rearrange("p c n -> p (c n)"),
                     xnT_d[bass.ds(g, 1)].rearrange("g p n -> (g p) n"))
                freed(sp, s("m_xb"), g)
                load("m_xn", xn_in, rows_of(xn_rows, g))

            def mix_out(g):
                sp.wait_ge(s("m_out"), g + 1)
                load("m_stored", rows_of(mix_rows, g), m_o)

            mix_in(0)
            def body(i):
                mix_in(i + 1)
                mix_out(i)

            repeated(sp, GROUPS - 1, body)
            mix_out(GROUPS - 1)
            sp.wait_ge(s("p_done"), 1)
            sp.wait_ge(s("pT_done"), 1)
            for l, t in enumerate((ew1, ew2, ew3)):
                for e in range(EXPERTS):
                    load("wexp_in", wexpv[:, l, e], cols(t[e]))
            sp.wait_ge(s("m_stored"), 16 * GROUPS)

            def last_in(g):
                freed(sp, s("f_gnn"), g)
                load("f_xnT", xnT_in.rearrange("p c n -> p (c n)"),
                     xnT_d[bass.ds(g, 1)].rearrange("g p n -> (g p) n"))
                freed(sp, s("f_x1"), g)
                load("f_rows", xn_in, rows_of(xn_rows, g))
                load("f_rows", f_x, rows_of(x, g))
                load("f_rows", f_mix, rows_of(mix_rows, g))

            def last_out(g):
                sp.wait_ge(s("f_x2"), EXPERTS * (g + 1))
                load("f_stored", rows_of(out, g), f_x2)

            last_in(0)
            def body(i):
                last_in(i + 1)
                last_out(i)

            repeated(sp, GROUPS - 1, body)
            last_out(GROUPS - 1)
            sp.wait_ge(s("f_stored"), 16 * GROUPS)

        @block.gpsimd
        def _(pool):
            own = Own(pool, s("pool_own"), 0, 0)
            iota = dict(allow_small_or_imprecise_dtypes=True)
            pool.iota(iota_t[:], [[1, PAIRS]], base=0, channel_multiplier=0, **iota).then_inc(s("iota_tabs"), 1)
            pool.iota(iota_s[:], [[1, CS]], base=0, channel_multiplier=CS, **iota).then_inc(s("iota_tabs"), 1)
            pool.memset(ones_row[:], 1.0).then_inc(s("iota_tabs"), 1)
            own.did(pool.memset(ident[:], 0.0))
            own.did(pool.memset(bmask[:], 1.0))
            own.settle()
            pool.affine_select(out=ident[:], in_=ident[:], compare_op=ALU.not_equal, fill=1.0, base=0,
                               pattern=[[-1, 128]], channel_multiplier=1).then_inc(s("ident_done"), 1)
            bm = bmask[:].rearrange("p (b k) -> p b k", k=HEAD)
            own.did(pool.affine_select(out=bm, in_=bm, compare_op=ALU.is_ge, fill=0.0, base=0,
                                       pattern=[[-HEAD, 128 // HEAD], [0, HEAD]], channel_multiplier=1))
            own.settle()
            pool.affine_select(out=bm, in_=bm, compare_op=ALU.is_ge, fill=0.0, base=HEAD - 1,
                               pattern=[[HEAD, 128 // HEAD], [0, HEAD]],
                               channel_multiplier=-1).then_inc(s("consts"), 1)
            pool.iota(iota_r[:], [[1, R]], base=0, channel_multiplier=0, **iota).then_inc(s("consts"), 1)
            pool.iota(iota_e[:], [[1, EXPERTS]], base=0, channel_multiplier=0, **iota).then_inc(s("consts"), 1)
            pool.memset(zeros, 0.0).then_inc(s("consts"), 1)

            pool.wait_ge(s("tab_done"), 1)
            for c in range(CS):
                at = bass.IndirectOffsetOnAxis(ap=tab_i[:, 0, c:c + 1], axis=0)
                for d_, s_ in ((src_i, src), (dst_i, dst)):
                    pool.indirect_dma_start(d_[:, c * 2 * R:(c + 1) * 2 * R], None,
                                            s_.rearrange("(t e) -> t e", e=2 * R), at).then_inc(s("sd_in"), 16)

            pool.wait_ge(s("a_done"), 4)
            pool.wait_ge(s("p1_s_out"), 32 * GROUPS)
            def body(i):
                for h in range(2):
                    q = i * 2 + h
                    freed(pool, s(f"s1_in{h}"), i * (16 * JS))
                    pool.tensor_copy(idx_slot[:, h, :], a_src[:, bass.ds(q, 1), :]
                                     .rearrange("p a j -> p (a j)")).then_inc(s("idx1"), 1)
                    pool.wait_ge(s("idx1"), q + 1)
                    freed(pool, s(f"s1_kept{h}"), i)
                    apart(pool, "past_pool")
                    for j in range(JS):
                        pool.indirect_dma_start(
                            s1_slot[:, h, j:j + 1], None, s1_d,
                            bass.IndirectOffsetOnAxis(ap=idx_slot[:, h, j:j + 1], axis=0)
                        ).then_inc(s(f"s1_in{h}"), 16)
                for h in range(2):
                    pool.wait_ge(s(f"s1_in{h}"), i * (16 * JS) + 16 * JS)
                    pool.tensor_copy(a_s1[:, bass.ds(i * 2 + h, 1), :].rearrange("p a j -> p (a j)"),
                                     s1_slot[:, h, :]).then_inc(s(f"s1_kept{h}"), 1)

            repeated(pool, QS // 2, body)
            pool.wait_ge(s("ew_out"), 16)
            for c in range(CS):
                pool.indirect_dma_start(ew_l[:, c * 2 * R:(c + 1) * 2 * R], None, ew_d,
                                        bass.IndirectOffsetOnAxis(ap=tab_i[:, 0, c:c + 1], axis=0)
                                        ).then_inc(s("ew_in"), 16)
            pool.wait_ge(s("ew_done"), 1)
            pool.memset(ring[:, :, D:D + 1], 1.0).then_inc(s("rows_free"), SLOTS)
            def body(i):
                for h in range(2):
                    q = i * 2 + h
                    for c in range(CS):
                        freed(pool, s(f"rows_in{h * CS + c}"), i * 32)
                    pool.tensor_copy(idx_slot[:, h, :], a_src[:, bass.ds(q, 1), :]
                                     .rearrange("p a j -> p (a j)")).then_inc(s("idx2"), 1)
                    for c in range(CS):
                        pool.wait_ge(s("rows_free"), i * SLOTS + h * CS + c + 1)
                        if c == 0:
                            pool.wait_ge(s("idx2"), q + 1)
                        apart(pool, "past_pool")
                        for k in range(2):
                            pool.indirect_dma_start(
                                ring[:, 2 * (h * CS + c) + k, 0:D], None, xn_rows,
                                bass.IndirectOffsetOnAxis(ap=idx_slot[:, h, 2 * c + k:2 * c + k + 1], axis=0)
                            ).then_inc(s(f"rows_in{h * CS + c}"), 16)

            repeated(pool, QS // 2, body)

        @block.tensor
        def _(pe):
            def mm(o, l, r, first, last_, **kw):
                return pe.matmul(o, l, r, start=first, stop=last_, **kw)

            pe.wait_ge(s("w_in"), 16 * LOADS_EARLY)
            for c in range(2):
                for o in range(2):
                    last = mm(bank[0][:, 2 * c:2 * c + 2], wfunc_s[:, o, c * 128:(c + 1) * 128],
                              attn_c[:, o, :], o == 0, o == 1)
            last.then_inc(s("u_ps"), 1)
            pe.wait_ge(s("e_row"), 1)
            mm(bank[1][0:QS, 0:PAIRS], ones_row[:, 0:QS], tab_t[:, 1, :], True, True).then_inc(s("e_bc"), 1)
            pe.wait_ge(s("ident_done"), 1)
            for a, (what, name) in enumerate(((src_f, "src_f"), (rel_l, "rel"))):
                pe.wait_ge(s(name), 1 if a == 0 else CS)
                for j in range(JS):
                    last = pe.transpose(bank[2 + 2 * a + j // 5][0:R, (j % 5) * QS:(j % 5 + 1) * QS],
                                        what[:, j * R:(j + 1) * R], ident[0:QS, 0:QS])
                    if j % 5 == 4:
                        last.then_inc(s("a_ps"), 1)
            pe.wait_ge(s("a_done"), 4)
            pe.wait_ge(s("u_done"), 1)
            pe.wait_ge(s("consts"), 4)
            mm(bank[7][:, 0:258], zeros[:, 0:128], zeros[:, 0:258], True, False, skip_group_check=True)

            def transposes(g):
                pe.wait_ge(s("p1_xn"), g + 1)
                freed(pe, s("p1_xnT"), g)
                for c in range(2):
                    for j in range(2):
                        last = pe.transpose(pt(0)[:, c, j * R:(j + 1) * R], p_xn[:, j, c * 128:(c + 1) * 128],
                                            ident[0:R, 0:R])
                last.then_inc(s("p1_T"), 1)

            def products(g, j):
                pe.wait_ge(s("p1_xnT"), g + 1)
                if j == 0:
                    freed(pe, s("p1_s"), g)
                    for c in range(2):
                        last = mm(bank[1][0:2, 0:GROUP], u_s[:, c, :], p_xnT[:, c, :], c == 0, c == 1)
                    last.then_inc(s("p1_s_ps"), 1)
                freed(pe, s("p1_kv_read"), 2 * g + j - 1)
                for c in range(2):
                    last = mm(bank[2 + j][0:R, :], p_xnT[:, c, j * R:(j + 1) * R], wkv_s[:, c, :], c == 0, c == 1)
                last.then_inc(s("p1_kv"), 1)

            def kv_sum(g, j):
                pe.wait_ge(s("p1_phi"), 2 * g + j + 1)
                for c in range(2):
                    last = mm(bank[7][:, c * 129:(c + 1) * 129], p_phi[:, j, c * 128:(c + 1) * 128],
                              p_v[j][:, c, :], False, False, skip_group_check=True)
                last.then_inc(s("p1_sum"), 1)

            transposes(0)
            products(0, 0)
            products(0, 1)
            def body(i):
                transposes(i + 1)
                kv_sum(i, 0)
                products(i + 1, 0)
                kv_sum(i, 1)
                products(i + 1, 1)

            repeated(pe, GROUPS - 1, body)
            kv_sum(GROUPS - 1, 0)
            kv_sum(GROUPS - 1, 1)
            mm(bank[7][:, 0:258], zeros[:, 0:128], zeros[:, 0:258], False, True,
               skip_group_check=True).then_inc(s("kv_done"), 1)

            pe.wait_ge(s("kvbd"), 4)

            def queries(g):
                pe.wait_ge(s("m_xnT"), 16 * (g + 1))
                freed(pe, s("m_qread"), 2 * g)
                freed(pe, s("m_min"), 2 * g)
                for o in range(2):
                    for c in range(2):
                        last = mm(pt(0)[:, o, :], wq_s[:, c, o * 128:(o + 1) * 128], xnT_in[:, c, :], c == 0, c == 1)
                last.then_inc(s("m_q"), 1)

            def attention(g):
                pe.wait_ge(s("m_phi"), g + 1)
                freed(pe, s("m_att"), g)
                for o in range(2):
                    mm(pt(1)[:, o, :], ksbd[:, o, :], m_n[:, o, :], True, True)
                for o in range(2):
                    last = mm(pt(2)[:, o, :], kvbd[:, o, :], m_n[:, o, :], True, True)
                last.then_inc(s("m_nd"), 1)

            def project(g):
                pe.wait_ge(s("m_att"), g + 1)
                freed(pe, s("m_z"), g)
                for j in range(2):
                    for c in range(2):
                        last = mm(pr_(3)[:, j, :], m_e[:, c, j * R:(j + 1) * R], wo_s[:, c, :], c == 0, c == 1)
                last.then_inc(s("m_o_ps"), 1)

            def turn(g):
                pe.wait_ge(s("m_y"), g + 1)
                freed(pe, s("m_yT"), g)
                for c in range(2):
                    for j in range(2):
                        last = pe.transpose(pt(4)[:, c, j * R:(j + 1) * R], m_y[:, j, c * 128:(c + 1) * 128],
                                            ident[0:R, 0:R])
                last.then_inc(s("m_T"), 1)

            def hidden(g, o2):
                pe.wait_ge(s("m_yT"), g + 1)
                for h in range(2):
                    f = 2 * o2 + h
                    freed(pe, s(f"m_hread{h}"), g * 4 + o2)
                    for c in range(2):
                        last = mm(bank[5 + h][:, 0:GROUP], w1_s[:, c, f * 128:(f + 1) * 128], m_yT[:, c, :],
                                  c == 0, c == 1)
                    last.then_inc(s(f"m_h{h}"), 1)

            def down(g, j):
                for h in range(2):
                    pe.wait_ge(s(f"m_hread{h}"), g * 4 + 4)
                if j == 0:
                    freed(pe, s("m_z2"), g)
                for f in range(FC):
                    last = mm(pr_(7)[:, j, :], m_h[:, f, j * R:(j + 1) * R], w2_s[:, f, :], f == 0, f == FC - 1)
                last.then_inc(s("m_d"), 1)

            queries(0)
            attention(0)
            project(0)
            turn(0)
            def body(i):
                queries(i + 1)
                for o2 in range(3):
                    hidden(i, o2)
                attention(i + 1)
                hidden(i, 3)
                down(i, 0)
                project(i + 1)
                down(i, 1)
                turn(i + 1)

            repeated(pe, GROUPS - 1, body)
            for o2 in range(4):
                hidden(GROUPS - 1, o2)
            for j in range(2):
                down(GROUPS - 1, j)

            pe.wait_ge(s("scores"), 1)
            pe.wait_ge(s("m_z2"), GROUPS)
            for j in range(JS):
                last = pe.transpose(bank[j // 4][0:QS, (j % 4) * R:(j % 4 + 1) * R], a_s2[:, :, j], ident[0:R, 0:R])
            last.then_inc(s("u_l"), 1)
            pe.wait_ge(s("summary"), 5)
            for k in range(5):
                last = mm(bank[3][0:1, k * QS:(k + 1) * QS], sm[:, k:k + 1], ident[0:QS, 0:QS], True, True)
            last.then_inc(s("sm_row"), 1)
            pe.wait_ge(s("carry"), 1)
            mm(bank[4][0:QS, 0:1], smr[0:1, 5, 0:QS], ones_row[:, 0:1], True, True)
            mm(bank[4][0:QS, 1:2], smr[0:1, 6, 0:QS], ones_row[:, 0:1], True, True).then_inc(s("carry_c"), 1)
            pe.wait_ge(s("p_l"), 1)
            for j in range(JS):
                last = pe.transpose(bank[5 + j // 5][0:R, (j % 5) * QS:(j % 5 + 1) * QS], t_l[:, j * R:(j + 1) * R],
                                    ident[0:QS, 0:QS])
            last.then_inc(s("pT_done"), 1)

            pe.wait_ge(s("rows_free"), SLOTS)
            def body(i):
                for z in range(SLOTS):
                    b = z % 2
                    pe.wait_ge(s(f"rows_in{z}"), i * 32 + 32)
                    pe.wait_ge(s("onehot"), i * (2 * SLOTS) + 2 * z + 2)
                    freed(pe, s("summed"), i * SLOTS + z)
                    for k in range(2):
                        last = mm(bank[b][0:R, 0:D + 1], onehot[:, 2 * b + k, :], ring[:, 2 * z + k, :], k == 0, k == 1)
                    last.then_inc(s("rows_free"), 1)

            repeated(pe, QS // 2, body)

            pe.wait_ge(s("wexp_in"), 16 * LOADS_LATE)

            def agg_turn(g):
                pe.wait_ge(s("f_an"), 2 * (g + 1))
                freed(pe, s("f_aT"), g)
                for c in range(2):
                    for j in range(2):
                        last = pe.transpose(pt(0)[:, c, j * R:(j + 1) * R], f_an[:, j, c * 128:(c + 1) * 128],
                                            ident[0:R, 0:R])
                last.then_inc(s("f_T"), 1)

            def gnn(g):
                pe.wait_ge(s("f_xnT"), 16 * (g + 1))
                pe.wait_ge(s("f_aT"), g + 1)
                freed(pe, s("f_start"), 2 * g)
                for j in range(2):
                    for c in range(2):
                        mm(pr_(2)[:, j, :], xnT_in[:, c, j * R:(j + 1) * R], wself_s[:, c, :], c == 0, False)
                    for c in range(2):
                        last = mm(pr_(2)[:, j, :], f_aT[:, c, j * R:(j + 1) * R], wfuncT_s[:, c, :], False, c == 1)
                last.then_inc(s("f_gnn"), 1)

            def norm_turn(g):
                pe.wait_ge(s("f_xn1"), 2 * (g + 1))
                freed(pe, s("f_xT"), g)
                for c in range(2):
                    for j in range(2):
                        last = pe.transpose(pt(1)[:, c, j * R:(j + 1) * R], f_t[:, j, c * 128:(c + 1) * 128],
                                            ident[0:R, 0:R])
                last.then_inc(s("f_T1"), 1)

            def router(g):
                pe.wait_ge(s("f_xT"), g + 1)
                freed(pe, s("f_wTc"), g)
                for c in range(2):
                    last = mm(bank[3][:, 0:GROUP], rw1_s[:, c, :], f_xT[:, c, :], c == 0, c == 1)
                last.then_inc(s("f_rh_ps"), 1)

            def logits(g):
                pe.wait_ge(s("f_rh"), g + 1)
                for j in range(2):
                    last = mm(bank[3][0:R, 256 + 8 * j:256 + 8 * j + EXPERTS], f_rh[:, j * R:(j + 1) * R], rw2_s[:],
                              True, True)
                last.then_inc(s("f_lg_ps"), 1)

            def weights_turn(g):
                pe.wait_ge(s("f_wt"), g + 1)
                for j in range(2):
                    last = mm(bank[3][0:EXPERTS, j * R:(j + 1) * R], wt[:, j, :], ident[0:R, 0:R], True, True)
                last.then_inc(s("f_wT_ps"), 1)

            def biases(g):
                pe.wait_ge(s("f_wTc"), g + 1)
                pe.wait_ge(s("f_r"), g + 1)
                for j in range(2):
                    last = mm(pr_(2)[:, j, :], f_wT[:, j * R:(j + 1) * R], eb3_s[:], True, True)
                last.then_inc(s("f_bias"), 1)

            def layer1(g, e):
                pe.wait_ge(s("f_xT"), g + 1)
                freed(pe, s("f_h1"), g * 6 + e)
                for o in range(2):
                    for c in range(2):
                        last = mm(pt(4)[:, o, :], wexpv[:, 0, e, c, o * 128:(o + 1) * 128], f_xT[:, c, :], c == 0, c == 1)
                last.then_inc(s("f_h1_ps"), 1)

            def layer2(g, e):
                pe.wait_ge(s("f_h1"), g * 6 + e + 1)
                freed(pe, s("f_h2"), g * 6 + e)
                for o in range(2):
                    for c in range(2):
                        last = mm(pt(5)[:, o, :], wexpv[:, 1, e, c, o * 128:(o + 1) * 128], f_h1[e % 2][:, c, :],
                                  c == 0, c == 1)
                last.then_inc(s("f_h2_ps"), 1)

            def layer3(g, e):
                pe.wait_ge(s("f_h2"), g * 6 + e + 1)
                if e % 2 == 0:
                    freed(pe, s("f_x2"), g * 6 + (e - 1) if e else g * 6)
                else:
                    freed(pe, s("f_x2"), g * 6 + (e - 1))
                for j in range(2):
                    for c in range(2):
                        last = mm(pr_(6 + e % 2)[:, j, :], f_h2[e % 2][:, c, j * R:(j + 1) * R], wexpv[:, 2, e, c, :],
                                  c == 0, c == 1)
                last.then_inc(s("f_o"), 1)

            def experts(g, between):
                router(g)
                layer1(g, 0)
                logits(g)
                layer1(g, 1)
                layer2(g, 0)
                layer1(g, 2)
                layer2(g, 1)
                weights_turn(g)
                between(agg_turn)
                layer1(g, 3)
                biases(g)
                layer3(g, 0)
                layer2(g, 2)
                layer3(g, 1)
                layer1(g, 4)
                layer2(g, 3)
                between(gnn)
                layer3(g, 2)
                layer1(g, 5)
                layer2(g, 4)
                layer3(g, 3)
                layer2(g, 5)
                between(norm_turn)
                layer3(g, 4)
                layer3(g, 5)

            pe.wait_ge(s("agg_done"), 1)
            agg_turn(0)
            gnn(0)
            norm_turn(0)
            def body(i):
                experts(i, lambda f: f(i + 1))

            repeated(pe, GROUPS - 1, body)
            experts(GROUPS - 1, lambda f: None)

        @block.scalar
        def _(act):
            def ln_rstd(g, var_ready, ln_done, rstd_done, v, l, r):
                act.wait_ge(s(var_ready), g + 1)
                act.activation(l[:], v[:, :, 1], ACT.Ln).then_inc(s(ln_done), 1)
                act.wait_ge(s(ln_done), g + 1)
                act.activation(r[:], l[:], ACT.Exp, scale=-0.5).then_inc(s(rstd_done), 1)

            act.preload_act_table_set("natural_log_exp_and_others")
            act.wait_ge(s("w_in"), 16 * LOADS_EARLY)

            def p1_a(g):
                ln_rstd(g, "var", "ln", "rstd", mv, lnv, rstd)

            def p1_b(g):
                act.wait_ge(s("p1_T"), g + 1)
                freed(act, s("p1_kv"), 2 * g)
                freed(act, s("p1_xnT_out"), g * 16)
                act.activation(p_xnT, pt(0), ACT.Copy).then_inc(s("p1_xnT"), 1)

            def p1_c(g):
                act.wait_ge(s("p1_s_ps"), g + 1)
                freed(act, s("p1_s_out"), g * 32)
                act.activation(p_s, bank[1][0:2, 0:GROUP], ACT.Copy).then_inc(s("p1_s"), 1)

            def p1_d(g):
                for j in range(2):
                    act.wait_ge(s("p1_min"), 2 * g + j + 1)
                    act.activation(p_exp[:, j], p_min[:, j], ACT.Exp).then_inc(s("p1_exp"), 1)

            p1_a(0)
            p1_b(0)
            p1_c(0)
            def body(i):
                p1_a(i + 1)
                p1_b(i + 1)
                p1_d(i)
                p1_c(i + 1)

            repeated(act, GROUPS - 1, body)
            p1_d(GROUPS - 1)

            def m_queries(g):
                act.wait_ge(s("m_min"), 2 * (g + 1))
                freed(act, s("m_o_ps"), g)
                act.activation(m_e, m_q, ACT.Exp).then_inc(s("m_exp"), 1)
                freed(act, s("m_phi"), g)
                for o in range(2):
                    act.activation(m_r[:, o], pt(0)[:, o], ACT.Relu, bias=bq_c[:, o:o + 1]).then_inc(s("m_qread"), 1)

            def m_norm(g):
                ln_rstd(GROUPS + g, "var", "ln", "rstd", mv, lnv, rstd)

            def m_turn(g):
                act.wait_ge(s("m_T"), g + 1)
                freed(act, s("m_h0"), g * 4)
                freed(act, s("m_h1"), g * 4)
                act.activation(m_yT, pt(4), ACT.Copy).then_inc(s("m_yT"), 1)

            def m_hidden(g, o2):
                act.wait_ge(s("m_h0"), g * 4 + o2 + 1)
                freed(act, s("m_d"), 2 * g)
                act.activation(m_h[:, 2 * o2], bank[5][:, 0:GROUP], ACT.Relu,
                               bias=b1_c[:, 2 * o2:2 * o2 + 1]).then_inc(s("m_hread0"), 1)

            def m_norm2(g):
                ln_rstd(g, "m_var2", "m_ln2", "m_rstd2", mv2, lnv2, rstd2)

            m_queries(0)
            m_norm(0)
            m_turn(0)
            def body(i):
                for o2 in range(2):
                    m_hidden(i, o2)
                m_queries(i + 1)
                for o2 in range(2, 4):
                    m_hidden(i, o2)
                m_norm(i + 1)
                m_turn(i + 1)
                m_norm2(i)

            repeated(act, GROUPS - 1, body)
            for o2 in range(4):
                m_hidden(GROUPS - 1, o2)
            m_norm2(GROUPS - 1)

            act.wait_ge(s("p_arg"), 1)
            act.activation(t_l, e_l, ACT.Exp).then_inc(s("p_exp"), 1)

            def f_first(g):
                act.wait_ge(s("f_T"), g + 1)
                freed(act, s("f_gnn"), g)
                act.activation(f_aT, pt(0), ACT.Copy).then_inc(s("f_aT"), 1)

            def f_norm(g):
                ln_rstd(2 * GROUPS + g, "var", "ln", "rstd", mv, lnv, rstd)

            def f_second(g):
                act.wait_ge(s("f_T1"), g + 1)
                freed(act, s("f_h1_ps"), 6 * g)
                freed(act, s("f_rh_ps"), g)
                act.activation(f_xT, pt(1), ACT.Copy).then_inc(s("f_xT"), 1)

            def f_router(g):
                act.wait_ge(s("f_rh_ps"), g + 1)
                act.activation(f_rh, bank[3][:, 0:GROUP], ACT.Relu, bias=rb1_c[:]).then_inc(s("f_rh"), 1)

            def f_soft(g):
                act.wait_ge(s("f_nmx"), g + 1)
                for j in range(2):
                    act.activation(pr[:, j, 0:EXPERTS], lg[:, j, 0:EXPERTS], ACT.Exp, bias=rt[:, 0, j:j + 1],
                                   accum_out=rt[:, 1, j:j + 1]).then_inc(s("f_sum"), 1)

            def f_soft2(g):
                act.wait_ge(s("f_dif"), g + 1)
                act.activation(rt[:, 4, :], rt[:, 3, :], ACT.Exp).then_inc(s("f_e2"), 1)

            def f_wT_copy(g):
                act.wait_ge(s("f_wT_ps"), g + 1)
                freed(act, s("f_bias"), g)
                act.activation(f_wT, bank[3][0:EXPERTS, 0:GROUP], ACT.Copy).then_inc(s("f_wTc"), 1)

            def relu1(g, e):
                act.wait_ge(s("f_h1_ps"), g * 6 + e + 1)
                freed(act, s("f_h2_ps"), g * 6 + e - 1 if e else g * 6)
                for o in range(2):
                    ins = act.activation(f_h1[e % 2][:, o], pt(4)[:, o], ACT.Relu, bias=eb_c[:, 0, e, o:o + 1])
                ins.then_inc(s("f_h1"), 1)

            def relu2(g, e):
                act.wait_ge(s("f_h2_ps"), g * 6 + e + 1)
                freed(act, s("f_o"), g * 6 + e - 1 if e else g * 6)
                for o in range(2):
                    ins = act.activation(f_h2[e % 2][:, o], pt(5)[:, o], ACT.Relu, bias=eb_c[:, 1, e, o:o + 1])
                ins.then_inc(s("f_h2"), 1)

            def f_experts(g, between):
                f_router(g)
                relu1(g, 0)
                f_soft(g)
                relu1(g, 1)
                f_soft2(g)
                relu2(g, 0)
                relu1(g, 2)
                relu2(g, 1)
                f_wT_copy(g)
                between(f_first)
                relu1(g, 3)
                relu2(g, 2)
                relu1(g, 4)
                relu2(g, 3)
                relu1(g, 5)
                relu2(g, 4)
                between(f_norm)
                relu2(g, 5)
                between(f_second)

            f_first(0)
            f_norm(0)
            f_second(0)
            def body(i):
                f_experts(i, lambda f: f(i + 1))

            repeated(act, GROUPS - 1, body)
            f_experts(GROUPS - 1, lambda f: None)

        @block.vector
        def _(v):
            t = Own(v, s("tab_own"), 0, 0)
            v.wait_ge(s("dlast_in"), 16)
            v.wait_ge(s("iota_tabs"), 3)
            t.did(v.tensor_scalar(tab_t[:, 0, :], dlast[:], -float((R - 1) // 2), 1.0 / R, ALU.add, ALU.mult))
            t.settle()
            t.did(v.tensor_scalar(tab_t[:, 1, :], tab_t[:, 0, :], ROUND, -ROUND, ALU.add, ALU.add))
            t.settle()
            v.tensor_tensor(tab_t[:, 1, :], tab_t[:, 1, :], iota_t[:], ALU.add).then_inc(s("e_row"), 1)
            v.wait_ge(s("e_bc"), 1)
            for c in range(CS):
                t.did(v.tensor_scalar(junk[0:QS, 0:PAIRS], bank[1][0:QS, 0:PAIRS], iota_s[:, c:c + 1], 0.0,
                                      ALU.is_lt, ALU.add, accum_out=tabs[:, 0, c:c + 1]))
                t.settle()
            t.did(v.tensor_scalar(tabs[:, 1, :], tabs[:, 0, :], float(PAIRS - 1), None, ALU.min))
            t.settle()
            t.did(v.tensor_tensor(tabs[:, 2, :], iota_s[:], tabs[:, 1, :], ALU.subtract))
            t.did(v.tensor_copy(tab_i[:, 0, :], tabs[:, 1, :]))
            t.settle()
            t.did(v.tensor_scalar(tabs[:, 3, :], tabs[:, 2, :], float(BLOCKS - 1), None, ALU.min))
            t.did(v.tensor_scalar(tabs[:, 4, :], tabs[:, 2, :], float(R), None, ALU.mult))
            t.settle()
            v.tensor_copy(tab_i[:, 1, :], tabs[:, 3, :]).then_inc(s("tab_done"), 1)
            v.wait_ge(s("u_ps"), 1)
            v.tensor_copy(u_s[:].rearrange("p c k -> p (c k)"), bank[0][:, 0:4]).then_inc(s("u_done"), 1)
            v.wait_ge(s("sd_in"), 16 * 2 * CS)
            v.tensor_copy(src_f, src_i).then_inc(s("src_f"), 1)
            t.did(v.tensor_copy(dst_f, dst_i))
            t.settle()
            for c in range(CS):
                e_ = slice(c * 2 * R, (c + 1) * 2 * R)
                v.tensor_scalar(rel_l[:, e_], dst_f[:, e_], tabs[:, 4, c:c + 1], None, ALU.subtract).then_inc(s("rel"), 1)
            for a in range(4):
                v.wait_ge(s("a_ps"), a + 1)
                to = (a_src, a_rel)[a // 2]
                j0 = 5 * (a % 2)
                v.tensor_copy(to[:, :, j0:j0 + 5].rearrange("p q j -> p j q"),
                              bank[2 + a][0:R, 0:5 * QS].rearrange("p (j q) -> p j q", q=QS)).then_inc(s("a_done"), 1)

            v.memset(p_v[0][:, :, 128:129], 1.0).then_inc(s("v_ones"), 1)
            v.memset(p_v[1][:, :, 128:129], 1.0).then_inc(s("v_ones"), 1)
            v.wait_ge(s("w_in"), 16 * LOADS_EARLY)

            def statistics(own, z, st_, mv_):
                for j in range(2):
                    own.did(v.bn_stats(st_[:, j, :], z[:, j, :]))
                own.settle()
                apart(v, "past_v")
                for j in range(2):
                    own.did(v.bn_aggr(mv_[:, j, :], st_[:, j, :]))
                own.settle()
                return v.tensor_scalar(mv_[:, :, 1], mv_[:, :, 1], EPS, None, ALU.add)

            def p1_norm(g):
                own = Own(v, s("p1a_own"), 4, g)
                v.wait_ge(s("p1_x"), 16 * (g + 1))
                statistics(own, p_x, st, mv).then_inc(s("var"), 1)
                v.wait_ge(s("rstd"), g + 1)
                freed(v, s("p1_T"), g)
                freed(v, s("p1_xn_out"), 16 * g)
                for j in range(2):
                    ins = v.tensor_scalar(p_xn[:, j], p_x[:, j], mv[:, j, 0:1], rstd[:, j:j + 1], ALU.subtract, ALU.mult)
                ins.then_inc(s("p1_xn"), 1)
                own.end()

            def p1_kv(g):
                own = Own(v, s("p1b_own"), 2, g)
                for j in range(2):
                    v.wait_ge(s("p1_kv"), 2 * g + j + 1)
                    own.did(v.tensor_tensor(p_k[:, j], bank[2 + j][0:R, 0:D], bkv_bc[:, 0:D], ALU.add))
                    freed(v, s("p1_sum"), 2 * g)
                    v.tensor_tensor(p_v[j][:, :, 0:128],
                                    bank[2 + j][0:R, D:2 * D].rearrange("p (c n) -> p c n", c=2),
                                    bkv_bc[:, D:2 * D].rearrange("p (c n) -> p c n", c=2),
                                    ALU.add).then_inc(s("p1_kv_read"), 1)
                    own.settle()
                    v.tensor_scalar(p_min[:, j], p_k[:, j], 0.0, None, ALU.min).then_inc(s("p1_min"), 1)
                for j in range(2):
                    v.wait_ge(s("p1_exp"), 2 * g + j + 1)
                    v.scalar_tensor_tensor(p_phi[:, j], p_k[:, j], 0.0, p_exp[:, j], ALU.max,
                                           ALU.add).then_inc(s("p1_phi"), 1)
                own.end()

            p1_norm(0)
            def body(i):
                p1_norm(i + 1)
                p1_kv(i)

            repeated(v, GROUPS - 1, body)
            p1_kv(GROUPS - 1)
            v.wait_ge(s("kv_done"), 1)
            v.wait_ge(s("consts"), 4)
            for c in range(2):
                v.tensor_tensor(kvbd[:, c, :], bank[7][:, c * 129:c * 129 + 128], bmask[:], ALU.mult).then_inc(s("kvbd"), 1)
                v.tensor_scalar(ksbd[:, c, :], bmask[:], bank[7][:, c * 129 + 128:c * 129 + 129], None,
                                ALU.mult).then_inc(s("kvbd"), 1)

            v.wait_ge(s("s2_in"), 16)
            v.wait_ge(s("blk_in"), 16)
            v.wait_ge(s("a_done"), 4)

            def blocks_of(q):
                _, values = nc.values_load_multi_w_load_instructions(
                    blk_row[:, bass.ds(q * CS, CS)], engines=[mybir.EngineType.DVE], min_val=0, max_val=BLOCKS - 1,
                    skip_runtime_bounds_check_because="tab_i is clamped to BLOCKS - 1 and counts up from 0")
                return values

            s2_v = s2_bc.rearrange("p (b n) -> p b n", n=R)
            def body(q):
                at = blocks_of(q)
                for j in range(JS):
                    freed(v, s("s2_e"), q * JS + max(j - 3, 0))
                    v.scalar_tensor_tensor(
                        junk[:, (j % 4) * R:(j % 4 + 1) * R], iota_r[:],
                        a_rel[:, bass.ds(q, 1), j:j + 1].rearrange("p a b -> p (a b)"),
                        s2_v[:, bass.ds(at[j // 2], 1), :].rearrange("p a n -> p (a n)"), ALU.is_equal, ALU.mult,
                        accum_out=a_s2[:, bass.ds(q, 1), j:j + 1].rearrange("p a b -> p (a b)")).then_inc(s("s2_e"), 1)

            repeated(v, QS, body)

            def body(i):
                for h in range(2):
                    v.wait_ge(s(f"attr_in{h}"), i * 16 + 16)
                    v.tensor_tensor(attr_s[:, h], attr_s[:, h], awe[:, None, :].to_broadcast([R, CHUNK, ED]),
                                    ALU.mult).then_inc(s("ew_mul"), 1)
                    v.wait_ge(s("ew_mul"), i * 2 + h + 1)
                    v.tensor_reduce(ew_n[:, bass.ds((i * 2 + h) * CHUNK, CHUNK)], attr_s[:, h], AX.X,
                                    ALU.add).then_inc(s(f"attr_used{h}"), 1)

            repeated(v, CHUNKS // 2, body)
            v.wait_ge(s("attr_used0"), CHUNKS // 2)
            v.wait_ge(s("attr_used1"), CHUNKS // 2)
            v.memset(mark[:], 0.0).then_inc(s("ew_done"), 1)

            def affine(own, z, mv_, rstd_, gain, bias, o, last_sem):
                for j in range(2):
                    own.did(v.tensor_scalar(z[:, j], z[:, j], mv_[:, j, 0:1], rstd_[:, j:j + 1], ALU.subtract, ALU.mult))
                own.settle()
                own.did(v.tensor_tensor(z, z, rv[:, gain:gain + 1, :].to_broadcast([R, 2, D]), ALU.mult))
                own.settle()
                v.tensor_tensor(o, z, rv[:, bias:bias + 1, :].to_broadcast([R, 2, D]), ALU.add).then_inc(s(last_sem), 1)

            def m_queries(g):
                v.wait_ge(s("m_q"), g + 1)
                freed(v, s("m_exp"), g)
                for o in range(2):
                    v.tensor_scalar(m_q[:, o], pt(0)[:, o], bq_c[:, o:o + 1], 0.0, ALU.add,
                                    ALU.min).then_inc(s("m_min"), 1)
                v.wait_ge(s("m_exp"), g + 1)
                v.wait_ge(s("m_qread"), 2 * g + 2)
                freed(v, s("m_nd"), g)
                v.tensor_tensor(m_n, m_e, m_r, ALU.add).then_inc(s("m_phi"), 1)

            def m_attention(g):
                own = Own(v, s("ma_own"), 2, g)
                v.wait_ge(s("m_nd"), g + 1)
                own.did(v.tensor_scalar(m_q, pt(1), 1e-6, None, ALU.add))
                own.settle()
                own.did(v.reciprocal(m_q, m_q))
                own.settle()
                freed(v, s("m_o_ps"), g)
                v.tensor_tensor(m_e, pt(2), m_q, ALU.mult).then_inc(s("m_att"), 1)
                own.end()

            def m_project(g):
                own = Own(v, s("mb_own"), 7, g)
                v.wait_ge(s("m_xn"), 16 * (g + 1))
                freed(v, s("m_T"), g)
                v.tensor_tensor(m_z, xn_in, rv[:, 0:1, :].to_broadcast([R, 2, D]), ALU.add).then_inc(s("m_xb"), 1)
                v.wait_ge(s("m_xb"), g + 1)
                v.wait_ge(s("m_o_ps"), g + 1)
                v.tensor_tensor(m_z, pr_(3), m_z, ALU.add).then_inc(s("m_z"), 1)
                v.wait_ge(s("m_z"), g + 1)
                statistics(own, m_z, st, mv).then_inc(s("var"), 1)
                v.wait_ge(s("rstd"), GROUPS + g + 1)
                affine(own, m_z, mv, rstd, 1, 2, m_y, "m_y")
                own.end()

            def m_keep(g):
                v.wait_ge(s("m_y"), g + 1)
                v.tensor_tensor(m_yb, m_y, rv[:, 3:4, :].to_broadcast([R, 2, D]), ALU.add).then_inc(s("m_yb"), 1)

            def m_hidden(g, o2):
                v.wait_ge(s("m_h1"), g * 4 + o2 + 1)
                freed(v, s("m_d"), 2 * g)
                v.tensor_scalar(m_h[:, 2 * o2 + 1], bank[6][:, 0:GROUP], b1_c[:, 2 * o2 + 1:2 * o2 + 2], 0.0,
                                ALU.add, ALU.max).then_inc(s("m_hread1"), 1)

            def m_last(g):
                own = Own(v, s("mc_own"), 7, g)
                v.wait_ge(s("m_d"), 2 * (g + 1))
                v.wait_ge(s("m_yb"), g + 1)
                v.tensor_tensor(m_z2, pr_(7), m_yb, ALU.add).then_inc(s("m_z2"), 1)
                v.wait_ge(s("m_z2"), g + 1)
                statistics(own, m_z2, st2, mv2).then_inc(s("m_var2"), 1)
                v.wait_ge(s("m_rstd2"), g + 1)
                freed(v, s("m_stored"), 16 * g)
                affine(own, m_z2, mv2, rstd2, 4, 5, m_o, "m_out")
                own.end()

            m_queries(0)
            m_attention(0)
            m_project(0)
            def body(i):
                m_keep(i)
                m_hidden(i, 0)
                m_queries(i + 1)
                m_hidden(i, 1)
                m_hidden(i, 2)
                m_hidden(i, 3)
                m_attention(i + 1)
                m_project(i + 1)
                m_last(i)

            repeated(v, GROUPS - 1, body)
            m_keep(GROUPS - 1)
            for o2 in range(4):
                m_hidden(GROUPS - 1, o2)
            m_last(GROUPS - 1)

            x_ = Own(v, s("soft_own"), 0, 0)
            for h in range(2):
                v.wait_ge(s(f"s1_kept{h}"), QS // 2)
            v.wait_ge(s("s2_e"), QS * JS)
            v.tensor_tensor(a_s2[:], a_s1[:], a_s2[:], ALU.add).then_inc(s("scores"), 1)
            x_.did(v.tensor_scalar(t_l, rel_l, 0.0, None, ALU.is_ge))
            x_.settle()
            x_.did(v.scalar_tensor_tensor(valid, rel_l, float(R), t_l, ALU.is_lt, ALU.mult))
            x_.did(v.memset(reset[:, 0:1], 0.0))
            x_.did(v.memset(reset[:, LROW:LROW + 1], 0.0))
            x_.did(v.tensor_tensor(reset[:, 1:LROW], dst_f[:, 1:LROW], dst_f[:, 0:LROW - 1], ALU.not_equal))
            x_.settle()
            x_.did(v.tensor_scalar(reset[:, 1:LROW], reset[:, 1:LROW], -BIG, None, ALU.mult))
            v.wait_ge(s("u_l"), 1)
            v.wait_ge(s("ew_in"), 16 * CS)
            for k in range(3):
                a, b = 4 * R * k, min(4 * R * (k + 1), LROW)
                x_.did(v.tensor_tensor(t_l[:, a:b], bank[k][0:QS, 0:b - a], ew_l[:, a:b], ALU.add))
            x_.settle()
            x_.did(v.scalar_tensor_tensor(e_l, t_l, 0.01, t_l, ALU.mult, ALU.max))
            x_.settle()
            x_.did(v.tensor_tensor(e_l, e_l, valid, ALU.mult))
            x_.did(v.tensor_scalar(t_l, valid, BIG, -BIG, ALU.mult, ALU.add))
            x_.settle()
            x_.did(v.tensor_tensor(e_l, e_l, t_l, ALU.add))
            x_.settle()

            def scans(first, last_):
                x_.did(v.tensor_tensor_scan(f_l, reset[:, 0:LROW], e_l, first, ALU.add, ALU.max))
                x_.settle()
                x_.did(v.tensor_tensor_scan(b_l[:, ::-1], reset[:, LROW:0:-1], f_l[:, ::-1], last_, ALU.add, ALU.max))
                x_.settle()

            scans(-BIG, -BIG)
            v.tensor_copy(sm[:, 0:1], f_l[:, LROW - 1:LROW]).then_inc(s("summary"), 1)
            v.tensor_copy(sm[:, 1:2], b_l[:, 0:1]).then_inc(s("summary"), 1)
            v.tensor_tensor(sm[:, 2:3], dst_f[:, 0:1], dst_f[:, LROW - 1:LROW], ALU.is_equal).then_inc(s("summary"), 1)
            v.tensor_copy(sm[:, 3:4], dst_f[:, 0:1]).then_inc(s("summary"), 1)
            v.tensor_copy(sm[:, 4:5], dst_f[:, LROW - 1:LROW]).then_inc(s("summary"), 1)
            v.wait_ge(s("sm_row"), 1)
            x_.did(v.tensor_copy(smr[:, 0:5, 0:QS], bank[3][0:1, 0:5 * QS].rearrange("p (k q) -> p k q", q=QS)))
            x_.did(v.memset(smr[:, 5:7, 0:QS], -BIG))
            x_.settle()
            row = lambda k, a, b: smr[:, k, a:b]
            x_.did(v.tensor_tensor(row(7, 1, QS), row(3, 1, QS), row(4, 0, QS - 1), ALU.is_equal))
            x_.settle()
            x_.did(v.tensor_scalar(row(8, 1, QS), row(7, 1, QS), BIG, -BIG, ALU.mult, ALU.add))
            x_.did(v.tensor_tensor(row(9, 1, QS), row(7, 1, QS), row(2, 0, QS - 1), ALU.mult))
            x_.did(v.tensor_tensor(row(10, 1, QS), row(7, 1, QS), row(2, 1, QS), ALU.mult))
            x_.settle()
            x_.did(v.tensor_scalar(row(9, 1, QS), row(9, 1, QS), BIG, -BIG, ALU.mult, ALU.add))
            x_.did(v.tensor_scalar(row(10, 1, QS), row(10, 1, QS), BIG, -BIG, ALU.mult, ALU.add))
            x_.did(v.tensor_tensor(row(0, 0, QS - 1), row(0, 0, QS - 1), row(8, 1, QS), ALU.add))
            x_.did(v.tensor_tensor(row(1, 1, QS), row(1, 1, QS), row(8, 1, QS), ALU.add))
            x_.settle()
            x_.did(v.tensor_tensor_scan(row(5, 1, QS), row(9, 1, QS), row(0, 0, QS - 1), -BIG, ALU.add, ALU.max))
            v.tensor_tensor_scan(smr[:, 6, QS - 2::-1], smr[:, 10, QS - 1:0:-1], smr[:, 1, QS - 1:0:-1], -BIG,
                                 ALU.add, ALU.max).then_inc(s("carry"), 1)
            v.wait_ge(s("carry_c"), 1)
            x_.did(v.tensor_copy(sm[:, 5:7], bank[4][0:QS, 0:2]))
            x_.settle()
            scans(sm[:, 5:6], sm[:, 6:7])
            v.tensor_tensor(e_l, e_l, b_l, ALU.subtract).then_inc(s("p_arg"), 1)
            v.wait_ge(s("p_exp"), 1)
            v.tensor_tensor(t_l, t_l, valid, ALU.mult).then_inc(s("p_l"), 1)
            v.wait_ge(s("pT_done"), 1)
            for a in range(2):
                x_.did(v.tensor_copy(a_p[:, :, 5 * a:5 * a + 5].rearrange("p q j -> p j q"),
                                     bank[5 + a][0:R, 0:5 * QS].rearrange("p (j q) -> p j q", q=QS)))
            v.memset(acc[:], 0.0).then_inc(s("summed"), 1)
            v.memset(mark[:], 0.0).then_inc(s("p_done"), 1)
            x_.settle()

            def one_hot(q, z):
                for k in range(2):
                    at = lambda a: a[:, bass.ds(q, 1), 2 * (z % CS) + k:2 * (z % CS) + k + 1].rearrange("p a b -> p (a b)")
                    v.tensor_scalar(onehot[:, 2 * (z % 2) + k, :], iota_r[:], at(a_rel), at(a_p), ALU.is_equal,
                                    ALU.mult).then_inc(s("onehot"), 1)

            def body(i):
                at = [*blocks_of(i * 2), *blocks_of(i * 2 + 1)]

                def add_up(z):
                    v.wait_ge(s("rows_free"), i * SLOTS + SLOTS + z + 1)
                    v.wait_ge(s("summed"), i * SLOTS + z + 1)
                    to = accv[:, bass.ds(at[z], 1), :].rearrange("p b n -> p (b n)")
                    v.tensor_tensor(to, bank[z % 2][0:R, 0:D + 1], to, ALU.add).then_inc(s("summed"), 1)

                for z in range(SLOTS):
                    if z >= 2:
                        add_up(z - 2)
                    one_hot(i * 2 + z // CS, z)
                add_up(SLOTS - 2)
                add_up(SLOTS - 1)

            repeated(v, QS // 2, body)
            v.wait_ge(s("summed"), STEPS + 1)
            v.memset(mark[:], 0.0).then_inc(s("agg_done"), 1)

            v.memset(lg[:], -BIG).then_inc(s("pads"), 1)
            v.memset(pr[:], -1.0).then_inc(s("pads"), 1)
            v.wait_ge(s("pads"), 2)

            def f_mean(g):
                own = Own(v, s("fa_own"), 4, g)
                den = acc[:].rearrange("p (g j n) -> p g j n", j=2, n=D + 1)[:, bass.ds(g, 1), :, D]
                den = den.rearrange("p g j -> p (g j)")
                freed(v, s("f_x1"), g)
                own.did(v.tensor_scalar(dn[:, 0, :], den, 0.5, None, ALU.max))
                own.did(v.tensor_scalar(dn[:, 1, :], den, 0.0, None, ALU.is_gt))
                own.settle()
                own.did(v.reciprocal(dn[:, 0, :], dn[:, 0, :]))
                own.did(v.tensor_scalar(dn[:, 2, :], dn[:, 1, :], -1.0, 1.0, ALU.mult, ALU.add))
                own.settle()
                freed(v, s("f_T"), g)
                for j in range(2):
                    a = acc[:].rearrange("p (g j n) -> p g j n", j=2, n=D + 1)[:, bass.ds(g, 1), j, 0:D]
                    v.tensor_scalar(f_an[:, j], a.rearrange("p g n -> p (g n)"), dn[:, 0, j:j + 1], None,
                                    ALU.mult).then_inc(s("f_an"), 1)
                own.end()

            def f_rows(g):
                own = Own(v, s("fb_own"), 9, g)
                v.wait_ge(s("f_rows"), 48 * (g + 1))
                freed(v, s("f_T1"), g)
                for j in range(2):
                    own.did(v.tensor_scalar(f_t[:, j], xn_in[:, j], dn[:, 2, j:j + 1], None, ALU.mult))
                own.settle()
                v.wait_ge(s("f_gnn"), g + 1)
                own.did(v.scalar_tensor_tensor(f_t[:, 0], pr_(2)[:, 0], dn[:, 1, 0:1], f_t[:, 0], ALU.mult, ALU.add))
                v.scalar_tensor_tensor(f_t[:, 1], pr_(2)[:, 1], dn[:, 1, 1:2], f_t[:, 1], ALU.mult,
                                       ALU.add).then_inc(s("f_r"), 1)
                v.wait_ge(s("f_r"), g + 1)
                own.settle()
                own.did(v.scalar_tensor_tensor(f_t, f_t, 0.0, xn_in, ALU.max, ALU.add))
                own.settle()
                own.did(v.tensor_tensor(f_t, f_t, f_x, ALU.add))
                own.settle()
                freed(v, s("f_start"), 2 * g)
                v.tensor_tensor(f_x1, f_t, f_mix, ALU.add).then_inc(s("f_x1"), 1)
                v.wait_ge(s("f_x1"), g + 1)
                statistics(own, f_x1, st, mv).then_inc(s("var"), 1)
                v.wait_ge(s("rstd"), 2 * GROUPS + g + 1)
                for j in range(2):
                    v.tensor_scalar(f_t[:, j], f_x1[:, j], mv[:, j, 0:1], rstd[:, j:j + 1], ALU.subtract,
                                    ALU.mult).then_inc(s("f_xn1"), 1)
                own.end()

            def f_route1(g):
                own = Own(v, s("fc_own"), 2, g)
                v.wait_ge(s("f_lg_ps"), g + 1)
                own.did(v.tensor_tensor(lg[:, :, 0:EXPERTS],
                                        bank[3][0:R, 256:272].rearrange("p (j n) -> p j n", j=2)[:, :, 0:EXPERTS],
                                        rb2_bc[:, None, :].to_broadcast([R, 2, EXPERTS]), ALU.add))
                own.settle()
                own.did(v.tensor_reduce(rt[:, 2, :], lg[:], AX.X, ALU.max))
                own.settle()
                v.tensor_scalar(rt[:, 0, :], rt[:, 2, :], -1.0, None, ALU.mult).then_inc(s("f_nmx"), 1)
                own.end()

            def f_route2(g):
                own = Own(v, s("fd_own"), 8, g)
                v.wait_ge(s("f_sum"), 2 * (g + 1))
                own.did(v.reciprocal(rt[:, 2, :], rt[:, 1, :]))
                own.settle()
                for j in range(2):
                    own.did(v.tensor_scalar(pr[:, j, 0:EXPERTS], pr[:, j, 0:EXPERTS], rt[:, 2, j:j + 1], None, ALU.mult))
                own.settle()
                apart(v, "past_v")
                for j in range(2):
                    own.did(v.max(top[:, j, :], pr[:, j, :]))
                own.settle()
                apart(v, "past_v")
                for j in range(2):
                    own.did(v.max_index(topi[:, j, :], top[:, j, :], pr[:, j, :]))
                v.tensor_tensor(rt[:, 3, :], top[:, :, 1], top[:, :, 0], ALU.subtract).then_inc(s("f_dif"), 1)
                own.settle()
                own.did(v.tensor_copy(topf[:], topi[:, :, 0:2]))
                own.end()

            def f_route3(g):
                own = Own(v, s("fe_own"), 7, g)
                v.wait_ge(s("f_e2"), g + 1)
                own.did(v.tensor_scalar(rt[:, 5, :], rt[:, 4, :], 1.0, None, ALU.add))
                own.settle()
                own.did(v.reciprocal(rt[:, 6, :], rt[:, 5, :]))
                own.settle()
                own.did(v.tensor_tensor(rt[:, 7, :], rt[:, 6, :], rt[:, 4, :], ALU.mult))
                own.settle()
                for j in range(2):
                    own.did(v.tensor_scalar(wt1[:, j], iota_e[:], topf[:, j, 0:1], rt[:, 6, j:j + 1], ALU.is_equal, ALU.mult))
                    own.did(v.tensor_scalar(wt2[:, j], iota_e[:], topf[:, j, 1:2], rt[:, 7, j:j + 1], ALU.is_equal, ALU.mult))
                own.settle()
                v.tensor_tensor(wt[:], wt1[:], wt2[:], ALU.add).then_inc(s("f_wt"), 1)
                own.end()

            def f_begin(g):
                v.wait_ge(s("f_bias"), g + 1)
                freed(v, s("f_stored"), 16 * g)
                for j in range(2):
                    v.tensor_tensor(f_x2[:, j], pr_(2)[:, j], f_x1[:, j], ALU.add).then_inc(s("f_start"), 1)
                v.wait_ge(s("f_start"), 2 * (g + 1))

            def f_add(g, e):
                v.wait_ge(s("f_o"), g * 6 + e + 1)
                if e:
                    v.wait_ge(s("f_x2"), g * 6 + e)
                for j in range(2):
                    ins = v.scalar_tensor_tensor(f_x2[:, j], pr_(6 + e % 2)[:, j], wt[:, j, e:e + 1], f_x2[:, j],
                                                 ALU.mult, ALU.add)
                ins.then_inc(s("f_x2"), 1)

            def f_experts(g, between):
                f_route1(g)
                f_route2(g)
                f_route3(g)
                between(f_mean)
                f_begin(g)
                f_add(g, 0)
                f_add(g, 1)
                f_add(g, 2)
                between(f_rows)
                for e in range(3, EXPERTS):
                    f_add(g, e)

            f_mean(0)
            f_rows(0)
            def body(i):
                f_experts(i, lambda f: f(i + 1))

            repeated(v, GROUPS - 1, body)
            f_experts(GROUPS - 1, lambda f: None)


_INS = ["x", "src", "dst", "attr", "wselfT", "wfuncT", "wfunc", "att_nodes", "att_edge", "wq", "wk", "wv", "wo",
        "w1", "w2", "bq", "b1", "bkv", "rowvecs", "rw1", "rb1", "rw2", "rb2", "ew1", "ew2", "ew3", "eb1", "eb2", "eb3"]


def lay_out(i):
    import numpy as np

    a = {k: np.asarray(v) for k, v in i.items()}
    c = np.ascontiguousarray
    col = lambda b: c(b.reshape(-1, 128).T)
    return dict(
        x=a["x"], src=a["src"], dst=a["dst"], attr=a["edge_attr_64"],
        wselfT=c(a["L0_gnn_W_self"].T), wfuncT=c(a["L0_gnn_W_func"].T), wfunc=a["L0_gnn_W_func"],
        att_nodes=c(a["L0_gnn_W_att"][0, :2 * D].reshape(2, 2, 128).transpose(2, 1, 0)),
        att_edge=c(a["L0_gnn_W_att"][:, 2 * D:]),
        wq=a["L0_mix_Wq"], wk=a["L0_mix_Wk"], wv=a["L0_mix_Wv"], wo=a["L0_mix_Wo"], w1=a["L0_mix_W1"], w2=a["L0_mix_W2"],
        bq=col(a["L0_mix_bq"]), b1=col(a["L0_mix_b1"]),
        bkv=c(np.concatenate([a["L0_mix_bk"], a["L0_mix_bv"]])[None]),
        rowvecs=c(np.stack([a["L0_mix_" + k] for k in ("bo", "ln1_g", "ln1_b", "b2", "ln2_g", "ln2_b")])),
        rw1=a["L0_ffn_router_w1"], rb1=col(a["L0_ffn_router_b1"]), rw2=a["L0_ffn_router_w2"], rb2=a["L0_ffn_router_b2"][None],
        ew1=a["L0_ffn_expert_w1"], ew2=a["L0_ffn_expert_w2"], ew3=a["L0_ffn_expert_w3"],
        eb1=c(a["L0_ffn_expert_b1"].reshape(EXPERTS, 2, 128).transpose(2, 0, 1)),
        eb2=c(a["L0_ffn_expert_b2"].reshape(EXPERTS, 2, 128).transpose(2, 0, 1)), eb3=a["L0_ffn_expert_b3"],
    )


def kernel(**inputs):
    import concourse.bacc as bacc
    from concourse.bass_utils import run_bass_kernel_spmd as run

    arrays = lay_out(inputs)
    nc = bacc.Bacc("TRN2", target_bir_lowering=False, num_devices=1)
    args = [nc.dram_tensor(f"in_{n}", arrays[n].shape, mybir.dt.from_np(arrays[n].dtype), kind="ExternalInput").ap()
            for n in _INS]
    out = nc.dram_tensor("out_0", (N, D), F32, kind="ExternalOutput").ap()
    build(nc, *args, out)
    r = run(nc, [{f"in_{n}": arrays[n] for n in _INS}], core_ids=[0])
    return r.results[0]["out_0"]
```

```python
from contextlib import ExitStack

import concourse.bass as bass
from concourse import mybir

F32 = mybir.dt.float32
I32 = mybir.dt.int32
U32 = mybir.dt.uint32
BF16 = mybir.dt.bfloat16
ALU = mybir.AluOpType
ACT = mybir.ActivationFunctionType
AX = mybir.AxisListType

N, D = 6250, 256
E, ED = 100000, 64
R = 125
GROUP = 2 * R
GROUPS = N // GROUP
BLOCKS = N // R
PAIRS = E // (2 * R)
STEPS = 450
QS, CS = 75, 6
JS = 2 * CS
LROW = CS * 2 * R
FF = 1024
FC = FF // 128
HEAD = 32
EXPERTS = 6
LO = 128
HIS = -(-N // LO)
PART = 3
ZS = STEPS // GROUPS
HS = ZS // CS
CHUNK = 16
BIG = 1e30
BIG = 1e30
EPS = 1e-5
ROUND = 12582912.0


class Own:

    def __init__(self, eng, sem, per, group):
        self.eng, self.sem, self.per, self.group, self.k = eng, sem, per, group, 0

    def did(self, ins):
        ins.then_inc(self.sem, 1)
        self.k += 1

    def settle(self):
        self.eng.wait_ge(self.sem, self.group * self.per + self.k)

    def end(self):
        assert self.k == self.per, (self.k, self.per)


def freed(eng, sem, count):
    if not (isinstance(count, int) and count <= 0):
        eng.wait_ge(sem, count)


def repeated(eng, n, body):
    body(0)
    with eng.Fori(1, n) as i:
        body(i)


def build(nc, x, src, dst, attr, wselfT, wfuncT, wfunc, att_nodes, att_edge, wq, wk, wv, wo, w1, w2,
          bq, b1, bkv, rowvecs, rw1, rb1, rw2, rb2, ew1, ew2, ew3, eb1, eb2, eb3, out):
    assert STEPS >= PAIRS + BLOCKS - 1 and QS * CS == STEPS
    ctx = ExitStack()
    with ctx:
        def sb(name, shape, dt=F32):
            return ctx.enter_context(nc.sbuf_tensor(name, shape, dt))

        sems = {}

        def s(name):
            if name not in sems:
                sems[name] = ctx.enter_context(nc.semaphore(name))
            return sems[name]

        xn_rows = nc.dram_tensor("xn_rows", (N, D), F32).ap()
        xnT_d = nc.dram_tensor("xnT_d", (GROUPS, 128, 2 * GROUP), F32).ap()
        mix_rows = nc.dram_tensor("mix_rows", (N, D), F32).ap()
        s1_d = nc.dram_tensor("s1_d", (N, 1), F32).ap()
        s2_d = nc.dram_tensor("s2_d", (1, N), F32).ap()
        ew_d = nc.dram_tensor("ew_d", (PAIRS, 2 * R), F32).ap()
        blk_d = nc.dram_tensor("blk_d", (STEPS,), I32).ap()
        lr_d = nc.dram_tensor("lr_d", (QS, 2 * LROW), BF16).ap()

        def rows_of(t, g):
            v = t.rearrange("(g j p) d -> g p j d", j=2, p=R)
            return v[bass.ds(g, 1)].rearrange("g p j d -> (g p) j d")

        ident = sb("ident", [128, 128])
        bmask = sb("bmask", [128, 128])
        iota_r = sb("iota_r", [R, R])
        iota_e = sb("iota_e", [R, EXPERTS])
        iota_s = sb("iota_s", [QS, CS])
        iota_t = sb("iota_t", [1, PAIRS])
        iota_p = sb("iota_p", [128, 1])
        iota_h = sb("iota_h", [R, HIS])
        ones_row = sb("ones_row", [1, 128])
        rv = sb("rv", [R, 6, D])
        rb2_bc = sb("rb2_bc", [R, EXPERTS])
        awe = sb("awe", [R, ED])
        bq_c = sb("bq_c", [128, 2])
        b1_c = sb("b1_c", [128, FC])
        rb1_c = sb("rb1_c", [128, 1])
        eb_c = sb("eb_c", [128, 2, EXPERTS, 2])
        eb3_s = sb("eb3_s", [EXPERTS, D])
        wq_s = sb("wq_s", [128, 2, D])
        wo_s = sb("wo_s", [128, 2, D])
        w1_s = sb("w1_s", [128, 2, FF])
        w2_s = sb("w2_s", [128, FC, D])
        wself_s = sb("wself_s", [128, 2, D])
        wfunc_s = sb("wfunc_s", [128, 2, D])
        wfuncT_s = sb("wfuncT_s", [128, 2, D])
        rw1_s = sb("rw1_s", [128, 2, 128])
        rw2_s = sb("rw2_s", [128, EXPERTS])
        attn_c = sb("attn_c", [128, 2, 2])
        u_s = sb("u_s", [128, 2, 2])
        kvbd = sb("kvbd", [128, 2, 128])
        ksbd = sb("ksbd", [128, 2, 128])
        a_src = sb("a_src", [R, QS, JS], I32)
        a_rel = sb("a_rel", [R, QS, JS])
        a_hi = sb("a_hi", [R, QS, JS])
        a_u = sb("a_u", [R, QS, JS])
        a_p = a_hi
        s1_p = sb("s1_p", [128, PART, HIS], BF16)
        s2_p = sb("s2_p", [R, CS * QS, PART], BF16)
        a_s = sb("a_s", [R, 2, JS])
        s1_rows = sb("s1_rows", [HIS, LO])
        blk_row = sb("blk_row", [1, STEPS], I32)
        acc = sb("acc", [R, BLOCKS * (D + 1)])
        accv = acc[:].rearrange("p (b n) -> p b n", n=D + 1)

        def early(k, n=LROW):
            return acc[0:QS, k * (LROW + 4):k * (LROW + 4) + n]

        src_i, dst_i, src_f, dst_f, rel_l = early(0).bitcast(I32), early(1).bitcast(I32), early(2), early(3), early(4)
        hi_l = early(0)
        lr_l = early(5, LROW).bitcast(BF16)
        lr_l = lr_l.rearrange("p (a e) -> p a e", a=2)
        s2_rows = early(6, CS * R)
        ew_l, reset, e_l, b_l = early(0), early(1, LROW + 1), early(2), early(4)
        valid, t_l, f_l = early(5), early(6), early(7)
        attr_s = acc[:, 5 * (LROW + 4):5 * (LROW + 4) + 2 * CHUNK * ED].rearrange("p (h k f) -> p h k f", h=2, f=ED)
        ew_n = acc[:, 6 * (LROW + 4) + CHUNK * ED:6 * (LROW + 4) + CHUNK * ED + E // R]
        wexp = sb("wexp", [128, 3 * EXPERTS * 2 * D])
        wexpv = wexp[:].rearrange("p (l e c n) -> p l e c n", l=3, e=EXPERTS, c=2)
        lr_bc = [wexp[:, k * LROW:(k + 1) * LROW].bitcast(BF16) for k in range(HS)]
        lr_oh = [wexp[:, HS * LROW + k * (LROW + 2):HS * LROW + (k + 1) * (LROW + 2)].bitcast(BF16) for k in range(HS)]
        ring = sb("ring", [R, 2 * CS, D + 1])
        onehot = sb("onehot", [R, 2 * CS, R])
        junk = onehot[:].rearrange("p a b -> p (a b)")
        tabs = sb("tabs", [QS, 8, CS])
        tab_i = sb("tab_i", [QS, 2, CS], I32)
        dlast = sb("dlast", [1, PAIRS], I32)
        idx_slot = sb("idx_slot", [R, HS, JS], I32)
        mark = sb("mark", [1, 1])
        sm = sb("sm", [QS, 8])
        smr = sb("smr", [1, 12, 92])
        work = sb("work", [128, 16 * 512])

        def w(k, shape, n=1):
            v = work[0:shape[0], 512 * k:512 * (k + n)]
            size = 1
            for a in shape[1:]:
                size *= a
            v = v[:, 0:size]
            if len(shape) == 3:
                v = v.rearrange("p (a b) -> p a b", a=shape[1])
            return v

        xn_in, xnT_in = w(0, [R, 2, D]), w(1, [128, 2, GROUP])
        p_x, p_xn, p_xnT = w(2, [R, 2, D]), w(3, [R, 2, D]), w(4, [128, 2, GROUP])
        p_s = w(5, [2, GROUP])
        p_k, p_min, p_exp, p_phi = w(6, [R, 2, D]), w(7, [R, 2, D]), w(8, [R, 2, D]), w(9, [R, 2, D])
        p_v = [w(10, [R, 2, 129]), w(11, [R, 2, 129])]
        wkv_s, bkv_bc, zeros = w(12, [128, 2, 2 * D], 2), w(14, [R, 2 * D]), w(15, [128, 260])
        tab_t = w(10, [1, 2, PAIRS], 2)
        away, sel = w(6, [R, HS, JS * HIS], 4), w(10, [R, JS, HIS], 2)
        s2_t = w(12, [R, 2, CS * QS], 2)
        s1_t = w(14, [128, 2, HIS])
        m_q, m_e, m_r, m_n = w(2, [128, 2, GROUP]), w(3, [128, 2, GROUP]), w(4, [128, 2, GROUP]), w(5, [128, 2, GROUP])
        m_z, m_y, m_yb, m_yT = w(6, [R, 2, D]), w(7, [R, 2, D]), w(8, [R, 2, D]), w(9, [128, 2, GROUP])
        m_h = w(10, [128, FC, GROUP], 4)
        m_z2, m_o = w(14, [R, 2, D]), w(15, [R, 2, D])
        f_x, f_mix, f_an, f_aT = w(2, [R, 2, D]), w(3, [R, 2, D]), w(4, [R, 2, D]), w(5, [128, 2, GROUP])
        f_t, f_x1, f_xT, f_x2 = w(6, [R, 2, D]), w(7, [R, 2, D]), w(8, [128, 2, GROUP]), w(9, [R, 2, D])
        f_h1 = [w(10, [128, 2, GROUP]), w(11, [128, 2, GROUP])]
        f_h2 = [w(12, [128, 2, GROUP]), w(13, [128, 2, GROUP])]
        f_rh, f_wT = w(14, [128, GROUP]), w(15, [EXPERTS, GROUP])
        st = sb("st", [R, 2, 6])
        mv = sb("mv", [R, 2, 2])
        lnv = sb("lnv", [R, 2])
        rstd = sb("rstd", [R, 2])
        st2, mv2 = sb("st2", [R, 2, 6]), sb("mv2", [R, 2, 2])
        lnv2, rstd2 = sb("lnv2", [R, 2]), sb("rstd2", [R, 2])
        dn = sb("dn", [R, 3, 2])
        lg = sb("lg", [R, 2, 8])
        pr = sb("pr", [R, 2, 8])
        top = sb("top", [R, 2, 8])
        topi = sb("topi", [R, 2, 8], U32)
        topf = sb("topf", [R, 2, 2])
        rt = sb("rt", [R, 8, 2])
        wt1, wt2, wt = sb("wt1", [R, 2, EXPERTS]), sb("wt2", [R, 2, EXPERTS]), sb("wt", [R, 2, EXPERTS])

        bank = [ctx.enter_context(nc.psum_tensor(f"bank{i}", [128, 512], F32)) for i in range(8)]

        def pt(b):
            return bank[b][:, 0:2 * GROUP].rearrange("p (c n) -> p c n", c=2)

        def pr_(b):
            return bank[b][0:R, :].rearrange("p (j n) -> p j n", j=2)

        def apart(eng, name):
            eng.sem_inc(s(name), 1)

        block = ctx.enter_context(nc.Block())
        LOADS_EARLY, LOADS_LATE, CONSTS = 27, 3 * EXPERTS, 8

        @block.sync
        def _(sp):
            def load(sem, dst_, src_):
                sp.dma_start(dst_, src_).then_inc(s(sem), 16)

            with nc.allow_non_contiguous_dma(reason="one index of each pair of edge tiles"):
                load("dlast_in", dlast[:], dst.rearrange("(t e) -> t e", e=2 * R)[:, 2 * R - 1:2 * R]
                     .rearrange("t e -> e t"))
            cols = lambda t: t.rearrange("(c p) n -> p c n", p=128)
            load("w_in", wfunc_s[:], cols(wfunc))
            load("w_in", attn_c[:], att_nodes)
            load("p1_x", p_x, rows_of(x, 0))
            load("w_in", wkv_s[:, :, 0:D], cols(wk))
            load("w_in", wkv_s[:, :, D:2 * D], cols(wv))
            load("w_in", bkv_bc, bkv.to_broadcast([R, 2 * D]))
            load("w_in", wq_s[:], cols(wq))
            load("w_in", wo_s[:], cols(wo))
            load("w_in", w1_s[:], cols(w1))
            load("w_in", w2_s[:], cols(w2))
            load("w_in", bq_c[:], bq)
            load("w_in", b1_c[:], b1)
            load("w_in", awe[:], att_edge.to_broadcast([R, ED]))
            load("w_in", rb2_bc[:], rb2.to_broadcast([R, EXPERTS]))
            load("w_in", rb1_c[:], rb1)
            for k in range(6):
                load("w_in", rv[:, k, :], rowvecs[k:k + 1, :].to_broadcast([R, D]))
            load("w_in", eb_c[:, 0], eb1)
            load("w_in", eb_c[:, 1], eb2)
            load("w_in", eb3_s[:], eb3)
            load("w_in", wself_s[:], cols(wselfT))
            load("w_in", wfuncT_s[:], cols(wfuncT))
            load("w_in", rw1_s[:], cols(rw1))
            load("w_in", rw2_s[:], rw2)
            sp.wait_ge(s("tab_done"), 1)
            load("blk_out", blk_d.rearrange("(q c) -> q c", c=CS), tab_i[:, 1, :])
            sp.wait_ge(s("blk_out"), 16)
            load("blk_in", blk_row[:], blk_d[None, :])

            attr_v = attr.rearrange("(p c k) f -> c p k f", p=R, k=CHUNK)

            def pass1(g, more):
                sp.wait_ge(s("p1_xn"), g + 1)
                if more:
                    load("p1_x", p_x, rows_of(x, g + 1))
                load("p1_xn_out", rows_of(xn_rows, g), p_xn)
                for h in range(2):
                    freed(sp, s(f"attr_used{h}"), g)
                    load(f"attr_in{h}", attr_s[:, h], attr_v[bass.ds(g * 2 + h, 1)].rearrange("c p k f -> (c p) k f"))
                sp.wait_ge(s("p1_xnT"), g + 1)
                load("p1_xnT_out", xnT_d[bass.ds(g, 1)].rearrange("g p n -> (g p) n"),
                     p_xnT.rearrange("p c n -> p (c n)"))
                sp.wait_ge(s("p1_s"), g + 1)
                load("p1_s_out", s1_d.rearrange("(g n) a -> a g n", n=GROUP)[:, bass.ds(g, 1), :]
                     .rearrange("a g n -> a (g n)"), p_s[0:1, :])
                load("p1_s_out", s2_d.rearrange("a (g n) -> a g n", n=GROUP)[:, bass.ds(g, 1), :]
                     .rearrange("a g n -> a (g n)"), p_s[1:2, :])

            def body(i):
                pass1(i, True)

            repeated(sp, GROUPS - 1, body)
            pass1(GROUPS - 1, False)
            for h in range(2):
                sp.wait_ge(s(f"attr_used{h}"), GROUPS)
            load("ew_out", ew_d.rearrange("t e -> (t e)").rearrange("(p k) -> p k", p=R), ew_n)
            sp.wait_ge(s("p1_s_out"), 32 * GROUPS)
            sp.wait_ge(s("consts"), CONSTS)
            load("s1_in", s1_rows[0:HIS - 1, :], s1_d[0:(HIS - 1) * LO, :].rearrange("(h l) a -> h (l a)", l=LO))
            load("s1_in", s1_rows[HIS - 1:HIS, 0:N - (HIS - 1) * LO], s1_d[(HIS - 1) * LO:N, :].rearrange("n a -> a n"))
            sp.wait_ge(s("lr_done"), 2)
            load("lr_out", lr_d, lr_l.rearrange("p a e -> p (a e)"))
            sp.wait_ge(s("lr_out"), 16)

            def body(i):
                for h in range(HS):
                    freed(sp, s("lr_oh"), i * HS + h - HS + 1)
                    load(f"lr_in{h}", lr_bc[h], lr_d[bass.ds(i * HS + h, 1)].to_broadcast([128, 2 * LROW]))

            repeated(sp, QS // HS, body)
            sp.wait_ge(s("lr_used"), QS)
            for l, t in enumerate((ew1, ew2, ew3)):
                for e in range(EXPERTS):
                    load("wexp_in", wexpv[:, l, e], cols(t[e]))
            sp.wait_ge(s("p1_xn_out"), 16 * GROUPS)
            sp.wait_ge(s("p1_xnT_out"), 16 * GROUPS)

            def mix_in(g):
                freed(sp, s("m_q"), g)
                load("m_xnT", xnT_in.rearrange("p c n -> p (c n)"),
                     xnT_d[bass.ds(g, 1)].rearrange("g p n -> (g p) n"))
                freed(sp, s("m_xb"), g)
                load("m_xn", xn_in, rows_of(xn_rows, g))

            def mix_out(g):
                sp.wait_ge(s("m_out"), g + 1)
                load("m_stored", rows_of(mix_rows, g), m_o)

            mix_in(0)
            def body(i):
                mix_in(i + 1)
                if not isinstance(i, int):
                    mix_out(i - 1)

            repeated(sp, GROUPS - 1, body)
            mix_out(GROUPS - 2)
            mix_out(GROUPS - 1)
            sp.wait_ge(s("m_stored"), 16 * (GROUPS + 1))

            def last_in(g):
                freed(sp, s("f_gnn"), g)
                load("f_xnT", xnT_in.rearrange("p c n -> p (c n)"),
                     xnT_d[bass.ds(g, 1)].rearrange("g p n -> (g p) n"))
                freed(sp, s("f_x1"), g)
                load("f_rows", xn_in, rows_of(xn_rows, g))
                load("f_rows", f_x, rows_of(x, g))
                load("f_rows", f_mix, rows_of(mix_rows, g))

            def last_out(g):
                sp.wait_ge(s("f_x2"), EXPERTS * (g + 1))
                load("f_stored", rows_of(out, g), f_x2)

            last_in(0)
            def body(i):
                last_in(i + 1)
                last_out(i)

            repeated(sp, GROUPS - 1, body)
            last_out(GROUPS - 1)
            sp.wait_ge(s("f_stored"), 16 * GROUPS)

        @block.gpsimd
        def _(pool):
            own = Own(pool, s("pool_own"), 0, 0)
            iota = dict(allow_small_or_imprecise_dtypes=True)
            pool.iota(iota_t[:], [[1, PAIRS]], base=0, channel_multiplier=0, **iota).then_inc(s("iota_tabs"), 1)
            pool.iota(iota_s[:], [[1, CS]], base=0, channel_multiplier=CS, **iota).then_inc(s("iota_tabs"), 1)
            pool.memset(ones_row[:], 1.0).then_inc(s("iota_tabs"), 1)
            own.did(pool.memset(ident[:], 0.0))
            own.did(pool.memset(bmask[:], 1.0))
            own.settle()
            pool.affine_select(out=ident[:], in_=ident[:], compare_op=ALU.not_equal, fill=1.0, base=0,
                               pattern=[[-1, 128]], channel_multiplier=1).then_inc(s("ident_done"), 1)
            bm = bmask[:].rearrange("p (b k) -> p b k", k=HEAD)
            own.did(pool.affine_select(out=bm, in_=bm, compare_op=ALU.is_ge, fill=0.0, base=0,
                                       pattern=[[-HEAD, 128 // HEAD], [0, HEAD]], channel_multiplier=1))
            own.settle()
            pool.affine_select(out=bm, in_=bm, compare_op=ALU.is_ge, fill=0.0, base=HEAD - 1,
                               pattern=[[HEAD, 128 // HEAD], [0, HEAD]],
                               channel_multiplier=-1).then_inc(s("consts"), 1)
            pool.iota(iota_r[:], [[1, R]], base=0, channel_multiplier=0, **iota).then_inc(s("consts"), 1)
            pool.iota(iota_e[:], [[1, EXPERTS]], base=0, channel_multiplier=0, **iota).then_inc(s("consts"), 1)
            pool.memset(zeros, 0.0).then_inc(s("consts"), 1)

            pool.iota(iota_p[:], [[0, 1]], base=0, channel_multiplier=1, **iota).then_inc(s("consts"), 1)
            pool.iota(iota_h[:], [[1, HIS]], base=0, channel_multiplier=0, **iota).then_inc(s("consts"), 1)
            pool.memset(s1_rows[:], 0.0).then_inc(s("consts"), 1)
            pool.memset(ring[:, :, D:D + 1], 1.0).then_inc(s("consts"), 1)

            pool.wait_ge(s("tab_done"), 1)
            for c in range(CS):
                at = bass.IndirectOffsetOnAxis(ap=tab_i[:, 0, c:c + 1], axis=0)
                for d_, s_ in ((src_i, src), (dst_i, dst)):
                    pool.indirect_dma_start(d_[:, c * 2 * R:(c + 1) * 2 * R], None,
                                            s_.rearrange("(t e) -> t e", e=2 * R), at).then_inc(s("sd_in"), 16)

            pool.wait_ge(s("w_in"), 16 * LOADS_EARLY)

            def body(i):
                own = Own(pool, s("attr_own"), 1, i)
                for h in range(2):
                    pool.wait_ge(s(f"attr_in{h}"), i * 16 + 16)
                    ins = pool.tensor_tensor(attr_s[:, h], attr_s[:, h],
                                             awe[:, None, :].to_broadcast([R, CHUNK, ED]), ALU.mult)
                    if h == 1:
                        ins.then_inc(s("attr_mul1"), 1)
                    else:
                        own.did(ins)
                        own.settle()
                        pool.tensor_tensor(attr_s[:, h, :, 0:ED // 2], attr_s[:, h, :, 0:ED // 2],
                                           attr_s[:, h, :, ED // 2:ED], ALU.add).then_inc(s("attr_mul0"), 1)

            repeated(pool, GROUPS, body)
            pool.wait_ge(s("p1_s_out"), 32 * GROUPS)
            pool.wait_ge(s("ew_out"), 16)
            for c in range(CS):
                pool.indirect_dma_start(s2_rows[:, c * R:(c + 1) * R], None, s2_d.rearrange("a (b n) -> (a b) n", n=R),
                                        bass.IndirectOffsetOnAxis(ap=tab_i[:, 1, c:c + 1], axis=0)
                                        ).then_inc(s("s2_in"), 16)
            pool.wait_ge(s("a_done"), 6)

            def body(q):
                for h in range(HS):
                    p = q * HS + h
                    freed(pool, s("selected"), p - HS + 1)
                    pool.tensor_tensor(
                        away[:, h, :].rearrange("p (j n) -> p j n", n=HIS),
                        iota_h[:, None, :].to_broadcast([R, JS, HIS]),
                        a_hi[:, bass.ds(p, 1), :].rearrange("p a j -> p j a").to_broadcast([R, JS, HIS]),
                        ALU.subtract).then_inc(s("away"), 1)

            repeated(pool, QS // HS, body)
            pool.wait_ge(s("a_ps"), 6)
            pool.wait_ge(s("lr_done"), 1)
            for c in range(CS):
                pool.indirect_dma_start(ew_l[:, c * 2 * R:(c + 1) * 2 * R], None, ew_d,
                                        bass.IndirectOffsetOnAxis(ap=tab_i[:, 0, c:c + 1], axis=0)
                                        ).then_inc(s("ew_in"), 16)
            def body(i):
                for h in range(HS):
                    q = i * HS + h
                    for c in range(CS):
                        freed(pool, s(f"rows_in{c}"), (q - HS + 1) * 32)
                    pool.tensor_copy(idx_slot[:, h, :], a_src[:, bass.ds(q, 1), :]
                                     .rearrange("p a j -> p (a j)")).then_inc(s("idx"), 1)
                    for c in range(CS):
                        freed(pool, s("stepped"), q * CS - CS + c + 1)
                        if c == 0:
                            pool.wait_ge(s("idx"), q + 1)
                        apart(pool, "past")
                        for k in range(2):
                            pool.indirect_dma_start(
                                ring[:, 2 * c + k, 0:D], None, xn_rows,
                                bass.IndirectOffsetOnAxis(ap=idx_slot[:, h, 2 * c + k:2 * c + k + 1], axis=0)
                            ).then_inc(s(f"rows_in{c}"), 16)

            pool.wait_ge(s("p1_xn_out"), 16 * GROUPS)
            repeated(pool, QS // HS, body)

        @block.tensor
        def _(pe):
            def mm(o, l, r, first, last_, **kw):
                return pe.matmul(o, l, r, start=first, stop=last_, **kw)

            pe.wait_ge(s("w_in"), 16 * LOADS_EARLY)
            for c in range(2):
                for o in range(2):
                    last = mm(bank[0][:, 2 * c:2 * c + 2], wfunc_s[:, o, c * 128:(c + 1) * 128],
                              attn_c[:, o, :], o == 0, o == 1)
            last.then_inc(s("u_ps"), 1)
            pe.wait_ge(s("e_row"), 1)
            mm(bank[1][0:QS, 0:PAIRS], ones_row[:, 0:QS], tab_t[:, 1, :], True, True).then_inc(s("e_bc"), 1)
            pe.wait_ge(s("tab_done"), 1)
            pe.wait_ge(s("ident_done"), 1)
            pe.wait_ge(s("u_done"), 1)
            pe.wait_ge(s("consts"), CONSTS)
            mm(bank[7][:, 0:258], zeros[:, 0:128], zeros[:, 0:258], True, False, skip_group_check=True)

            def transposes(g):
                pe.wait_ge(s("p1_xn"), g + 1)
                freed(pe, s("p1_xnT"), g)
                for c in range(2):
                    for j in range(2):
                        last = pe.transpose(pt(0)[:, c, j * R:(j + 1) * R], p_xn[:, j, c * 128:(c + 1) * 128],
                                            ident[0:R, 0:R])
                last.then_inc(s("p1_T"), 1)

            def products(g, j):
                pe.wait_ge(s("p1_xnT"), g + 1)
                if j == 0:
                    freed(pe, s("p1_s"), g)
                    for c in range(2):
                        last = mm(bank[1][0:2, 0:GROUP], u_s[:, c, :], p_xnT[:, c, :], c == 0, c == 1)
                    last.then_inc(s("p1_s_ps"), 1)
                freed(pe, s("p1_kv_read"), 2 * g + j - 1)
                for c in range(2):
                    last = mm(bank[2 + j][0:R, :], p_xnT[:, c, j * R:(j + 1) * R], wkv_s[:, c, :], c == 0, c == 1)
                last.then_inc(s("p1_kv"), 1)

            def kv_sum(g, j):
                pe.wait_ge(s("p1_phi"), 2 * g + j + 1)
                for c in range(2):
                    last = mm(bank[7][:, c * 129:(c + 1) * 129], p_phi[:, j, c * 128:(c + 1) * 128],
                              p_v[j][:, c, :], False, False, skip_group_check=True)
                last.then_inc(s("p1_sum"), 1)

            transposes(0)
            products(0, 0)
            products(0, 1)
            def body(i):
                transposes(i + 1)
                kv_sum(i, 0)
                products(i + 1, 0)
                kv_sum(i, 1)
                products(i + 1, 1)

            repeated(pe, GROUPS - 1, body)
            kv_sum(GROUPS - 1, 0)
            kv_sum(GROUPS - 1, 1)
            mm(bank[7][:, 0:258], zeros[:, 0:128], zeros[:, 0:258], False, True,
               skip_group_check=True).then_inc(s("kv_done"), 1)

            pe.wait_ge(s("p1_s"), GROUPS)
            pe.wait_ge(s("p1_kv_read"), 2 * GROUPS)
            for a, what in enumerate((src_f, rel_l, hi_l)):
                pe.wait_ge(s("l_done"), a + 1)
                for j in range(JS):
                    last = pe.transpose(bank[1 + 2 * a + j // CS][0:R, (j % CS) * QS:(j % CS + 1) * QS],
                                        what[:, j * R:(j + 1) * R], ident[0:QS, 0:QS])
                    if j % CS == CS - 1:
                        last.then_inc(s("a_ps"), 1)
            pe.wait_ge(s("s1_in"), 32)
            pe.wait_ge(s("kvbd"), 4)
            pe.transpose(bank[7][:, 0:HIS], s1_rows[:], ident[0:HIS, 0:HIS]).then_inc(s("s1_ps"), 1)
            pe.wait_ge(s("s2_in"), 16 * CS)
            pe.wait_ge(s("p1_xnT"), GROUPS)
            for c in range(CS):
                last = pe.transpose(bank[0][0:R, c * QS:(c + 1) * QS], s2_rows[:, c * R:(c + 1) * R], ident[0:QS, 0:QS])
            last.then_inc(s("s2_ps"), 1)
            pe.wait_ge(s("a_done"), 6)
            pe.wait_ge(s("s1_parts"), PART)
            pe.wait_ge(s("s2_parts"), PART)

            def body(i):
                for h in range(HS):
                    q = i * HS + h
                    pe.wait_ge(s("lr_oh"), q + 1)
                    freed(pe, s("selected"), q - HS + 1)
                    for j in range(JS):
                        for p in range(PART):
                            mm(bank[1 + 2 * h + j // CS][:, (j % CS) * HIS:(j % CS + 1) * HIS],
                               lr_oh[h][:, j * R:j * R + 128], s1_p[:, p, :], p == 0, p == PART - 1)
                    for j in range(JS):
                        last = mm(bank[2 + 2 * h][:, CS * HIS + PART * j:CS * HIS + PART * (j + 1)],
                                  lr_oh[h][0:R, LROW + j * R:LROW + j * R + 128],
                                  s2_p[:, bass.ds(q + j // 2 * QS, 1), :].rearrange("p a k -> p (a k)"), True, True)
                    last.then_inc(s("lr_used"), 1)

            repeated(pe, QS // HS, body)
            pe.wait_ge(s("selected"), QS)


            for j in range(JS):
                last = pe.transpose(bank[j // 4][0:QS, (j % 4) * R:(j % 4 + 1) * R], a_u[:, :, j], ident[0:R, 0:R])
            last.then_inc(s("u_l"), 1)
            pe.wait_ge(s("summary"), 5)
            for k in range(5):
                last = mm(bank[3][0:1, k * QS:(k + 1) * QS], sm[:, k:k + 1], ident[0:QS, 0:QS], True, True)
            last.then_inc(s("sm_row"), 1)
            pe.wait_ge(s("carry"), 1)
            mm(bank[4][0:QS, 0:1], smr[0:1, 5, 0:QS], ones_row[:, 0:1], True, True)
            mm(bank[4][0:QS, 1:2], smr[0:1, 6, 0:QS], ones_row[:, 0:1], True, True).then_inc(s("carry_c"), 1)
            pe.wait_ge(s("p_l"), 1)
            for j in range(JS):
                last = pe.transpose(bank[5 + j // CS][0:R, (j % CS) * QS:(j % CS + 1) * QS], t_l[:, j * R:(j + 1) * R],
                                    ident[0:QS, 0:QS])
            last.then_inc(s("pT_done"), 1)

            pe.wait_ge(s("p_done"), 1)

            def queries(g):
                pe.wait_ge(s("m_xnT"), 16 * (g + 1))
                freed(pe, s("m_qread"), 2 * g)
                freed(pe, s("m_min"), 2 * g)
                for o in range(2):
                    for c in range(2):
                        last = mm(pt(0)[:, o, :], wq_s[:, c, o * 128:(o + 1) * 128], xnT_in[:, c, :], c == 0, c == 1)
                last.then_inc(s("m_q"), 1)

            def attention(g):
                pe.wait_ge(s("m_phi"), g + 1)
                freed(pe, s("m_z"), g)
                freed(pe, s("m_yT"), g)
                for o in range(2):
                    mm(pt(1)[:, o, :], ksbd[:, o, :], m_n[:, o, :], True, True)
                for o in range(2):
                    last = mm(pt(2)[:, o, :], kvbd[:, o, :], m_n[:, o, :], True, True)
                last.then_inc(s("m_nd"), 1)

            def project(g):
                pe.wait_ge(s("m_att"), g + 1)
                for j in range(2):
                    for c in range(2):
                        last = mm(pr_(1)[:, j, :], m_e[:, c, j * R:(j + 1) * R], wo_s[:, c, :], c == 0, c == 1)
                last.then_inc(s("m_o_ps"), 1)

            def turn(g):
                pe.wait_ge(s("m_y"), g + 1)
                freed(pe, s("m_yT"), g)
                for c in range(2):
                    for j in range(2):
                        last = pe.transpose(pt(2)[:, c, j * R:(j + 1) * R], m_y[:, j, c * 128:(c + 1) * 128],
                                            ident[0:R, 0:R])
                last.then_inc(s("m_T"), 1)

            def hidden(g, o2):
                pe.wait_ge(s("m_yT"), g + 1)
                for h in range(2):
                    f = 2 * o2 + h
                    freed(pe, s("m_hread"), g * 8 + f - 1)
                    for c in range(2):
                        last = mm(bank[5 + h][:, 0:GROUP], w1_s[:, c, f * 128:(f + 1) * 128], m_yT[:, c, :],
                                  c == 0, c == 1)
                    last.then_inc(s("m_h"), 1)

            def down(g, j):
                pe.wait_ge(s("m_hread"), g * 8 + 8)
                if j == 0:
                    freed(pe, s("m_z2"), g)
                for f in range(FC):
                    last = mm(pr_(7)[:, j, :], m_h[:, f, j * R:(j + 1) * R], w2_s[:, f, :], f == 0, f == FC - 1)
                last.then_inc(s("m_d"), 1)

            def step(i, z):
                n = i * ZS + z
                pe.wait_ge(s(f"rows_in{z % CS}"), i * (32 * HS) + 32 * (z // CS) + 32)
                pe.wait_ge(s("onehot"), 2 * n + 2)
                freed(pe, s("summed"), n - 1)
                for k in range(2):
                    last = mm(bank[3 + z % 2][0:R, 0:D + 1], onehot[:, 2 * (z % CS) + k, :], ring[:, 2 * (z % CS) + k, :],
                              k == 0, k == 1)
                last.then_inc(s("stepped"), 1)

            def body(i, more=True):
                if more:
                    queries(i + 1)
                for o2 in range(3):
                    hidden(i, o2)
                for z in range(CS):
                    step(i, z)
                if more:
                    attention(i + 1)
                hidden(i, 3)
                down(i, 0)
                for z in range(CS, 2 * CS):
                    step(i, z)
                if more:
                    project(i + 1)
                down(i, 1)
                for z in range(2 * CS, 3 * CS):
                    step(i, z)
                if more:
                    turn(i + 1)

            queries(0)
            attention(0)
            project(0)
            turn(0)
            repeated(pe, GROUPS - 1, body)
            body(GROUPS - 1, False)

            pe.wait_ge(s("wexp_in"), 16 * LOADS_LATE)

            def agg_turn(g):
                pe.wait_ge(s("f_an"), 2 * (g + 1))
                freed(pe, s("f_aT"), g)
                for c in range(2):
                    for j in range(2):
                        last = pe.transpose(pt(0)[:, c, j * R:(j + 1) * R], f_an[:, j, c * 128:(c + 1) * 128],
                                            ident[0:R, 0:R])
                last.then_inc(s("f_T"), 1)

            def gnn(g):
                pe.wait_ge(s("f_xnT"), 16 * (g + 1))
                pe.wait_ge(s("f_aT"), g + 1)
                freed(pe, s("f_start"), 2 * g)
                for j in range(2):
                    for c in range(2):
                        mm(pr_(2)[:, j, :], xnT_in[:, c, j * R:(j + 1) * R], wself_s[:, c, :], c == 0, False)
                    for c in range(2):
                        last = mm(pr_(2)[:, j, :], f_aT[:, c, j * R:(j + 1) * R], wfuncT_s[:, c, :], False, c == 1)
                last.then_inc(s("f_gnn"), 1)

            def norm_turn(g):
                pe.wait_ge(s("f_xn1"), 2 * (g + 1))
                freed(pe, s("f_xT"), g)
                for c in range(2):
                    for j in range(2):
                        last = pe.transpose(pt(1)[:, c, j * R:(j + 1) * R], f_t[:, j, c * 128:(c + 1) * 128],
                                            ident[0:R, 0:R])
                last.then_inc(s("f_T1"), 1)

            def router(g):
                pe.wait_ge(s("f_xT"), g + 1)
                freed(pe, s("f_wTc"), g)
                for c in range(2):
                    last = mm(bank[3][:, 0:GROUP], rw1_s[:, c, :], f_xT[:, c, :], c == 0, c == 1)
                last.then_inc(s("f_rh_ps"), 1)

            def logits(g):
                pe.wait_ge(s("f_rh"), g + 1)
                for j in range(2):
                    last = mm(bank[3][0:R, 256 + 8 * j:256 + 8 * j + EXPERTS], f_rh[:, j * R:(j + 1) * R], rw2_s[:],
                              True, True)
                last.then_inc(s("f_lg_ps"), 1)

            def weights_turn(g):
                pe.wait_ge(s("f_wt"), g + 1)
                for j in range(2):
                    last = mm(bank[3][0:EXPERTS, j * R:(j + 1) * R], wt[:, j, :], ident[0:R, 0:R], True, True)
                last.then_inc(s("f_wT_ps"), 1)

            def biases(g):
                pe.wait_ge(s("f_wTc"), g + 1)
                pe.wait_ge(s("f_r"), g + 1)
                for j in range(2):
                    last = mm(pr_(2)[:, j, :], f_wT[:, j * R:(j + 1) * R], eb3_s[:], True, True)
                last.then_inc(s("f_bias"), 1)

            def layer1(g, e):
                pe.wait_ge(s("f_xT"), g + 1)
                freed(pe, s("f_h1"), g * 6 + e)
                for o in range(2):
                    for c in range(2):
                        last = mm(pt(4)[:, o, :], wexpv[:, 0, e, c, o * 128:(o + 1) * 128], f_xT[:, c, :], c == 0, c == 1)
                last.then_inc(s("f_h1_ps"), 1)

            def layer2(g, e):
                pe.wait_ge(s("f_h1"), g * 6 + e + 1)
                freed(pe, s("f_h2"), g * 6 + e)
                for o in range(2):
                    for c in range(2):
                        last = mm(pt(5)[:, o, :], wexpv[:, 1, e, c, o * 128:(o + 1) * 128], f_h1[e % 2][:, c, :],
                                  c == 0, c == 1)
                last.then_inc(s("f_h2_ps"), 1)

            def layer3(g, e):
                pe.wait_ge(s("f_h2"), g * 6 + e + 1)
                if e % 2 == 0:
                    freed(pe, s("f_x2"), g * 6 + (e - 1) if e else g * 6)
                else:
                    freed(pe, s("f_x2"), g * 6 + (e - 1))
                for j in range(2):
                    for c in range(2):
                        last = mm(pr_(6 + e % 2)[:, j, :], f_h2[e % 2][:, c, j * R:(j + 1) * R], wexpv[:, 2, e, c, :],
                                  c == 0, c == 1)
                last.then_inc(s("f_o"), 1)

            def experts(g, between):
                router(g)
                layer1(g, 0)
                logits(g)
                layer1(g, 1)
                layer2(g, 0)
                layer1(g, 2)
                layer2(g, 1)
                weights_turn(g)
                between(agg_turn)
                layer1(g, 3)
                biases(g)
                layer3(g, 0)
                layer2(g, 2)
                layer3(g, 1)
                layer1(g, 4)
                layer2(g, 3)
                between(gnn)
                layer3(g, 2)
                layer1(g, 5)
                layer2(g, 4)
                layer3(g, 3)
                layer2(g, 5)
                between(norm_turn)
                layer3(g, 4)
                layer3(g, 5)

            pe.wait_ge(s("summed"), STEPS)
            agg_turn(0)
            gnn(0)
            norm_turn(0)
            def body(i):
                experts(i, lambda f: f(i + 1))

            repeated(pe, GROUPS - 1, body)
            experts(GROUPS - 1, lambda f: None)

        @block.scalar
        def _(act):
            def ln_rstd(g, var_ready, ln_done, rstd_done, v, l, r):
                act.wait_ge(s(var_ready), g + 1)
                act.activation(l[:], v[:, :, 1], ACT.Ln).then_inc(s(ln_done), 1)
                act.wait_ge(s(ln_done), g + 1)
                act.activation(r[:], l[:], ACT.Exp, scale=-0.5).then_inc(s(rstd_done), 1)

            act.preload_act_table_set("natural_log_exp_and_others")
            act.wait_ge(s("w_in"), 16 * LOADS_EARLY)

            def p1_a(g):
                ln_rstd(g, "var", "ln", "rstd", mv, lnv, rstd)

            def p1_b(g):
                act.wait_ge(s("p1_T"), g + 1)
                freed(act, s("p1_kv"), 2 * g)
                freed(act, s("p1_xnT_out"), g * 16)
                act.activation(p_xnT, pt(0), ACT.Copy).then_inc(s("p1_xnT"), 1)

            def p1_c(g):
                act.wait_ge(s("p1_s_ps"), g + 1)
                freed(act, s("p1_s_out"), g * 32)
                act.activation(p_s, bank[1][0:2, 0:GROUP], ACT.Copy).then_inc(s("p1_s"), 1)

            def p1_d(g):
                for j in range(2):
                    act.wait_ge(s("p1_min"), 2 * g + j + 1)
                    act.activation(p_exp[:, j], p_min[:, j], ACT.Exp).then_inc(s("p1_exp"), 1)

            p1_a(0)
            p1_b(0)
            p1_c(0)
            def body(i):
                p1_a(i + 1)
                p1_b(i + 1)
                p1_d(i)
                p1_c(i + 1)

            repeated(act, GROUPS - 1, body)
            p1_d(GROUPS - 1)

            act.wait_ge(s("p_arg"), 1)
            act.activation(t_l, e_l, ACT.Exp).then_inc(s("p_exp"), 1)

            def m_queries(g):
                act.wait_ge(s("m_min"), 2 * (g + 1))
                freed(act, s("m_o_ps"), g)
                act.activation(m_e, m_q, ACT.Exp).then_inc(s("m_exp"), 1)
                freed(act, s("m_phi"), g)
                for o in range(2):
                    act.activation(m_r[:, o], pt(0)[:, o], ACT.Relu, bias=bq_c[:, o:o + 1]).then_inc(s("m_qread"), 1)

            def m_norm(g):
                ln_rstd(GROUPS + g, "var", "ln", "rstd", mv, lnv, rstd)

            def m_turn(g):
                act.wait_ge(s("m_T"), g + 1)
                freed(act, s("m_h"), g * 8)
                act.activation(m_yT, pt(2), ACT.Copy).then_inc(s("m_yT"), 1)

            def m_hidden(g, o2):
                for h in range(2):
                    f = 2 * o2 + h
                    act.wait_ge(s("m_h"), g * 8 + f + 1)
                    freed(act, s("m_d"), 2 * g)
                    act.activation(m_h[:, f], bank[5 + h][:, 0:GROUP], ACT.Relu,
                                   bias=b1_c[:, f:f + 1]).then_inc(s("m_hread"), 1)

            def m_norm2(g):
                ln_rstd(g, "m_var2", "m_ln2", "m_rstd2", mv2, lnv2, rstd2)

            def body(i, more=True):
                if not (isinstance(i, int) and i == 0):
                    m_norm2(i - 1)
                m_hidden(i, 0)
                m_hidden(i, 1)
                if more:
                    m_queries(i + 1)
                for o2 in range(2, 4):
                    m_hidden(i, o2)
                if more:
                    m_norm(i + 1)
                    m_turn(i + 1)

            m_queries(0)
            m_norm(0)
            m_turn(0)
            repeated(act, GROUPS - 1, body)
            body(GROUPS - 1, False)
            m_norm2(GROUPS - 1)

            def f_first(g):
                act.wait_ge(s("f_T"), g + 1)
                freed(act, s("f_gnn"), g)
                act.activation(f_aT, pt(0), ACT.Copy).then_inc(s("f_aT"), 1)

            def f_norm(g):
                ln_rstd(2 * GROUPS + g, "var", "ln", "rstd", mv, lnv, rstd)

            def f_second(g):
                act.wait_ge(s("f_T1"), g + 1)
                freed(act, s("f_h1_ps"), 6 * g)
                freed(act, s("f_rh_ps"), g)
                act.activation(f_xT, pt(1), ACT.Copy).then_inc(s("f_xT"), 1)

            def f_router(g):
                act.wait_ge(s("f_rh_ps"), g + 1)
                act.activation(f_rh, bank[3][:, 0:GROUP], ACT.Relu, bias=rb1_c[:]).then_inc(s("f_rh"), 1)

            def f_soft(g):
                act.wait_ge(s("f_nmx"), g + 1)
                for j in range(2):
                    act.activation(pr[:, j, 0:EXPERTS], lg[:, j, 0:EXPERTS], ACT.Exp, bias=rt[:, 0, j:j + 1],
                                   accum_out=rt[:, 1, j:j + 1]).then_inc(s("f_sum"), 1)

            def f_soft2(g):
                act.wait_ge(s("f_dif"), g + 1)
                act.activation(rt[:, 4, :], rt[:, 3, :], ACT.Exp).then_inc(s("f_e2"), 1)

            def f_wT_copy(g):
                act.wait_ge(s("f_wT_ps"), g + 1)
                freed(act, s("f_bias"), g)
                act.activation(f_wT, bank[3][0:EXPERTS, 0:GROUP], ACT.Copy).then_inc(s("f_wTc"), 1)

            def relu1(g, e):
                act.wait_ge(s("f_h1_ps"), g * 6 + e + 1)
                freed(act, s("f_h2_ps"), g * 6 + e - 1 if e else g * 6)
                for o in range(2):
                    ins = act.activation(f_h1[e % 2][:, o], pt(4)[:, o], ACT.Relu, bias=eb_c[:, 0, e, o:o + 1])
                ins.then_inc(s("f_h1"), 1)

            def relu2(g, e):
                act.wait_ge(s("f_h2_ps"), g * 6 + e + 1)
                freed(act, s("f_o"), g * 6 + e - 1 if e else g * 6)
                for o in range(2):
                    ins = act.activation(f_h2[e % 2][:, o], pt(5)[:, o], ACT.Relu, bias=eb_c[:, 1, e, o:o + 1])
                ins.then_inc(s("f_h2"), 1)

            def f_experts(g, between):
                f_router(g)
                relu1(g, 0)
                f_soft(g)
                relu1(g, 1)
                f_soft2(g)
                relu2(g, 0)
                relu1(g, 2)
                relu2(g, 1)
                f_wT_copy(g)
                between(f_first)
                relu1(g, 3)
                relu2(g, 2)
                relu1(g, 4)
                relu2(g, 3)
                relu1(g, 5)
                relu2(g, 4)
                between(f_norm)
                relu2(g, 5)
                between(f_second)

            f_first(0)
            f_norm(0)
            f_second(0)
            def body(i):
                f_experts(i, lambda f: f(i + 1))

            repeated(act, GROUPS - 1, body)
            f_experts(GROUPS - 1, lambda f: None)

        @block.vector
        def _(v):
            t = Own(v, s("tab_own"), 0, 0)
            v.wait_ge(s("dlast_in"), 16)
            v.wait_ge(s("iota_tabs"), 3)
            t.did(v.tensor_scalar(tab_t[:, 0, :], dlast[:], -float((R - 1) // 2), 1.0 / R, ALU.add, ALU.mult))
            t.settle()
            t.did(v.tensor_scalar(tab_t[:, 1, :], tab_t[:, 0, :], ROUND, -ROUND, ALU.add, ALU.add))
            t.settle()
            v.tensor_tensor(tab_t[:, 1, :], tab_t[:, 1, :], iota_t[:], ALU.add).then_inc(s("e_row"), 1)
            v.wait_ge(s("e_bc"), 1)
            for c in range(CS):
                t.did(v.tensor_scalar(junk[0:QS, 0:PAIRS], bank[1][0:QS, 0:PAIRS], iota_s[:, c:c + 1], 0.0,
                                      ALU.is_lt, ALU.add, accum_out=tabs[:, 0, c:c + 1]))
                t.settle()
            t.did(v.tensor_scalar(tabs[:, 1, :], tabs[:, 0, :], float(PAIRS - 1), None, ALU.min))
            t.settle()
            t.did(v.tensor_tensor(tabs[:, 2, :], iota_s[:], tabs[:, 1, :], ALU.subtract))
            t.did(v.tensor_copy(tab_i[:, 0, :], tabs[:, 1, :]))
            t.settle()
            t.did(v.tensor_scalar(tabs[:, 3, :], tabs[:, 2, :], float(BLOCKS - 1), None, ALU.min))
            t.did(v.tensor_scalar(tabs[:, 4, :], tabs[:, 2, :], float(R), None, ALU.mult))
            t.settle()
            v.tensor_copy(tab_i[:, 1, :], tabs[:, 3, :]).then_inc(s("tab_done"), 1)
            v.wait_ge(s("u_ps"), 1)
            v.tensor_copy(u_s[:].rearrange("p c k -> p (c k)"), bank[0][:, 0:4]).then_inc(s("u_done"), 1)
            v.memset(p_v[0][:, :, 128:129], 1.0).then_inc(s("v_ones"), 1)
            v.memset(p_v[1][:, :, 128:129], 1.0).then_inc(s("v_ones"), 1)
            v.wait_ge(s("w_in"), 16 * LOADS_EARLY)

            def statistics(own, z, st_, mv_):
                for j in range(2):
                    own.did(v.bn_stats(st_[:, j, :], z[:, j, :]))
                own.settle()
                apart(v, "past")
                for j in range(2):
                    own.did(v.bn_aggr(mv_[:, j, :], st_[:, j, :]))
                own.settle()
                return v.tensor_scalar(mv_[:, :, 1], mv_[:, :, 1], EPS, None, ALU.add)

            def p1_norm(g):
                own = Own(v, s("p1a_own"), 4, g)
                v.wait_ge(s("p1_x"), 16 * (g + 1))
                statistics(own, p_x, st, mv).then_inc(s("var"), 1)
                v.wait_ge(s("rstd"), g + 1)
                freed(v, s("p1_T"), g)
                freed(v, s("p1_xn_out"), 16 * g)
                for j in range(2):
                    ins = v.tensor_scalar(p_xn[:, j], p_x[:, j], mv[:, j, 0:1], rstd[:, j:j + 1], ALU.subtract, ALU.mult)
                ins.then_inc(s("p1_xn"), 1)
                own.end()

            def p1_kv(g):
                own = Own(v, s("p1b_own"), 2, g)
                for j in range(2):
                    v.wait_ge(s("p1_kv"), 2 * g + j + 1)
                    own.did(v.tensor_tensor(p_k[:, j], bank[2 + j][0:R, 0:D], bkv_bc[:, 0:D], ALU.add))
                    freed(v, s("p1_sum"), 2 * g)
                    v.tensor_tensor(p_v[j][:, :, 0:128],
                                    bank[2 + j][0:R, D:2 * D].rearrange("p (c n) -> p c n", c=2),
                                    bkv_bc[:, D:2 * D].rearrange("p (c n) -> p c n", c=2),
                                    ALU.add).then_inc(s("p1_kv_read"), 1)
                    own.settle()
                    v.tensor_scalar(p_min[:, j], p_k[:, j], 0.0, None, ALU.min).then_inc(s("p1_min"), 1)
                for j in range(2):
                    v.wait_ge(s("p1_exp"), 2 * g + j + 1)
                    v.scalar_tensor_tensor(p_phi[:, j], p_k[:, j], 0.0, p_exp[:, j], ALU.max,
                                           ALU.add).then_inc(s("p1_phi"), 1)
                own.end()

            p1_norm(0)
            def p1_edges(g):
                for h in range(2):
                    v.wait_ge(s(f"attr_mul{h}"), g + 1)
                    v.tensor_reduce(ew_n[:, bass.ds((g * 2 + h) * CHUNK, CHUNK)], attr_s[:, h, :, 0:ED // (2 - h)], AX.X,
                                    ALU.add).then_inc(s(f"attr_used{h}"), 1)

            def body(i):
                p1_norm(i + 1)
                p1_kv(i)
                p1_edges(i)

            repeated(v, GROUPS - 1, body)
            p1_kv(GROUPS - 1)
            p1_edges(GROUPS - 1)
            v.wait_ge(s("kv_done"), 1)
            v.wait_ge(s("consts"), CONSTS)
            for c in range(2):
                v.tensor_tensor(kvbd[:, c, :], bank[7][:, c * 129:c * 129 + 128], bmask[:], ALU.mult).then_inc(s("kvbd"), 1)
                v.tensor_scalar(ksbd[:, c, :], bmask[:], bank[7][:, c * 129 + 128:c * 129 + 129], None,
                                ALU.mult).then_inc(s("kvbd"), 1)

            v.wait_ge(s("sd_in"), 16 * 2 * CS)
            v.tensor_copy(src_f, src_i).then_inc(s("l_done"), 1)
            t.did(v.tensor_copy(dst_f, dst_i))
            t.settle()
            for c in range(CS):
                e_ = slice(c * 2 * R, (c + 1) * 2 * R)
                ins = v.tensor_scalar(rel_l[:, e_], dst_f[:, e_], tabs[:, 4, c:c + 1], None, ALU.subtract)
                if c < CS - 1:
                    t.did(ins)
            ins.then_inc(s("l_done"), 1)
            v.wait_ge(s("l_done"), 2)
            t.settle()
            t.did(v.tensor_scalar(hi_l, src_f, -(LO - 1) / 2, 1.0 / LO, ALU.add, ALU.mult))
            t.settle()
            v.tensor_scalar(hi_l, hi_l, ROUND, -ROUND, ALU.add, ALU.add).then_inc(s("l_done"), 1)
            v.wait_ge(s("l_done"), 3)
            v.wait_ge(s("ew_out"), 16)
            v.scalar_tensor_tensor(lr_l[:, 0, :], hi_l, -float(LO), src_f, ALU.mult, ALU.add).then_inc(s("lr_done"), 1)
            v.tensor_copy(lr_l[:, 1, :], rel_l).then_inc(s("lr_done"), 1)
            for a in range(6):
                v.wait_ge(s("a_ps"), a + 1)
                to = (a_src, a_rel, a_hi)[a // 2]
                j0 = CS * (a % 2)
                v.tensor_copy(to[:, :, j0:j0 + CS].rearrange("p q j -> p j q"),
                              bank[1 + a][0:R, 0:CS * QS].rearrange("p (j q) -> p j q", q=QS)).then_inc(s("a_done"), 1)

            def parts(whole, part, sem):
                for k in range(PART):
                    v.tensor_copy(part(k), whole(0)).then_inc(s(sem), 1)
                    if k < PART - 1:
                        v.wait_ge(s(sem), k + 1)
                        t.did(v.tensor_copy(whole(1), part(k)))
                        t.settle()
                        t.did(v.tensor_tensor(whole(0), whole(0), whole(1), ALU.subtract))
                        t.settle()

            v.wait_ge(s("s1_ps"), 1)
            t.did(v.tensor_copy(s1_t[:, 0, :], bank[7][:, 0:HIS]))
            t.settle()
            parts(lambda k: s1_t[:, k, :], lambda k: s1_p[:, k, :], "s1_parts")
            v.wait_ge(s("s2_ps"), 1)
            t.did(v.tensor_copy(s2_t[:, 0, :], bank[0][0:R, 0:CS * QS]))
            t.settle()
            parts(lambda k: s2_t[:, k, :], lambda k: s2_p[:, :, k], "s2_parts")

            def select(i, h):
                own = Own(v, s("sel_own"), 4 * HS, i)
                own.k = 4 * h
                n = i * HS + h
                v.wait_ge(s("lr_used"), n + 1)
                v.wait_ge(s("away"), n + 1)
                freed(v, s("selected"), n)
                for a in range(2):
                    own.did(v.scalar_tensor_tensor(
                        sel[:, a * CS:(a + 1) * CS, :],
                        away[:, h, a * CS * HIS:(a + 1) * CS * HIS].rearrange("p (j n) -> p j n", n=HIS), 0.0,
                        bank[1 + 2 * h + a][0:R, 0:CS * HIS].rearrange("p (j n) -> p j n", n=HIS),
                        ALU.is_equal, ALU.mult))
                own.did(v.tensor_reduce(a_s[:, 1, :], bank[2 + 2 * h][0:R, CS * HIS:CS * HIS + PART * JS]
                                        .rearrange("p (j k) -> p j k", k=PART), AX.X, ALU.add))
                own.settle()
                own.did(v.tensor_reduce(a_s[:, 0, :], sel, AX.X, ALU.add))
                own.settle()
                v.tensor_tensor(a_u[:, bass.ds(n, 1), :].rearrange("p a j -> p (a j)"), a_s[:, 0, :], a_s[:, 1, :],
                                ALU.add).then_inc(s("selected"), 1)

            def one_hots(i, h):
                n = i * HS + h
                v.wait_ge(s(f"lr_in{h}"), i * 16 + 16)
                freed(v, s("lr_used"), n - HS + 1)
                v.tensor_scalar(lr_oh[h][:, 0:2 * LROW], lr_bc[h], iota_p[:], None, ALU.is_equal).then_inc(s("lr_oh"), 1)

            def body(i, more=True):
                one_hots(i, 2)
                select(i, 0)
                if more:
                    one_hots(i + 1, 0)
                select(i, 1)
                if more:
                    one_hots(i + 1, 1)
                select(i, 2)

            for h in range(HS):
                t.did(v.memset(lr_oh[h][:, 2 * LROW:], 0.0))
            t.settle()
            one_hots(0, 0)
            one_hots(0, 1)
            repeated(v, QS // HS - 1, body)
            body(QS // HS - 1, False)
            v.wait_ge(s("selected"), QS)

            def blocks_of(q):
                _, values = nc.values_load_multi_w_load_instructions(
                    blk_row[:, bass.ds(q * CS, CS)], engines=[mybir.EngineType.DVE], min_val=0, max_val=BLOCKS - 1,
                    skip_runtime_bounds_check_because="tab_i is clamped to BLOCKS - 1 and counts up from 0")
                return values

            def affine(own, z, mv_, rstd_, gain, bias, o, last_sem):
                for j in range(2):
                    own.did(v.tensor_scalar(z[:, j], z[:, j], mv_[:, j, 0:1], rstd_[:, j:j + 1], ALU.subtract, ALU.mult))
                own.settle()
                own.did(v.tensor_tensor(z, z, rv[:, gain:gain + 1, :].to_broadcast([R, 2, D]), ALU.mult))
                own.settle()
                v.tensor_tensor(o, z, rv[:, bias:bias + 1, :].to_broadcast([R, 2, D]), ALU.add).then_inc(s(last_sem), 1)

            def m_queries(g):
                v.wait_ge(s("m_q"), g + 1)
                freed(v, s("m_exp"), g)
                for o in range(2):
                    v.tensor_scalar(m_q[:, o], pt(0)[:, o], bq_c[:, o:o + 1], 0.0, ALU.add,
                                    ALU.min).then_inc(s("m_min"), 1)
                v.wait_ge(s("m_exp"), g + 1)
                v.wait_ge(s("m_qread"), 2 * g + 2)
                freed(v, s("m_nd"), g)
                v.tensor_tensor(m_n, m_e, m_r, ALU.add).then_inc(s("m_phi"), 1)

            def m_attention(g):
                own = Own(v, s("ma_own"), 2, g)
                v.wait_ge(s("m_nd"), g + 1)
                own.did(v.tensor_scalar(m_q, pt(1), 1e-6, None, ALU.add))
                own.settle()
                own.did(v.reciprocal(m_q, m_q))
                own.settle()
                freed(v, s("m_o_ps"), g)
                v.tensor_tensor(m_e, pt(2), m_q, ALU.mult).then_inc(s("m_att"), 1)
                own.end()

            def m_project(g):
                own = Own(v, s("mb_own"), 7, g)
                v.wait_ge(s("m_xn"), 16 * (g + 1))
                freed(v, s("m_T"), g)
                v.tensor_tensor(m_z, xn_in, rv[:, 0:1, :].to_broadcast([R, 2, D]), ALU.add).then_inc(s("m_xb"), 1)
                v.wait_ge(s("m_xb"), g + 1)
                v.wait_ge(s("m_o_ps"), g + 1)
                v.tensor_tensor(m_z, pr_(1), m_z, ALU.add).then_inc(s("m_z"), 1)
                v.wait_ge(s("m_z"), g + 1)
                statistics(own, m_z, st, mv).then_inc(s("var"), 1)
                v.wait_ge(s("rstd"), GROUPS + g + 1)
                affine(own, m_z, mv, rstd, 1, 2, m_y, "m_y")
                own.end()

            def m_keep(g):
                v.wait_ge(s("m_y"), g + 1)
                v.tensor_tensor(m_yb, m_y, rv[:, 3:4, :].to_broadcast([R, 2, D]), ALU.add).then_inc(s("m_yb"), 1)

            def m_last(g):
                own = Own(v, s("mc_own"), 7, g)
                v.wait_ge(s("m_d"), 2 * (g + 1))
                v.wait_ge(s("m_yb"), g + 1)
                v.tensor_tensor(m_z2, pr_(7), m_yb, ALU.add).then_inc(s("m_z2"), 1)
                v.wait_ge(s("m_z2"), g + 1)
                statistics(own, m_z2, st2, mv2).then_inc(s("m_var2"), 1)
                v.wait_ge(s("m_rstd2"), g + 1)
                v.wait_ge(s("m_stored"), 16 * (g + 1))
                affine(own, m_z2, mv2, rstd2, 4, 5, m_o, "m_out")
                own.end()

            x_ = t
            x_.did(v.tensor_scalar(t_l, rel_l, 0.0, None, ALU.is_ge))
            x_.settle()
            x_.did(v.scalar_tensor_tensor(valid, rel_l, float(R), t_l, ALU.is_lt, ALU.mult))
            x_.did(v.memset(reset[:, 0:1], 0.0))
            x_.did(v.memset(reset[:, LROW:LROW + 1], 0.0))
            x_.did(v.tensor_tensor(reset[:, 1:LROW], dst_f[:, 1:LROW], dst_f[:, 0:LROW - 1], ALU.not_equal))
            x_.settle()
            x_.did(v.tensor_scalar(reset[:, 1:LROW], reset[:, 1:LROW], -BIG, None, ALU.mult))
            v.wait_ge(s("u_l"), 1)
            v.wait_ge(s("ew_in"), 16 * CS)
            for k in range(3):
                a, b = 4 * R * k, min(4 * R * (k + 1), LROW)
                x_.did(v.tensor_tensor(t_l[:, a:b], bank[k][0:QS, 0:b - a], ew_l[:, a:b], ALU.add))
            x_.settle()
            x_.did(v.scalar_tensor_tensor(e_l, t_l, 0.01, t_l, ALU.mult, ALU.max))
            x_.settle()
            x_.did(v.tensor_tensor(e_l, e_l, valid, ALU.mult))
            x_.did(v.tensor_scalar(t_l, valid, BIG, -BIG, ALU.mult, ALU.add))
            x_.settle()
            x_.did(v.tensor_tensor(e_l, e_l, t_l, ALU.add))
            x_.settle()

            def scans(first, last_):
                x_.did(v.tensor_tensor_scan(f_l, reset[:, 0:LROW], e_l, first, ALU.add, ALU.max))
                x_.settle()
                x_.did(v.tensor_tensor_scan(b_l[:, ::-1], reset[:, LROW:0:-1], f_l[:, ::-1], last_, ALU.add, ALU.max))
                x_.settle()

            scans(-BIG, -BIG)
            v.tensor_copy(sm[:, 0:1], f_l[:, LROW - 1:LROW]).then_inc(s("summary"), 1)
            v.tensor_copy(sm[:, 1:2], b_l[:, 0:1]).then_inc(s("summary"), 1)
            v.tensor_tensor(sm[:, 2:3], dst_f[:, 0:1], dst_f[:, LROW - 1:LROW], ALU.is_equal).then_inc(s("summary"), 1)
            v.tensor_copy(sm[:, 3:4], dst_f[:, 0:1]).then_inc(s("summary"), 1)
            v.tensor_copy(sm[:, 4:5], dst_f[:, LROW - 1:LROW]).then_inc(s("summary"), 1)
            v.wait_ge(s("sm_row"), 1)
            x_.did(v.tensor_copy(smr[:, 0:5, 0:QS], bank[3][0:1, 0:5 * QS].rearrange("p (k q) -> p k q", q=QS)))
            x_.did(v.memset(smr[:, 5:7, 0:QS], -BIG))
            x_.settle()
            row = lambda k, a, b: smr[:, k, a:b]
            x_.did(v.tensor_tensor(row(7, 1, QS), row(3, 1, QS), row(4, 0, QS - 1), ALU.is_equal))
            x_.settle()
            x_.did(v.tensor_scalar(row(8, 1, QS), row(7, 1, QS), BIG, -BIG, ALU.mult, ALU.add))
            x_.did(v.tensor_tensor(row(9, 1, QS), row(7, 1, QS), row(2, 0, QS - 1), ALU.mult))
            x_.did(v.tensor_tensor(row(10, 1, QS), row(7, 1, QS), row(2, 1, QS), ALU.mult))
            x_.settle()
            x_.did(v.tensor_scalar(row(9, 1, QS), row(9, 1, QS), BIG, -BIG, ALU.mult, ALU.add))
            x_.did(v.tensor_scalar(row(10, 1, QS), row(10, 1, QS), BIG, -BIG, ALU.mult, ALU.add))
            x_.did(v.tensor_tensor(row(0, 0, QS - 1), row(0, 0, QS - 1), row(8, 1, QS), ALU.add))
            x_.did(v.tensor_tensor(row(1, 1, QS), row(1, 1, QS), row(8, 1, QS), ALU.add))
            x_.settle()
            x_.did(v.tensor_tensor_scan(row(5, 1, QS), row(9, 1, QS), row(0, 0, QS - 1), -BIG, ALU.add, ALU.max))
            v.tensor_tensor_scan(smr[:, 6, QS - 2::-1], smr[:, 10, QS - 1:0:-1], smr[:, 1, QS - 1:0:-1], -BIG,
                                 ALU.add, ALU.max).then_inc(s("carry"), 1)
            v.wait_ge(s("carry_c"), 1)
            x_.did(v.tensor_copy(sm[:, 5:7], bank[4][0:QS, 0:2]))
            x_.settle()
            scans(sm[:, 5:6], sm[:, 6:7])
            v.tensor_tensor(e_l, e_l, b_l, ALU.subtract).then_inc(s("p_arg"), 1)
            v.wait_ge(s("p_exp"), 1)
            v.tensor_tensor(t_l, t_l, valid, ALU.mult).then_inc(s("p_l"), 1)
            v.wait_ge(s("pT_done"), 1)
            for a in range(2):
                x_.did(v.tensor_copy(a_p[:, :, CS * a:CS * a + CS].rearrange("p q j -> p j q"),
                                     bank[5 + a][0:R, 0:CS * QS].rearrange("p (j q) -> p j q", q=QS)))
            x_.did(v.memset(acc[:], 0.0))
            v.memset(mark[:], 0.0).then_inc(s("p_done"), 1)
            x_.settle()

            def one_hot(i, z):
                q = i * HS + z // CS
                for k in range(2):
                    at = lambda a: a[:, bass.ds(q, 1), 2 * (z % CS) + k:2 * (z % CS) + k + 1].rearrange("p a b -> p (a b)")
                    v.tensor_scalar(onehot[:, 2 * (z % CS) + k, :], iota_r[:], at(a_rel), at(a_p), ALU.is_equal,
                                    ALU.mult).then_inc(s("onehot"), 1)

            def steps(i, h):
                at = blocks_of(i * HS + h)
                for c in range(CS):
                    z = h * CS + c
                    n = i * ZS + z
                    v.wait_ge(s("stepped"), n + 1)
                    freed(v, s("summed"), n)
                    to = accv[:, bass.ds(at[c], 1), :].rearrange("p b n -> p (b n)")
                    v.tensor_tensor(to, bank[3 + z % 2][0:R, 0:D + 1], to, ALU.add).then_inc(s("summed"), 1)
                    if h + 1 < HS:
                        one_hot(i, z + CS)
                    elif not (isinstance(i, int) and i == GROUPS - 1):
                        one_hot(i + 1, c)

            def body(i, more=True):
                if not (isinstance(i, int) and i == 0):
                    m_last(i - 1)
                m_keep(i)
                if more:
                    m_queries(i + 1)
                steps(i, 0)
                if more:
                    m_attention(i + 1)
                steps(i, 1)
                if more:
                    m_project(i + 1)
                steps(i, 2)

            v.wait_ge(s("p_done"), 1)
            v.memset(mark[:], 0.0).then_inc(s("m_stored"), 16)
            v.wait_ge(s("blk_in"), 16)
            for z in range(CS):
                one_hot(0, z)
            m_queries(0)
            m_attention(0)
            m_project(0)
            repeated(v, GROUPS - 1, body)
            body(GROUPS - 1, False)
            m_last(GROUPS - 1)
            v.wait_ge(s("summed"), STEPS)

            v.memset(lg[:], -BIG).then_inc(s("pads"), 1)
            v.memset(pr[:], -1.0).then_inc(s("pads"), 1)
            v.wait_ge(s("pads"), 2)

            def f_mean(g):
                own = Own(v, s("fa_own"), 4, g)
                den = acc[:].rearrange("p (g j n) -> p g j n", j=2, n=D + 1)[:, bass.ds(g, 1), :, D]
                den = den.rearrange("p g j -> p (g j)")
                freed(v, s("f_x1"), g)
                own.did(v.tensor_scalar(dn[:, 0, :], den, 0.5, None, ALU.max))
                own.did(v.tensor_scalar(dn[:, 1, :], den, 0.0, None, ALU.is_gt))
                own.settle()
                own.did(v.reciprocal(dn[:, 0, :], dn[:, 0, :]))
                own.did(v.tensor_scalar(dn[:, 2, :], dn[:, 1, :], -1.0, 1.0, ALU.mult, ALU.add))
                own.settle()
                freed(v, s("f_T"), g)
                for j in range(2):
                    a = acc[:].rearrange("p (g j n) -> p g j n", j=2, n=D + 1)[:, bass.ds(g, 1), j, 0:D]
                    v.tensor_scalar(f_an[:, j], a.rearrange("p g n -> p (g n)"), dn[:, 0, j:j + 1], None,
                                    ALU.mult).then_inc(s("f_an"), 1)
                own.end()

            def f_rows(g):
                own = Own(v, s("fb_own"), 9, g)
                v.wait_ge(s("f_rows"), 48 * (g + 1))
                freed(v, s("f_T1"), g)
                for j in range(2):
                    own.did(v.tensor_scalar(f_t[:, j], xn_in[:, j], dn[:, 2, j:j + 1], None, ALU.mult))
                own.settle()
                v.wait_ge(s("f_gnn"), g + 1)
                own.did(v.scalar_tensor_tensor(f_t[:, 0], pr_(2)[:, 0], dn[:, 1, 0:1], f_t[:, 0], ALU.mult, ALU.add))
                v.scalar_tensor_tensor(f_t[:, 1], pr_(2)[:, 1], dn[:, 1, 1:2], f_t[:, 1], ALU.mult,
                                       ALU.add).then_inc(s("f_r"), 1)
                v.wait_ge(s("f_r"), g + 1)
                own.settle()
                own.did(v.scalar_tensor_tensor(f_t, f_t, 0.0, xn_in, ALU.max, ALU.add))
                own.settle()
                own.did(v.tensor_tensor(f_t, f_t, f_x, ALU.add))
                own.settle()
                freed(v, s("f_start"), 2 * g)
                v.tensor_tensor(f_x1, f_t, f_mix, ALU.add).then_inc(s("f_x1"), 1)
                v.wait_ge(s("f_x1"), g + 1)
                statistics(own, f_x1, st, mv).then_inc(s("var"), 1)
                v.wait_ge(s("rstd"), 2 * GROUPS + g + 1)
                for j in range(2):
                    v.tensor_scalar(f_t[:, j], f_x1[:, j], mv[:, j, 0:1], rstd[:, j:j + 1], ALU.subtract,
                                    ALU.mult).then_inc(s("f_xn1"), 1)
                own.end()

            def f_route1(g):
                own = Own(v, s("fc_own"), 2, g)
                v.wait_ge(s("f_lg_ps"), g + 1)
                own.did(v.tensor_tensor(lg[:, :, 0:EXPERTS],
                                        bank[3][0:R, 256:272].rearrange("p (j n) -> p j n", j=2)[:, :, 0:EXPERTS],
                                        rb2_bc[:, None, :].to_broadcast([R, 2, EXPERTS]), ALU.add))
                own.settle()
                own.did(v.tensor_reduce(rt[:, 2, :], lg[:], AX.X, ALU.max))
                own.settle()
                v.tensor_scalar(rt[:, 0, :], rt[:, 2, :], -1.0, None, ALU.mult).then_inc(s("f_nmx"), 1)
                own.end()

            def f_route2(g):
                own = Own(v, s("fd_own"), 8, g)
                v.wait_ge(s("f_sum"), 2 * (g + 1))
                own.did(v.reciprocal(rt[:, 2, :], rt[:, 1, :]))
                own.settle()
                for j in range(2):
                    own.did(v.tensor_scalar(pr[:, j, 0:EXPERTS], pr[:, j, 0:EXPERTS], rt[:, 2, j:j + 1], None, ALU.mult))
                own.settle()
                apart(v, "past")
                for j in range(2):
                    own.did(v.max(top[:, j, :], pr[:, j, :]))
                own.settle()
                apart(v, "past")
                for j in range(2):
                    own.did(v.max_index(topi[:, j, :], top[:, j, :], pr[:, j, :]))
                v.tensor_tensor(rt[:, 3, :], top[:, :, 1], top[:, :, 0], ALU.subtract).then_inc(s("f_dif"), 1)
                own.settle()
                own.did(v.tensor_copy(topf[:], topi[:, :, 0:2]))
                own.end()

            def f_route3(g):
                own = Own(v, s("fe_own"), 7, g)
                v.wait_ge(s("f_e2"), g + 1)
                own.did(v.tensor_scalar(rt[:, 5, :], rt[:, 4, :], 1.0, None, ALU.add))
                own.settle()
                own.did(v.reciprocal(rt[:, 6, :], rt[:, 5, :]))
                own.settle()
                own.did(v.tensor_tensor(rt[:, 7, :], rt[:, 6, :], rt[:, 4, :], ALU.mult))
                own.settle()
                for j in range(2):
                    own.did(v.tensor_scalar(wt1[:, j], iota_e[:], topf[:, j, 0:1], rt[:, 6, j:j + 1], ALU.is_equal, ALU.mult))
                    own.did(v.tensor_scalar(wt2[:, j], iota_e[:], topf[:, j, 1:2], rt[:, 7, j:j + 1], ALU.is_equal, ALU.mult))
                own.settle()
                v.tensor_tensor(wt[:], wt1[:], wt2[:], ALU.add).then_inc(s("f_wt"), 1)
                own.end()

            def f_begin(g):
                v.wait_ge(s("f_bias"), g + 1)
                freed(v, s("f_stored"), 16 * g)
                for j in range(2):
                    v.tensor_tensor(f_x2[:, j], pr_(2)[:, j], f_x1[:, j], ALU.add).then_inc(s("f_start"), 1)
                v.wait_ge(s("f_start"), 2 * (g + 1))

            def f_add(g, e):
                v.wait_ge(s("f_o"), g * 6 + e + 1)
                if e:
                    v.wait_ge(s("f_x2"), g * 6 + e)
                for j in range(2):
                    ins = v.scalar_tensor_tensor(f_x2[:, j], pr_(6 + e % 2)[:, j], wt[:, j, e:e + 1], f_x2[:, j],
                                                 ALU.mult, ALU.add)
                ins.then_inc(s("f_x2"), 1)

            def f_experts(g, between):
                f_route1(g)
                f_route2(g)
                f_route3(g)
                between(f_mean)
                f_begin(g)
                f_add(g, 0)
                f_add(g, 1)
                f_add(g, 2)
                between(f_rows)
                for e in range(3, EXPERTS):
                    f_add(g, e)

            f_mean(0)
            f_rows(0)
            def body(i):
                f_experts(i, lambda f: f(i + 1))

            repeated(v, GROUPS - 1, body)
            f_experts(GROUPS - 1, lambda f: None)


_INS = ["x", "src", "dst", "attr", "wselfT", "wfuncT", "wfunc", "att_nodes", "att_edge", "wq", "wk", "wv", "wo",
        "w1", "w2", "bq", "b1", "bkv", "rowvecs", "rw1", "rb1", "rw2", "rb2", "ew1", "ew2", "ew3", "eb1", "eb2", "eb3"]


def lay_out(i):
    import numpy as np

    a = {k: np.asarray(v) for k, v in i.items()}
    c = np.ascontiguousarray
    col = lambda b: c(b.reshape(-1, 128).T)
    return dict(
        x=a["x"], src=a["src"], dst=a["dst"], attr=a["edge_attr_64"],
        wselfT=c(a["L0_gnn_W_self"].T), wfuncT=c(a["L0_gnn_W_func"].T), wfunc=a["L0_gnn_W_func"],
        att_nodes=c(a["L0_gnn_W_att"][0, :2 * D].reshape(2, 2, 128).transpose(2, 1, 0)),
        att_edge=c(a["L0_gnn_W_att"][:, 2 * D:]),
        wq=a["L0_mix_Wq"], wk=a["L0_mix_Wk"], wv=a["L0_mix_Wv"], wo=a["L0_mix_Wo"], w1=a["L0_mix_W1"], w2=a["L0_mix_W2"],
        bq=col(a["L0_mix_bq"]), b1=col(a["L0_mix_b1"]),
        bkv=c(np.concatenate([a["L0_mix_bk"], a["L0_mix_bv"]])[None]),
        rowvecs=c(np.stack([a["L0_mix_" + k] for k in ("bo", "ln1_g", "ln1_b", "b2", "ln2_g", "ln2_b")])),
        rw1=a["L0_ffn_router_w1"], rb1=col(a["L0_ffn_router_b1"]), rw2=a["L0_ffn_router_w2"], rb2=a["L0_ffn_router_b2"][None],
        ew1=a["L0_ffn_expert_w1"], ew2=a["L0_ffn_expert_w2"], ew3=a["L0_ffn_expert_w3"],
        eb1=c(a["L0_ffn_expert_b1"].reshape(EXPERTS, 2, 128).transpose(2, 0, 1)),
        eb2=c(a["L0_ffn_expert_b2"].reshape(EXPERTS, 2, 128).transpose(2, 0, 1)), eb3=a["L0_ffn_expert_b3"],
    )


def kernel(**inputs):
    import concourse.bacc as bacc
    from concourse.bass_utils import run_bass_kernel_spmd as run

    arrays = lay_out(inputs)
    nc = bacc.Bacc("TRN2", target_bir_lowering=False, num_devices=1)
    args = [nc.dram_tensor(f"in_{n}", arrays[n].shape, mybir.dt.from_np(arrays[n].dtype), kind="ExternalInput").ap()
            for n in _INS]
    out = nc.dram_tensor("out_0", (N, D), F32, kind="ExternalOutput").ap()
    build(nc, *args, out)
    r = run(nc, [{f"in_{n}": arrays[n] for n in _INS}], core_ids=[0])
    return r.results[0]["out_0"]
```

```python
from contextlib import ExitStack

import concourse.bass as bass
from concourse import mybir

F32 = mybir.dt.float32
I32 = mybir.dt.int32
U32 = mybir.dt.uint32
BF16 = mybir.dt.bfloat16
F32R = mybir.dt.float32r
ALU = mybir.AluOpType
ACT = mybir.ActivationFunctionType
AX = mybir.AxisListType

N, D = 6250, 256
E, ED = 100000, 64
R = 125
GROUP = 2 * R
GROUPS = N // GROUP
BLOCKS = N // R
PAIRS = E // (2 * R)
STEPS = 450
QS, CS = 75, 6
JS = 2 * CS
LROW = CS * 2 * R
FF = 1024
FC = FF // 128
HEAD = 32
EXPERTS = 6
LO = 128
HIS = -(-N // LO)
PART = 3
ZS = STEPS // GROUPS
HS = ZS // CS
CHUNK = 16
BIG = 1e30
BIG = 1e30
EPS = 1e-5
ROUND = 12582912.0


class Own:

    def __init__(self, eng, sem, per, group):
        self.eng, self.sem, self.per, self.group, self.k = eng, sem, per, group, 0

    def did(self, ins):
        ins.then_inc(self.sem, 1)
        self.k += 1

    def settle(self):
        self.eng.wait_ge(self.sem, self.group * self.per + self.k)

    def end(self):
        assert self.k == self.per, (self.k, self.per)


def freed(eng, sem, count):
    if not (isinstance(count, int) and count <= 0):
        eng.wait_ge(sem, count)


def repeated(eng, n, body):
    body(0)
    with eng.Fori(1, n) as i:
        body(i)


def build(nc, x, src, dst, attr, wselfT, wfuncT, wfunc, att_nodes, att_edge, wq, wk, wv, wo, w1, w2,
          bq, b1, bkv, rowvecs, rw1, rb1, rw2, rb2, ew1, ew2, ew3, eb1, eb2, eb3, out):
    assert STEPS >= PAIRS + BLOCKS - 1 and QS * CS == STEPS
    ctx = ExitStack()
    with ctx:
        def sb(name, shape, dt=F32, stack=ctx):
            return stack.enter_context(nc.sbuf_tensor(name, shape, dt))

        sems = {}

        def s(name):
            if name not in sems:
                sems[name] = ctx.enter_context(nc.semaphore(name))
            return sems[name]

        xn_rows = nc.dram_tensor("xn_rows", (N, D), F32).ap()
        xnT_d = nc.dram_tensor("xnT_d", (GROUPS, 128, 2 * GROUP), F32).ap()
        self_rows = nc.dram_tensor("self_rows", (N, D), F32).ap()
        mix_rows = nc.dram_tensor("mix_rows", (N, D), F32).ap()
        s1_d = nc.dram_tensor("s1_d", (N, 1), F32).ap()
        s2_d = nc.dram_tensor("s2_d", (1, N), F32).ap()
        ew_d = nc.dram_tensor("ew_d", (PAIRS, 2 * R), F32).ap()
        blk_d = nc.dram_tensor("blk_d", (STEPS,), I32).ap()
        lr_d = nc.dram_tensor("lr_d", (QS, 2 * LROW), BF16).ap()

        def rows_of(t, g):
            v = t.rearrange("(g j p) d -> g p j d", j=2, p=R)
            return v[bass.ds(g, 1)].rearrange("g p j d -> (g p) j d")

        ident = sb("ident", [128, 128])
        bmask = sb("bmask", [128, 128])
        iota_r = sb("iota_r", [R, R])
        iota_e = sb("iota_e", [R, EXPERTS])
        iota_s = sb("iota_s", [QS, CS])
        iota_t = sb("iota_t", [1, PAIRS])
        iota_p = sb("iota_p", [128, 1])
        iota_h = sb("iota_h", [R, HIS])
        ones_row = sb("ones_row", [1, 128])
        rv = sb("rv", [R, 6, D])
        rb2_bc = sb("rb2_bc", [R, EXPERTS])
        awe = sb("awe", [R, ED])
        bq_c = sb("bq_c", [128, 2])
        b1_c = sb("b1_c", [128, FC])
        rb1_c = sb("rb1_c", [128, 1])
        eb_c = sb("eb_c", [128, 2, EXPERTS, 2])
        eb3_s = sb("eb3_s", [EXPERTS, D])
        wself_s = sb("wself_s", [128, 2, D])
        wfunc_s = sb("wfunc_s", [128, 2, D])
        wfuncT_s = sb("wfuncT_s", [128, 2, D])
        rw1_s = sb("rw1_s", [128, 2, 128])
        rw2_s = sb("rw2_s", [128, EXPERTS])
        attn_c = sb("attn_c", [128, 2, 2])
        u_s = sb("u_s", [128, 2, 2])
        a_s = sb("a_s", [R, 2, JS])
        s1_rows = sb("s1_rows", [HIS, LO])
        blk_row = sb("blk_row", [1, STEPS], I32)
        acc = sb("acc", [R, BLOCKS * (D + 1)])
        accv = acc[:].rearrange("p (b n) -> p b n", n=D + 1)

        def early(k, n=LROW):
            return acc[0:QS, k * (LROW + 4):k * (LROW + 4) + n]

        src_i, dst_i, src_f, dst_f, rel_l = early(0).bitcast(I32), early(1).bitcast(I32), early(2), early(3), early(4)
        hi_l = early(0)
        lr_l = early(5, LROW).bitcast(BF16)
        lr_l = lr_l.rearrange("p (a e) -> p a e", a=2)
        s2_rows = early(6, CS * R)
        ew_l, reset, e_l, b_l = early(0), early(1, LROW + 1), early(2), early(4)
        valid, t_l, f_l = early(5), early(6), early(7)
        attr_s = acc[:, 5 * (LROW + 4):5 * (LROW + 4) + 2 * CHUNK * ED].rearrange("p (h k f) -> p h k f", h=2, f=ED)
        ew_n = acc[:, 6 * (LROW + 4) + CHUNK * ED:6 * (LROW + 4) + CHUNK * ED + E // R]
        tabs = sb("tabs", [QS, 8, CS])
        tab_i = sb("tab_i", [QS, 2, CS], I32)
        dlast = sb("dlast", [1, PAIRS], I32)
        idx_slot = sb("idx_slot", [R, HS, JS], I32)
        mark = sb("mark", [1, 1])
        sm = sb("sm", [QS, 8])
        smr = sb("smr", [1, 12, 92])
        work = sb("work", [128, 16 * 512])

        def w(k, shape, n=1):
            v = work[0:shape[0], 512 * k:512 * (k + n)]
            size = 1
            for a in shape[1:]:
                size *= a
            v = v[:, 0:size]
            if len(shape) == 3:
                v = v.rearrange("p (a b) -> p a b", a=shape[1])
            return v

        xn_in, xnT_in = w(0, [R, 2, D]), w(1, [128, 2, GROUP])
        f_self = w(1, [R, 2, D])
        p_x, p_xn, p_xnT = w(2, [R, 2, D]), w(3, [R, 2, D]), w(4, [128, 2, GROUP])
        p_s = w(5, [2, GROUP])
        p_k, p_min, p_exp, p_phi = w(6, [R, 2, D]), w(7, [R, 2, D]), w(8, [R, 2, D]), w(9, [R, 2, D])
        p_v = [w(10, [R, 2, 129]), w(11, [R, 2, 129])]
        wkv_s, bkv_bc, zeros = w(12, [128, 2, 2 * D], 2), w(14, [R, 2 * D]), w(15, [128, 260])
        tab_t = w(10, [1, 2, PAIRS], 2)
        l_self = w(2, [R, 2, D])
        away, sel = w(6, [R, HS, JS * HIS], 4), w(10, [R, JS, HIS], 2)
        s2_t = w(12, [R, 2, CS * QS], 2)
        s1_t = w(14, [128, 2, HIS])
        m_q, m_e, m_r, m_n = w(2, [128, 2, GROUP]), w(3, [128, 2, GROUP]), w(4, [128, 2, GROUP]), w(5, [128, 2, GROUP])
        m_z, m_y, m_yb, m_yT = w(6, [R, 2, D]), w(7, [R, 2, D]), w(8, [R, 2, D]), w(9, [128, 2, GROUP])
        m_h = w(10, [128, FC, GROUP], 4)
        m_z2, m_o = w(14, [R, 2, D]), w(15, [R, 2, D])
        f_x, f_mix, f_an, f_aT = w(2, [R, 2, D]), w(3, [R, 2, D]), w(4, [R, 2, D]), w(5, [128, 2, GROUP])
        f_t, f_x1, f_xT, f_x2 = w(6, [R, 2, D]), w(7, [R, 2, D]), w(8, [128, 2, GROUP]), w(9, [R, 2, D])
        f_h1 = [w(10, [128, 2, GROUP]), w(11, [128, 2, GROUP])]
        f_h2 = [w(12, [128, 2, GROUP]), w(13, [128, 2, GROUP])]
        f_rh, f_wT = w(14, [128, GROUP]), w(15, [EXPERTS, GROUP])
        st = sb("st", [R, 2, 6])
        mv = sb("mv", [R, 2, 2])
        lnv = sb("lnv", [R, 2])
        rstd = sb("rstd", [R, 2])
        st2, mv2 = sb("st2", [R, 2, 6]), sb("mv2", [R, 2, 2])
        lnv2, rstd2 = sb("lnv2", [R, 2]), sb("rstd2", [R, 2])
        dn = sb("dn", [R, 3, 2])
        lg = sb("lg", [R, 2, 8])
        pr = sb("pr", [R, 2, 8])
        top = sb("top", [R, 2, 8])
        topi = sb("topi", [R, 2, 8], U32)
        topf = sb("topf", [R, 2, 2])
        rt = sb("rt", [R, 8, 2])
        wt1, wt2, wt = sb("wt1", [R, 2, EXPERTS]), sb("wt2", [R, 2, EXPERTS]), sb("wt", [R, 2, EXPERTS])

        place = ExitStack()
        wexp = sb("wexp", [128, 3 * EXPERTS * 2 * D], stack=place)
        wexpv = wexp[:].rearrange("p (l e c n) -> p l e c n", l=3, e=EXPERTS, c=2)
        lr_bc = [wexp[:, k * LROW:(k + 1) * LROW].bitcast(BF16) for k in range(HS)]
        lr_oh = [wexp[:, HS * LROW + k * (LROW + 2):HS * LROW + (k + 1) * (LROW + 2)].bitcast(BF16) for k in range(HS)]
        place.close()
        w_lo = sb("w_lo", [128, 3, EXPERTS, 2, D], F32R)
        place = ExitStack()
        wq_s = sb("wq_s", [128, 2, D], stack=place)
        wo_s = sb("wo_s", [128, 2, D], stack=place)
        w1_s = sb("w1_s", [128, 2, FF], stack=place)
        w2_s = sb("w2_s", [128, FC, D], stack=place)
        kvbd = sb("kvbd", [128, 2, 128], stack=place)
        ksbd = sb("ksbd", [128, 2, 128], stack=place)
        a_src = sb("a_src", [R, QS, JS], I32, stack=place)
        a_rel = sb("a_rel", [R, QS, JS], stack=place)
        a_hi = sb("a_hi", [R, QS, JS], stack=place)
        a_u = sb("a_u", [R, QS, JS], stack=place)
        a_p = a_hi
        s1_p = sb("s1_p", [128, PART, HIS], BF16, stack=place)
        s2_p = sb("s2_p", [R, CS * QS, PART], BF16, stack=place)
        ring = sb("ring", [R, 2 * CS, D + 1], stack=place)
        onehot = sb("onehot", [R, 2 * CS, R], stack=place)
        junk = onehot[:].rearrange("p a b -> p (a b)")
        place.close()
        w_hi = sb("w_hi", [128, 3, EXPERTS, 2, D], F32R)
        x_hl = [sb(f"x_{n}", [128, 2, GROUP], F32R) for n in ("hi", "lo")]
        h1_hl = [[sb(f"h1_{n}{k}", [128, 2, GROUP], F32R) for n in ("hi", "lo")] for k in range(2)]
        h2_hl = [[sb(f"h2_{n}{k}", [128, 2, GROUP], F32R) for n in ("hi", "lo")] for k in range(2)]

        bank = [ctx.enter_context(nc.psum_tensor(f"bank{i}", [128, 512], F32)) for i in range(8)]

        def pt(b):
            return bank[b][:, 0:2 * GROUP].rearrange("p (c n) -> p c n", c=2)

        def pr_(b):
            return bank[b][0:R, :].rearrange("p (j n) -> p j n", j=2)

        def apart(eng, name):
            eng.sem_inc(s(name), 1)

        block = ctx.enter_context(nc.Block())
        LOADS_EARLY, LOADS_MIX, LOADS_LATE, CONSTS = 6, 21, 3 * EXPERTS, 8

        @block.sync
        def _(sp):
            def load(sem, dst_, src_):
                sp.dma_start(dst_, src_).then_inc(s(sem), 16)

            with nc.allow_non_contiguous_dma(reason="one index of each pair of edge tiles"):
                load("dlast_in", dlast[:], dst.rearrange("(t e) -> t e", e=2 * R)[:, 2 * R - 1:2 * R]
                     .rearrange("t e -> e t"))
            cols = lambda t: t.rearrange("(c p) n -> p c n", p=128)
            load("p1_x", p_x, rows_of(x, 0))
            load("w_in", wfunc_s[:], cols(wfunc))
            load("w_in", attn_c[:], att_nodes)
            load("w_in", wkv_s[:, :, 0:D], cols(wk))
            load("w_in", wkv_s[:, :, D:2 * D], cols(wv))
            load("w_in", bkv_bc, bkv.to_broadcast([R, 2 * D]))
            load("w_in", awe[:], att_edge.to_broadcast([R, ED]))
            load("w2_in", wq_s[:], cols(wq))
            load("w2_in", wo_s[:], cols(wo))
            load("w2_in", w1_s[:], cols(w1))
            load("w2_in", w2_s[:], cols(w2))
            load("w2_in", bq_c[:], bq)
            load("w2_in", b1_c[:], b1)
            load("w2_in", rb2_bc[:], rb2.to_broadcast([R, EXPERTS]))
            load("w2_in", rb1_c[:], rb1)
            for k in range(6):
                load("w2_in", rv[:, k, :], rowvecs[k:k + 1, :].to_broadcast([R, D]))
            load("w2_in", eb_c[:, 0], eb1)
            load("w2_in", eb_c[:, 1], eb2)
            load("w2_in", eb3_s[:], eb3)
            load("w2_in", wself_s[:], cols(wselfT))
            load("w2_in", wfuncT_s[:], cols(wfuncT))
            load("w2_in", rw1_s[:], cols(rw1))
            load("w2_in", rw2_s[:], rw2)
            sp.wait_ge(s("tab_v"), 2)
            load("blk_out", blk_d.rearrange("(q c) -> q c", c=CS), tab_i[:, 1, :])
            sp.wait_ge(s("blk_out"), 16)
            load("blk_in", blk_row[:], blk_d[None, :])

            attr_v = attr.rearrange("(p c k) f -> c p k f", p=R, k=CHUNK)

            def pass1(g, more):
                sp.wait_ge(s("p1_xn"), g + 1)
                if more:
                    load("p1_x", p_x, rows_of(x, g + 1))
                load("p1_xn_out", rows_of(xn_rows, g), p_xn)
                for h in range(2):
                    freed(sp, s(f"attr_used{h}"), g)
                    load(f"attr_in{h}", attr_s[:, h], attr_v[bass.ds(g * 2 + h, 1)].rearrange("c p k f -> (c p) k f"))
                sp.wait_ge(s("p1_xnT"), g + 1)
                load("p1_xnT_out", xnT_d[bass.ds(g, 1)].rearrange("g p n -> (g p) n"),
                     p_xnT.rearrange("p c n -> p (c n)"))
                sp.wait_ge(s("p1_s"), g + 1)
                load("p1_s_out", s1_d.rearrange("(g n) a -> a g n", n=GROUP)[:, bass.ds(g, 1), :]
                     .rearrange("a g n -> a (g n)"), p_s[0:1, :])
                load("p1_s_out", s2_d.rearrange("a (g n) -> a g n", n=GROUP)[:, bass.ds(g, 1), :]
                     .rearrange("a g n -> a (g n)"), p_s[1:2, :])

            def body(i):
                pass1(i, True)

            repeated(sp, GROUPS - 1, body)
            pass1(GROUPS - 1, False)
            for h in range(2):
                sp.wait_ge(s(f"attr_used{h}"), GROUPS)
            load("ew_out", ew_d.rearrange("t e -> (t e)").rearrange("(p k) -> p k", p=R), ew_n)
            sp.wait_ge(s("p1_s_out"), 32 * GROUPS)
            sp.wait_ge(s("consts"), CONSTS)
            load("s1_in", s1_rows[0:HIS - 1, :], s1_d[0:(HIS - 1) * LO, :].rearrange("(h l) a -> h (l a)", l=LO))
            load("s1_in", s1_rows[HIS - 1:HIS, 0:N - (HIS - 1) * LO], s1_d[(HIS - 1) * LO:N, :].rearrange("n a -> a n"))
            sp.wait_ge(s("lr_done"), 2)
            load("lr_out", lr_d, lr_l.rearrange("p a e -> p (a e)"))
            sp.wait_ge(s("lr_out"), 16)

            def self_out(i):
                sp.wait_ge(s("l_self"), i + 1)
                load("self_out", rows_of(self_rows, i), l_self)

            sp.wait_ge(s("p1_xn_out"), 16 * GROUPS)
            sp.wait_ge(s("p1_xnT_out"), 16 * GROUPS)

            def body(i):
                for h in range(HS):
                    freed(sp, s("lr_oh"), i * HS + h - HS + 1)
                    load(f"lr_in{h}", lr_bc[h], lr_d[bass.ds(i * HS + h, 1)].to_broadcast([128, 2 * LROW]))
                freed(sp, s("l_self_ps"), i)
                load("self_in", xnT_in.rearrange("p c n -> p (c n)"),
                     xnT_d[bass.ds(i, 1)].rearrange("g p n -> (g p) n"))
                if not isinstance(i, int):
                    self_out(i - 1)

            repeated(sp, QS // HS, body)
            self_out(GROUPS - 1)
            sp.wait_ge(s("l_self_ps"), GROUPS)
            def mix_in(g):
                freed(sp, s("m_q"), g)
                load("m_xnT", xnT_in.rearrange("p c n -> p (c n)"),
                     xnT_d[bass.ds(g, 1)].rearrange("g p n -> (g p) n"))
                freed(sp, s("m_xb"), g)
                load("m_xn", xn_in, rows_of(xn_rows, g))

            def mix_out(g):
                sp.wait_ge(s("m_out"), g + 1)
                load("m_stored", rows_of(mix_rows, g), m_o)

            mix_in(0)
            sp.wait_ge(s("lr_used"), QS)
            for l, t in enumerate((ew1, ew2, ew3)):
                for e in range(EXPERTS):
                    load("wexp_in", wexpv[:, l, e], cols(t[e]))

            def body(i):
                mix_in(i + 1)
                if not isinstance(i, int):
                    mix_out(i - 1)

            repeated(sp, GROUPS - 1, body)
            mix_out(GROUPS - 2)
            mix_out(GROUPS - 1)
            sp.wait_ge(s("m_stored"), 16 * (GROUPS + 1))

            sp.wait_ge(s("self_out"), 16 * GROUPS)

            def last_in(g):
                freed(sp, s("f_x1"), g)
                load("f_rows", f_self, rows_of(self_rows, g))
                load("f_rows", xn_in, rows_of(xn_rows, g))
                load("f_rows", f_x, rows_of(x, g))
                load("f_rows", f_mix, rows_of(mix_rows, g))

            def last_out(g):
                sp.wait_ge(s("f_x2"), EXPERTS * (g + 1))
                load("f_stored", rows_of(out, g), f_x2)

            last_in(0)
            def body(i):
                last_in(i + 1)
                last_out(i)

            repeated(sp, GROUPS - 1, body)
            last_out(GROUPS - 1)
            sp.wait_ge(s("f_stored"), 16 * GROUPS)

        @block.gpsimd
        def _(pool):
            own = Own(pool, s("pool_own"), 0, 0)
            iota = dict(allow_small_or_imprecise_dtypes=True)
            pool.iota(iota_t[:], [[1, PAIRS]], base=0, channel_multiplier=0, **iota).then_inc(s("iota_tabs"), 1)
            pool.iota(iota_s[:], [[1, CS]], base=0, channel_multiplier=CS, **iota).then_inc(s("iota_tabs"), 1)
            pool.memset(ones_row[:], 1.0).then_inc(s("iota_tabs"), 1)
            own.did(pool.memset(ident[:], 0.0))
            own.did(pool.memset(bmask[:], 1.0))
            own.settle()
            pool.affine_select(out=ident[:], in_=ident[:], compare_op=ALU.not_equal, fill=1.0, base=0,
                               pattern=[[-1, 128]], channel_multiplier=1).then_inc(s("ident_done"), 1)
            bm = bmask[:].rearrange("p (b k) -> p b k", k=HEAD)
            own.did(pool.affine_select(out=bm, in_=bm, compare_op=ALU.is_ge, fill=0.0, base=0,
                                       pattern=[[-HEAD, 128 // HEAD], [0, HEAD]], channel_multiplier=1))
            own.settle()
            pool.affine_select(out=bm, in_=bm, compare_op=ALU.is_ge, fill=0.0, base=HEAD - 1,
                               pattern=[[HEAD, 128 // HEAD], [0, HEAD]],
                               channel_multiplier=-1).then_inc(s("consts"), 1)
            pool.iota(iota_r[:], [[1, R]], base=0, channel_multiplier=0, **iota).then_inc(s("consts"), 1)
            pool.iota(iota_e[:], [[1, EXPERTS]], base=0, channel_multiplier=0, **iota).then_inc(s("consts"), 1)
            pool.memset(zeros, 0.0).then_inc(s("consts"), 1)

            pool.iota(iota_p[:], [[0, 1]], base=0, channel_multiplier=1, **iota).then_inc(s("consts"), 1)
            pool.iota(iota_h[:], [[1, HIS]], base=0, channel_multiplier=0, **iota).then_inc(s("consts"), 1)
            pool.memset(s1_rows[:], 0.0).then_inc(s("consts"), 1)
            pool.memset(ring[:, :, D:D + 1], 1.0).then_inc(s("consts"), 1)

            pool.wait_ge(s("tab_v"), 2)
            for c in range(CS):
                at = bass.IndirectOffsetOnAxis(ap=tab_i[:, 0, c:c + 1], axis=0)
                for d_, s_ in ((src_i, src), (dst_i, dst)):
                    pool.indirect_dma_start(d_[:, c * 2 * R:(c + 1) * 2 * R], None,
                                            s_.rearrange("(t e) -> t e", e=2 * R), at).then_inc(s("sd_in"), 16)

            pool.wait_ge(s("w_in"), 16 * LOADS_EARLY)

            def body(i):
                own = Own(pool, s("attr_own"), 1, i)
                for h in range(2):
                    pool.wait_ge(s(f"attr_in{h}"), i * 16 + 16)
                    ins = pool.tensor_tensor(attr_s[:, h], attr_s[:, h],
                                             awe[:, None, :].to_broadcast([R, CHUNK, ED]), ALU.mult)
                    if h == 1:
                        ins.then_inc(s("attr_mul1"), 1)
                    else:
                        own.did(ins)
                        own.settle()
                        pool.tensor_tensor(attr_s[:, h, :, 0:ED // 2], attr_s[:, h, :, 0:ED // 2],
                                           attr_s[:, h, :, ED // 2:ED], ALU.add).then_inc(s("attr_mul0"), 1)

            repeated(pool, GROUPS, body)
            pool.wait_ge(s("p1_s_out"), 32 * GROUPS)
            pool.wait_ge(s("ew_out"), 16)
            for c in range(CS):
                pool.indirect_dma_start(s2_rows[:, c * R:(c + 1) * R], None, s2_d.rearrange("a (b n) -> (a b) n", n=R),
                                        bass.IndirectOffsetOnAxis(ap=tab_i[:, 1, c:c + 1], axis=0)
                                        ).then_inc(s("s2_in"), 16)
            pool.wait_ge(s("a_done"), 6)

            def body(q):
                for h in range(HS):
                    p = q * HS + h
                    freed(pool, s("selected"), p - HS + 1)
                    pool.tensor_tensor(
                        away[:, h, :].rearrange("p (j n) -> p j n", n=HIS),
                        iota_h[:, None, :].to_broadcast([R, JS, HIS]),
                        a_hi[:, bass.ds(p, 1), :].rearrange("p a j -> p j a").to_broadcast([R, JS, HIS]),
                        ALU.subtract).then_inc(s("away"), 1)

            repeated(pool, QS // HS, body)
            pool.wait_ge(s("a_ps"), 6)
            pool.wait_ge(s("lr_done"), 1)
            for c in range(CS):
                pool.indirect_dma_start(ew_l[:, c * 2 * R:(c + 1) * 2 * R], None, ew_d,
                                        bass.IndirectOffsetOnAxis(ap=tab_i[:, 0, c:c + 1], axis=0)
                                        ).then_inc(s("ew_in"), 16)
            pool.wait_ge(s("soft_v"), 3)
            for k0, k1 in ((0, 2), (3, 5)):
                pool.memset(acc[:, k0 * (LROW + 4):k1 * (LROW + 4)], 0.0).then_inc(s("soft_in"), 1)
            pool.memset(acc[:, 7 * (LROW + 4):], 0.0).then_inc(s("soft_in"), 1)

            def body(i):
                for h in range(HS):
                    q = i * HS + h
                    for c in range(CS):
                        freed(pool, s(f"rows_in{c}"), (q - HS + 1) * 32)
                    pool.tensor_copy(idx_slot[:, h, :], a_src[:, bass.ds(q, 1), :]
                                     .rearrange("p a j -> p (a j)")).then_inc(s("idx"), 1)
                    for c in range(CS):
                        freed(pool, s("stepped"), q * CS - CS + c + 1)
                        if c == 0:
                            pool.wait_ge(s("idx"), q + 1)
                        apart(pool, "past")
                        for k in range(2):
                            pool.indirect_dma_start(
                                ring[:, 2 * c + k, 0:D], None, xn_rows,
                                bass.IndirectOffsetOnAxis(ap=idx_slot[:, h, 2 * c + k:2 * c + k + 1], axis=0)
                            ).then_inc(s(f"rows_in{c}"), 16)

            pool.wait_ge(s("p1_xn_out"), 16 * GROUPS)
            repeated(pool, QS // HS, body)

            def body(g):
                pool.wait_ge(s("f_an"), 2 * (g + 1))
                freed(pool, s("f_T1"), g)
                pool.wait_ge(s("f_rows"), 64 * (g + 1))
                apart(pool, "past")
                for j in range(2):
                    pool.tensor_scalar(f_t[:, j], xn_in[:, j], dn[:, 2, j:j + 1], None, ALU.mult).then_inc(s("f_pre"), 1)
                    pool.tensor_scalar(f_self[:, j], f_self[:, j], dn[:, 1, j:j + 1], None,
                                       ALU.mult).then_inc(s("f_pre"), 1)
                pool.tensor_tensor(f_x, f_x, xn_in, ALU.add).then_inc(s("f_pre"), 1)
                pool.wait_ge(s("f_pre"), 7 * g + 4)
                pool.tensor_tensor(f_t, f_t, f_self, ALU.add).then_inc(s("f_pre"), 1)
                pool.wait_ge(s("f_pre"), 7 * g + 5)
                pool.tensor_tensor(f_x, f_x, f_mix, ALU.add).then_inc(s("f_pre"), 1)

            repeated(pool, GROUPS, body)

        @block.tensor
        def _(pe):
            def mm(o, l, r, first, last_, **kw):
                return pe.matmul(o, l, r, start=first, stop=last_, **kw)

            pe.wait_ge(s("w_in"), 16 * LOADS_EARLY)
            for c in range(2):
                for o in range(2):
                    last = mm(bank[0][:, 2 * c:2 * c + 2], wfunc_s[:, o, c * 128:(c + 1) * 128],
                              attn_c[:, o, :], o == 0, o == 1)
            last.then_inc(s("tab_ps"), 1)
            pe.wait_ge(s("tab_v"), 1)
            mm(bank[1][0:QS, 0:PAIRS], ones_row[:, 0:QS], tab_t[:, 1, :], True, True).then_inc(s("tab_ps"), 1)
            pe.wait_ge(s("tab_v"), 2)
            pe.wait_ge(s("ident_done"), 1)
            pe.wait_ge(s("tab_v"), 3)
            pe.wait_ge(s("consts"), CONSTS)
            mm(bank[7][:, 0:258], zeros[:, 0:128], zeros[:, 0:258], True, False, skip_group_check=True)

            def transposes(g):
                pe.wait_ge(s("p1_xn"), g + 1)
                freed(pe, s("p1_xnT"), g)
                for c in range(2):
                    for j in range(2):
                        last = pe.transpose(pt(0)[:, c, j * R:(j + 1) * R], p_xn[:, j, c * 128:(c + 1) * 128],
                                            ident[0:R, 0:R])
                last.then_inc(s("p1_T"), 1)

            def products(g, j):
                pe.wait_ge(s("p1_xnT"), g + 1)
                if j == 0:
                    freed(pe, s("p1_s"), g)
                    for c in range(2):
                        last = mm(bank[1][0:2, 0:GROUP], u_s[:, c, :], p_xnT[:, c, :], c == 0, c == 1)
                    last.then_inc(s("p1_s_ps"), 1)
                freed(pe, s("p1_kv_read"), 2 * g + j - 1)
                for c in range(2):
                    last = mm(bank[2 + j][0:R, :], p_xnT[:, c, j * R:(j + 1) * R], wkv_s[:, c, :], c == 0, c == 1)
                last.then_inc(s("p1_kv"), 1)

            def kv_sum(g, j):
                pe.wait_ge(s("p1_phi"), 2 * g + j + 1)
                for c in range(2):
                    last = mm(bank[7][:, c * 129:(c + 1) * 129], p_phi[:, j, c * 128:(c + 1) * 128],
                              p_v[j][:, c, :], False, False, skip_group_check=True)
                last.then_inc(s("p1_sum"), 1)

            transposes(0)
            products(0, 0)
            products(0, 1)
            def body(i):
                transposes(i + 1)
                kv_sum(i, 0)
                products(i + 1, 0)
                kv_sum(i, 1)
                products(i + 1, 1)

            repeated(pe, GROUPS - 1, body)
            kv_sum(GROUPS - 1, 0)
            kv_sum(GROUPS - 1, 1)
            mm(bank[7][:, 0:258], zeros[:, 0:128], zeros[:, 0:258], False, True,
               skip_group_check=True).then_inc(s("kv_done"), 1)

            pe.wait_ge(s("p1_s"), GROUPS)
            pe.wait_ge(s("p1_kv_read"), 2 * GROUPS)
            for a, what in enumerate((src_f, rel_l, hi_l)):
                pe.wait_ge(s("l_done"), a + 1)
                for j in range(JS):
                    last = pe.transpose(bank[1 + 2 * a + j // CS][0:R, (j % CS) * QS:(j % CS + 1) * QS],
                                        what[:, j * R:(j + 1) * R], ident[0:QS, 0:QS])
                    if j % CS == CS - 1:
                        last.then_inc(s("a_ps"), 1)
            pe.wait_ge(s("s1_in"), 32)
            pe.wait_ge(s("kvbd"), 4)
            pe.transpose(bank[7][:, 0:HIS], s1_rows[:], ident[0:HIS, 0:HIS]).then_inc(s("look_ps"), 1)
            pe.wait_ge(s("s2_in"), 16 * CS)
            pe.wait_ge(s("p1_xnT"), GROUPS)
            for c in range(CS):
                last = pe.transpose(bank[0][0:R, c * QS:(c + 1) * QS], s2_rows[:, c * R:(c + 1) * R], ident[0:QS, 0:QS])
            last.then_inc(s("look_ps"), 1)
            pe.wait_ge(s("a_done"), 6)
            pe.wait_ge(s("s1_parts"), PART)
            pe.wait_ge(s("s2_parts"), PART)

            pe.wait_ge(s("w2_in"), 16 * LOADS_MIX)

            def self_part(g):
                pe.wait_ge(s("self_in"), 16 * (g + 1))
                freed(pe, s("l_self"), g)
                for j in range(2):
                    for c in range(2):
                        last = mm(pr_(0)[:, j, :], xnT_in[:, c, j * R:(j + 1) * R], wself_s[:, c, :], c == 0, c == 1)
                last.then_inc(s("l_self_ps"), 1)

            def body(i):
                for h in range(HS):
                    if h == 1:
                        self_part(i)
                    q = i * HS + h
                    pe.wait_ge(s("lr_oh"), q + 1)
                    freed(pe, s("selected"), q - HS + 1)
                    for j in range(JS):
                        for p in range(PART):
                            mm(bank[1 + 2 * h + j // CS][:, (j % CS) * HIS:(j % CS + 1) * HIS],
                               lr_oh[h][:, j * R:j * R + 128], s1_p[:, p, :], p == 0, p == PART - 1)
                    for j in range(JS):
                        last = mm(bank[2 + 2 * h][:, CS * HIS + PART * j:CS * HIS + PART * (j + 1)],
                                  lr_oh[h][0:R, LROW + j * R:LROW + j * R + 128],
                                  s2_p[:, bass.ds(q + j // 2 * QS, 1), :].rearrange("p a k -> p (a k)"), True, True)
                    last.then_inc(s("lr_used"), 1)

            repeated(pe, QS // HS, body)
            pe.wait_ge(s("selected"), QS)
            pe.wait_ge(s("l_self"), GROUPS)


            def queries(g):
                pe.wait_ge(s("m_xnT"), 16 * (g + 1))
                freed(pe, s("m_qread"), 2 * g)
                freed(pe, s("m_min"), 2 * g)
                for o in range(2):
                    for c in range(2):
                        last = mm(pt(0)[:, o, :], wq_s[:, c, o * 128:(o + 1) * 128], xnT_in[:, c, :], c == 0, c == 1)
                last.then_inc(s("m_q"), 1)

            def attention(g):
                pe.wait_ge(s("m_phi"), g + 1)
                freed(pe, s("m_z"), g)
                freed(pe, s("m_yT"), g)
                for o in range(2):
                    mm(pt(1)[:, o, :], ksbd[:, o, :], m_n[:, o, :], True, True)
                for o in range(2):
                    last = mm(pt(2)[:, o, :], kvbd[:, o, :], m_n[:, o, :], True, True)
                last.then_inc(s("m_nd"), 1)

            def project(g):
                pe.wait_ge(s("m_att"), g + 1)
                for j in range(2):
                    for c in range(2):
                        last = mm(pr_(1)[:, j, :], m_e[:, c, j * R:(j + 1) * R], wo_s[:, c, :], c == 0, c == 1)
                last.then_inc(s("m_o_ps"), 1)

            def turn(g):
                pe.wait_ge(s("m_y"), g + 1)
                freed(pe, s("m_yT"), g)
                for c in range(2):
                    for j in range(2):
                        last = pe.transpose(pt(2)[:, c, j * R:(j + 1) * R], m_y[:, j, c * 128:(c + 1) * 128],
                                            ident[0:R, 0:R])
                last.then_inc(s("m_T"), 1)

            def hidden(g, o2):
                pe.wait_ge(s("m_yT"), g + 1)
                for h in range(2):
                    f = 2 * o2 + h
                    freed(pe, s("m_hread"), g * 8 + f - 1)
                    for c in range(2):
                        last = mm(bank[5 + h][:, 0:GROUP], w1_s[:, c, f * 128:(f + 1) * 128], m_yT[:, c, :],
                                  c == 0, c == 1)
                    last.then_inc(s("m_h"), 1)

            def down(g, j):
                pe.wait_ge(s("m_hread"), g * 8 + 8)
                if j == 0:
                    freed(pe, s("m_z2"), g)
                for f in range(FC):
                    last = mm(pr_(7)[:, j, :], m_h[:, f, j * R:(j + 1) * R], w2_s[:, f, :], f == 0, f == FC - 1)
                last.then_inc(s("m_d"), 1)

            def step(i, z):
                n = i * ZS + z
                pe.wait_ge(s(f"rows_in{z % CS}"), i * (32 * HS) + 32 * (z // CS) + 32)
                pe.wait_ge(s("onehot"), 2 * n + 2)
                freed(pe, s("summed"), n - 1)
                for k in range(2):
                    last = mm(bank[3 + z % 2][0:R, 0:D + 1], onehot[:, 2 * (z % CS) + k, :], ring[:, 2 * (z % CS) + k, :],
                              k == 0, k == 1)
                last.then_inc(s("stepped"), 1)

            def body(i, more=True):
                if more:
                    queries(i + 1)
                for o2 in range(3):
                    hidden(i, o2)
                for z in range(CS):
                    step(i, z)
                if more:
                    attention(i + 1)
                hidden(i, 3)
                down(i, 0)
                for z in range(CS, 2 * CS):
                    step(i, z)
                if more:
                    project(i + 1)
                down(i, 1)
                for z in range(2 * CS, 3 * CS):
                    step(i, z)
                if more:
                    turn(i + 1)

            for j in range(JS):
                last = pe.transpose(bank[j // 4][0:QS, (j % 4) * R:(j % 4 + 1) * R], a_u[:, :, j], ident[0:R, 0:R])
            last.then_inc(s("soft_ps"), 1)
            pe.wait_ge(s("soft_v"), 1)
            queries(0)
            attention(0)
            pe.wait_ge(s("summary"), 5)
            for k in range(5):
                last = mm(bank[3][0:1, k * QS:(k + 1) * QS], sm[:, k:k + 1], ident[0:QS, 0:QS], True, True)
            last.then_inc(s("soft_ps"), 1)
            pe.wait_ge(s("soft_v"), 2)
            mm(bank[4][0:QS, 0:1], smr[0:1, 5, 0:QS], ones_row[:, 0:1], True, True)
            mm(bank[4][0:QS, 1:2], smr[0:1, 6, 0:QS], ones_row[:, 0:1], True, True).then_inc(s("soft_ps"), 1)
            project(0)
            pe.wait_ge(s("soft_v"), 4)
            for j in range(JS):
                last = pe.transpose(bank[5 + j // CS][0:R, (j % CS) * QS:(j % CS + 1) * QS], t_l[:, j * R:(j + 1) * R],
                                    ident[0:QS, 0:QS])
            last.then_inc(s("soft_ps"), 1)

            turn(0)
            pe.wait_ge(s("soft_v"), 5)
            repeated(pe, GROUPS - 1, body)
            body(GROUPS - 1, False)

            def agg_turn(g):
                pe.wait_ge(s("f_an"), 2 * (g + 1))
                freed(pe, s("f_aT"), g)
                for c in range(2):
                    for j in range(2):
                        last = pe.transpose(pt(0)[:, c, j * R:(j + 1) * R], f_an[:, j, c * 128:(c + 1) * 128],
                                            ident[0:R, 0:R])
                last.then_inc(s("f_T"), 1)

            def gnn(g):
                pe.wait_ge(s("f_aT"), g + 1)
                freed(pe, s("f_start"), 2 * g)
                for j in range(2):
                    for c in range(2):
                        last = mm(pr_(2)[:, j, :], f_aT[:, c, j * R:(j + 1) * R], wfuncT_s[:, c, :], c == 0, c == 1)
                last.then_inc(s("f_gnn"), 1)

            def norm_turn(g):
                pe.wait_ge(s("f_xn1"), 2 * (g + 1))
                freed(pe, s("f_xT"), g)
                freed(pe, s("f_full1"), g * 6)
                for c in range(2):
                    for j in range(2):
                        last = pe.transpose(pt(1)[:, c, j * R:(j + 1) * R], f_t[:, j, c * 128:(c + 1) * 128],
                                            ident[0:R, 0:R])
                last.then_inc(s("f_T1"), 1)

            def router(g):
                pe.wait_ge(s("f_xT"), g + 1)
                freed(pe, s("f_wTc"), g)
                for c in range(2):
                    last = mm(bank[3][:, 0:GROUP], rw1_s[:, c, :], f_xT[:, c, :], c == 0, c == 1)
                last.then_inc(s("f_rh_ps"), 1)

            def logits(g):
                pe.wait_ge(s("f_rh"), g + 1)
                for j in range(2):
                    last = mm(bank[3][0:R, 256 + 8 * j:256 + 8 * j + EXPERTS], f_rh[:, j * R:(j + 1) * R], rw2_s[:],
                              True, True)
                last.then_inc(s("f_lg_ps"), 1)

            def weights_turn(g):
                pe.wait_ge(s("f_wt"), g + 1)
                for j in range(2):
                    last = mm(bank[3][0:EXPERTS, j * R:(j + 1) * R], wt[:, j, :], ident[0:R, 0:R], True, True)
                last.then_inc(s("f_wT_ps"), 1)

            def biases(g):
                pe.wait_ge(s("f_wTc"), g + 1)
                pe.wait_ge(s("f_r"), g + 1)
                for j in range(2):
                    last = mm(pr_(2)[:, j, :], f_wT[:, j * R:(j + 1) * R], eb3_s[:], True, True)
                last.then_inc(s("f_bias"), 1)

            def exact(o, lo_l, hi_l_, lo_r, hi_r, first, last_):
                mm(o, hi_l_, hi_r, first, False)
                mm(o, lo_l, hi_r, False, False)
                return mm(o, hi_l_, lo_r, False, last_)

            def layer1(g, e):
                pe.wait_ge(s("f_xl"), g + 1)
                freed(pe, s("f_full1"), g * 6 + e - 1 if e else g * 6)
                for o in range(2):
                    f = slice(o * 128, (o + 1) * 128)
                    for c in range(2):
                        last = exact(pt(4 - 3 * (e % 2))[:, o, :], w_lo[:, 0, e, c, f], w_hi[:, 0, e, c, f],
                                     x_hl[1][:, c, :], x_hl[0][:, c, :], c == 0, c == 1)
                last.then_inc(s("f_h1_ps"), 1)

            def layer2(g, e):
                pe.wait_ge(s("f_lo1"), g * 6 + e + 1)
                freed(pe, s("f_full2"), g * 6 + e)
                h_hi, h_lo = h1_hl[e % 2]
                for o in range(2):
                    f = slice(o * 128, (o + 1) * 128)
                    for c in range(2):
                        last = exact(pt(5)[:, o, :], w_lo[:, 1, e, c, f], w_hi[:, 1, e, c, f],
                                     h_lo[:, c, :], h_hi[:, c, :], c == 0, c == 1)
                last.then_inc(s("f_h2_ps"), 1)

            def layer3(g, e):
                pe.wait_ge(s("f_lo2"), g * 6 + e + 1)
                if e % 2 == 0:
                    freed(pe, s("f_x2"), g * 6 + (e - 1) if e else g * 6)
                else:
                    freed(pe, s("f_x2"), g * 6 + (e - 1))
                h_hi, h_lo = h2_hl[e % 2]
                for j in range(2):
                    f = slice(j * R, (j + 1) * R)
                    for c in range(2):
                        last = exact(pr_(6 + e % 2)[:, j, :], h_lo[:, c, f], h_hi[:, c, f],
                                     w_lo[:, 2, e, c, :], w_hi[:, 2, e, c, :], c == 0, c == 1)
                last.then_inc(s("f_o"), 1)

            def experts(g, between):
                router(g)
                layer1(g, 0)
                logits(g)
                layer1(g, 1)
                between(agg_turn)
                layer2(g, 0)
                layer1(g, 2)
                layer2(g, 1)
                layer3(g, 0)
                weights_turn(g)
                layer1(g, 3)
                layer2(g, 2)
                biases(g)
                layer3(g, 1)
                layer1(g, 4)
                between(gnn)
                layer2(g, 3)
                layer1(g, 5)
                layer2(g, 4)
                layer3(g, 2)
                layer3(g, 3)
                layer2(g, 5)
                layer3(g, 4)
                between(norm_turn)
                layer3(g, 5)

            pe.wait_ge(s("summed"), STEPS)
            agg_turn(0)
            gnn(0)
            norm_turn(0)
            pe.wait_ge(s("w_lo"), 3)
            def body(i):
                experts(i, lambda f: f(i + 1))

            repeated(pe, GROUPS - 1, body)
            experts(GROUPS - 1, lambda f: None)

        @block.scalar
        def _(act):
            def ln_rstd(g, var_ready, ln_done, rstd_done, v, l, r):
                act.wait_ge(s(var_ready), g + 1)
                act.activation(l[:], v[:, :, 1], ACT.Ln).then_inc(s(ln_done), 1)
                act.wait_ge(s(ln_done), g + 1)
                act.activation(r[:], l[:], ACT.Exp, scale=-0.5).then_inc(s(rstd_done), 1)

            act.preload_act_table_set("natural_log_exp_and_others")
            def p1_a(g):
                ln_rstd(g, "var", "ln", "rstd", mv, lnv, rstd)

            def p1_b(g):
                act.wait_ge(s("p1_T"), g + 1)
                freed(act, s("p1_kv"), 2 * g)
                freed(act, s("p1_xnT_out"), g * 16)
                act.activation(p_xnT, pt(0), ACT.Copy).then_inc(s("p1_xnT"), 1)

            def p1_c(g):
                act.wait_ge(s("p1_s_ps"), g + 1)
                freed(act, s("p1_s_out"), g * 32)
                act.activation(p_s, bank[1][0:2, 0:GROUP], ACT.Copy).then_inc(s("p1_s"), 1)

            def p1_d(g):
                for j in range(2):
                    act.wait_ge(s("p1_min"), 2 * g + j + 1)
                    act.activation(p_exp[:, j], p_min[:, j], ACT.Exp).then_inc(s("p1_exp"), 1)

            p1_a(0)
            p1_b(0)
            p1_c(0)
            def body(i):
                p1_a(i + 1)
                p1_b(i + 1)
                p1_d(i)
                p1_c(i + 1)

            repeated(act, GROUPS - 1, body)
            p1_d(GROUPS - 1)

            def m_queries(g):
                act.wait_ge(s("m_min"), 2 * (g + 1))
                freed(act, s("m_o_ps"), g)
                act.activation(m_e, m_q, ACT.Exp).then_inc(s("m_exp"), 1)
                freed(act, s("m_phi"), g)
                for o in range(2):
                    act.activation(m_r[:, o], pt(0)[:, o], ACT.Relu, bias=bq_c[:, o:o + 1]).then_inc(s("m_qread"), 1)

            def m_norm(g):
                ln_rstd(GROUPS + g, "var", "ln", "rstd", mv, lnv, rstd)

            def m_turn(g):
                act.wait_ge(s("m_T"), g + 1)
                freed(act, s("m_h"), g * 8)
                act.activation(m_yT, pt(2), ACT.Copy).then_inc(s("m_yT"), 1)

            def m_hidden(g, o2):
                for h in range(2):
                    f = 2 * o2 + h
                    act.wait_ge(s("m_h"), g * 8 + f + 1)
                    freed(act, s("m_d"), 2 * g)
                    act.activation(m_h[:, f], bank[5 + h][:, 0:GROUP], ACT.Relu,
                                   bias=b1_c[:, f:f + 1]).then_inc(s("m_hread"), 1)

            def m_norm2(g):
                ln_rstd(g, "m_var2", "m_ln2", "m_rstd2", mv2, lnv2, rstd2)

            def body(i, more=True):
                if not (isinstance(i, int) and i == 0):
                    m_norm2(i - 1)
                m_hidden(i, 0)
                m_hidden(i, 1)
                if more:
                    m_queries(i + 1)
                for o2 in range(2, 4):
                    m_hidden(i, o2)
                if more:
                    m_norm(i + 1)
                    m_turn(i + 1)

            def self_copy(i):
                act.wait_ge(s("l_self_ps"), i + 1)
                freed(act, s("self_out"), 16 * i)
                act.activation(l_self, pr_(0), ACT.Copy).then_inc(s("l_self"), 1)

            repeated(act, GROUPS, self_copy)
            act.wait_ge(s("w2_in"), 16 * LOADS_MIX)
            m_queries(0)
            act.wait_ge(s("soft_v"), 3)
            act.activation(t_l, e_l, ACT.Exp).then_inc(s("p_exp"), 1)
            m_norm(0)
            m_turn(0)
            repeated(act, GROUPS - 1, body)
            body(GROUPS - 1, False)
            m_norm2(GROUPS - 1)

            def f_first(g):
                act.wait_ge(s("f_T"), g + 1)
                freed(act, s("f_gnn"), g)
                act.activation(f_aT, pt(0), ACT.Copy).then_inc(s("f_aT"), 1)

            def f_norm(g):
                ln_rstd(2 * GROUPS + g, "var", "ln", "rstd", mv, lnv, rstd)

            def f_second(g):
                act.wait_ge(s("f_T1"), g + 1)
                freed(act, s("f_h1_ps"), 6 * g)
                freed(act, s("f_rh_ps"), g)
                freed(act, s("f_xl"), g)
                act.activation(f_xT, pt(1), ACT.Copy).then_inc(s("f_xT"), 1)
                act.wait_ge(s("f_xT"), g + 1)
                act.activation(x_hl[0][:], f_xT, ACT.Copy).then_inc(s("f_xh"), 1)

            def f_router(g):
                act.wait_ge(s("f_rh_ps"), g + 1)
                act.activation(f_rh, bank[3][:, 0:GROUP], ACT.Relu, bias=rb1_c[:]).then_inc(s("f_rh"), 1)

            def f_soft(g):
                act.wait_ge(s("f_nmx"), g + 1)
                for j in range(2):
                    act.activation(pr[:, j, 0:EXPERTS], lg[:, j, 0:EXPERTS], ACT.Exp, bias=rt[:, 0, j:j + 1],
                                   accum_out=rt[:, 1, j:j + 1]).then_inc(s("f_sum"), 1)

            def f_soft2(g):
                act.wait_ge(s("f_dif"), g + 1)
                act.activation(rt[:, 4, :], rt[:, 3, :], ACT.Exp).then_inc(s("f_e2"), 1)

            def f_wT_copy(g):
                act.wait_ge(s("f_wT_ps"), g + 1)
                freed(act, s("f_bias"), g)
                act.activation(f_wT, bank[3][0:EXPERTS, 0:GROUP], ACT.Copy).then_inc(s("f_wTc"), 1)

            def relu1(g, e):
                act.wait_ge(s("f_h1_ps"), g * 6 + e + 1)
                freed(act, s("f_lo1"), g * 6 + e - 1 if e else g * 6)
                for o in range(2):
                    ins = act.activation(f_h1[e % 2][:, o], pt(4 - 3 * (e % 2))[:, o], ACT.Relu, bias=eb_c[:, 0, e, o:o + 1])
                ins.then_inc(s("f_full1"), 1)
                act.wait_ge(s("f_full1"), g * 6 + e + 1)
                freed(act, s("f_h2_ps"), g * 6 + e - 1 if e else g * 6)
                act.activation(h1_hl[e % 2][0][:], f_h1[e % 2], ACT.Copy).then_inc(s("f_hi1"), 1)

            def relu2(g, e):
                act.wait_ge(s("f_h2_ps"), g * 6 + e + 1)
                freed(act, s("f_lo2"), g * 6 + e - 1 if e else g * 6)
                for o in range(2):
                    ins = act.activation(f_h2[e % 2][:, o], pt(5)[:, o], ACT.Relu, bias=eb_c[:, 1, e, o:o + 1])
                ins.then_inc(s("f_full2"), 1)
                act.wait_ge(s("f_full2"), g * 6 + e + 1)
                freed(act, s("f_o"), g * 6 + e - 1 if e else g * 6)
                act.activation(h2_hl[e % 2][0][:], f_h2[e % 2], ACT.Copy).then_inc(s("f_hi2"), 1)

            def f_experts(g, between):
                f_router(g)
                relu1(g, 0)
                f_soft(g)
                relu1(g, 1)
                between(f_first)
                f_soft2(g)
                relu2(g, 0)
                relu1(g, 2)
                relu2(g, 1)
                f_wT_copy(g)
                relu1(g, 3)
                relu2(g, 2)
                relu1(g, 4)
                relu2(g, 3)
                relu1(g, 5)
                between(f_norm)
                relu2(g, 4)
                relu2(g, 5)
                between(f_second)

            act.wait_ge(s("wexp_in"), 16 * LOADS_LATE)
            act.wait_ge(s("stepped"), STEPS)
            act.wait_ge(s("m_d"), 2 * GROUPS)
            for l in range(3):
                act.activation(w_hi[:, l], wexpv[:, l], ACT.Copy).then_inc(s("w_hi"), 1)
            f_first(0)
            f_norm(0)
            f_second(0)
            def body(i):
                f_experts(i, lambda f: f(i + 1))

            repeated(act, GROUPS - 1, body)
            f_experts(GROUPS - 1, lambda f: None)

        @block.vector
        def _(v):
            t = Own(v, s("tab_own"), 0, 0)

            def statistics(own, z, st_, mv_):
                for j in range(2):
                    own.did(v.bn_stats(st_[:, j, :], z[:, j, :]))
                own.settle()
                apart(v, "past")
                for j in range(2):
                    own.did(v.bn_aggr(mv_[:, j, :], st_[:, j, :]))
                own.settle()
                return v.tensor_scalar(mv_[:, :, 1], mv_[:, :, 1], EPS, None, ALU.add)

            def p1_norm(g):
                own = Own(v, s("p1a_own"), 4, g)
                v.wait_ge(s("p1_x"), 16 * (g + 1))
                statistics(own, p_x, st, mv).then_inc(s("var"), 1)
                v.wait_ge(s("rstd"), g + 1)
                freed(v, s("p1_T"), g)
                freed(v, s("p1_xn_out"), 16 * g)
                for j in range(2):
                    ins = v.tensor_scalar(p_xn[:, j], p_x[:, j], mv[:, j, 0:1], rstd[:, j:j + 1], ALU.subtract, ALU.mult)
                ins.then_inc(s("p1_xn"), 1)
                own.end()

            def p1_kv(g):
                own = Own(v, s("p1b_own"), 2, g)
                for j in range(2):
                    v.wait_ge(s("p1_kv"), 2 * g + j + 1)
                    own.did(v.tensor_tensor(p_k[:, j], bank[2 + j][0:R, 0:D], bkv_bc[:, 0:D], ALU.add))
                    freed(v, s("p1_sum"), 2 * g)
                    v.tensor_tensor(p_v[j][:, :, 0:128],
                                    bank[2 + j][0:R, D:2 * D].rearrange("p (c n) -> p c n", c=2),
                                    bkv_bc[:, D:2 * D].rearrange("p (c n) -> p c n", c=2),
                                    ALU.add).then_inc(s("p1_kv_read"), 1)
                    own.settle()
                    v.tensor_scalar(p_min[:, j], p_k[:, j], 0.0, None, ALU.min).then_inc(s("p1_min"), 1)
                for j in range(2):
                    v.wait_ge(s("p1_exp"), 2 * g + j + 1)
                    v.scalar_tensor_tensor(p_phi[:, j], p_k[:, j], 0.0, p_exp[:, j], ALU.max,
                                           ALU.add).then_inc(s("p1_phi"), 1)
                own.end()

            v.wait_ge(s("dlast_in"), 16)
            v.wait_ge(s("iota_tabs"), 3)
            t.did(v.tensor_scalar(tab_t[:, 0, :], dlast[:], -float((R - 1) // 2), 1.0 / R, ALU.add, ALU.mult))
            t.settle()
            t.did(v.tensor_scalar(tab_t[:, 1, :], tab_t[:, 0, :], ROUND, -ROUND, ALU.add, ALU.add))
            t.settle()
            v.tensor_tensor(tab_t[:, 1, :], tab_t[:, 1, :], iota_t[:], ALU.add).then_inc(s("tab_v"), 1)
            p1_norm(0)
            v.wait_ge(s("tab_ps"), 2)
            for c in range(CS):
                t.did(v.tensor_scalar(junk[0:QS, 0:PAIRS], bank[1][0:QS, 0:PAIRS], iota_s[:, c:c + 1], 0.0,
                                      ALU.is_lt, ALU.add, accum_out=tabs[:, 0, c:c + 1]))
                t.settle()
            t.did(v.tensor_scalar(tabs[:, 1, :], tabs[:, 0, :], float(PAIRS - 1), None, ALU.min))
            t.settle()
            t.did(v.tensor_tensor(tabs[:, 2, :], iota_s[:], tabs[:, 1, :], ALU.subtract))
            t.did(v.tensor_copy(tab_i[:, 0, :], tabs[:, 1, :]))
            t.settle()
            t.did(v.tensor_scalar(tabs[:, 3, :], tabs[:, 2, :], float(BLOCKS - 1), None, ALU.min))
            t.did(v.tensor_scalar(tabs[:, 4, :], tabs[:, 2, :], float(R), None, ALU.mult))
            t.settle()
            v.tensor_copy(tab_i[:, 1, :], tabs[:, 3, :]).then_inc(s("tab_v"), 1)
            v.wait_ge(s("tab_ps"), 1)
            v.tensor_copy(u_s[:].rearrange("p c k -> p (c k)"), bank[0][:, 0:4]).then_inc(s("tab_v"), 1)
            v.memset(p_v[0][:, :, 128:129], 1.0).then_inc(s("v_ones"), 1)
            v.memset(p_v[1][:, :, 128:129], 1.0).then_inc(s("v_ones"), 1)
            v.wait_ge(s("w_in"), 16 * LOADS_EARLY)
            def p1_edges(g):
                for h in range(2):
                    v.wait_ge(s(f"attr_mul{h}"), g + 1)
                    v.tensor_reduce(ew_n[:, bass.ds((g * 2 + h) * CHUNK, CHUNK)], attr_s[:, h, :, 0:ED // (2 - h)], AX.X,
                                    ALU.add).then_inc(s(f"attr_used{h}"), 1)

            def body(i):
                p1_norm(i + 1)
                p1_kv(i)
                p1_edges(i)

            repeated(v, GROUPS - 1, body)
            p1_kv(GROUPS - 1)
            p1_edges(GROUPS - 1)
            v.wait_ge(s("kv_done"), 1)
            v.wait_ge(s("consts"), CONSTS)
            for c in range(2):
                v.tensor_tensor(kvbd[:, c, :], bank[7][:, c * 129:c * 129 + 128], bmask[:], ALU.mult).then_inc(s("kvbd"), 1)
                v.tensor_scalar(ksbd[:, c, :], bmask[:], bank[7][:, c * 129 + 128:c * 129 + 129], None,
                                ALU.mult).then_inc(s("kvbd"), 1)

            v.wait_ge(s("sd_in"), 16 * 2 * CS)
            v.tensor_copy(src_f, src_i).then_inc(s("l_done"), 1)
            t.did(v.tensor_copy(dst_f, dst_i))
            t.settle()
            for c in range(CS):
                e_ = slice(c * 2 * R, (c + 1) * 2 * R)
                ins = v.tensor_scalar(rel_l[:, e_], dst_f[:, e_], tabs[:, 4, c:c + 1], None, ALU.subtract)
                if c < CS - 1:
                    t.did(ins)
            ins.then_inc(s("l_done"), 1)
            v.wait_ge(s("l_done"), 2)
            t.settle()
            t.did(v.tensor_scalar(hi_l, src_f, -(LO - 1) / 2, 1.0 / LO, ALU.add, ALU.mult))
            t.settle()
            v.tensor_scalar(hi_l, hi_l, ROUND, -ROUND, ALU.add, ALU.add).then_inc(s("l_done"), 1)
            v.wait_ge(s("l_done"), 3)
            v.wait_ge(s("ew_out"), 16)
            v.scalar_tensor_tensor(lr_l[:, 0, :], hi_l, -float(LO), src_f, ALU.mult, ALU.add).then_inc(s("lr_done"), 1)
            v.tensor_copy(lr_l[:, 1, :], rel_l).then_inc(s("lr_done"), 1)
            for a in range(6):
                v.wait_ge(s("a_ps"), a + 1)
                to = (a_src, a_rel, a_hi)[a // 2]
                j0 = CS * (a % 2)
                v.tensor_copy(to[:, :, j0:j0 + CS].rearrange("p q j -> p j q"),
                              bank[1 + a][0:R, 0:CS * QS].rearrange("p (j q) -> p j q", q=QS)).then_inc(s("a_done"), 1)

            def parts(whole, part, sem):
                for k in range(PART):
                    v.tensor_copy(part(k), whole(0)).then_inc(s(sem), 1)
                    if k < PART - 1:
                        v.wait_ge(s(sem), k + 1)
                        t.did(v.tensor_copy(whole(1), part(k)))
                        t.settle()
                        t.did(v.tensor_tensor(whole(0), whole(0), whole(1), ALU.subtract))
                        t.settle()

            v.wait_ge(s("look_ps"), 1)
            t.did(v.tensor_copy(s1_t[:, 0, :], bank[7][:, 0:HIS]))
            t.settle()
            parts(lambda k: s1_t[:, k, :], lambda k: s1_p[:, k, :], "s1_parts")
            v.wait_ge(s("look_ps"), 2)
            t.did(v.tensor_copy(s2_t[:, 0, :], bank[0][0:R, 0:CS * QS]))
            t.settle()
            parts(lambda k: s2_t[:, k, :], lambda k: s2_p[:, :, k], "s2_parts")

            def select(i, h):
                own = Own(v, s("sel_own"), 4 * HS, i)
                own.k = 4 * h
                n = i * HS + h
                v.wait_ge(s("lr_used"), n + 1)
                v.wait_ge(s("away"), n + 1)
                freed(v, s("selected"), n)
                for a in range(2):
                    own.did(v.scalar_tensor_tensor(
                        sel[:, a * CS:(a + 1) * CS, :],
                        away[:, h, a * CS * HIS:(a + 1) * CS * HIS].rearrange("p (j n) -> p j n", n=HIS), 0.0,
                        bank[1 + 2 * h + a][0:R, 0:CS * HIS].rearrange("p (j n) -> p j n", n=HIS),
                        ALU.is_equal, ALU.mult))
                own.did(v.tensor_reduce(a_s[:, 1, :], bank[2 + 2 * h][0:R, CS * HIS:CS * HIS + PART * JS]
                                        .rearrange("p (j k) -> p j k", k=PART), AX.X, ALU.add))
                own.settle()
                own.did(v.tensor_reduce(a_s[:, 0, :], sel, AX.X, ALU.add))
                own.settle()
                v.tensor_tensor(a_u[:, bass.ds(n, 1), :].rearrange("p a j -> p (a j)"), a_s[:, 0, :], a_s[:, 1, :],
                                ALU.add).then_inc(s("selected"), 1)

            def one_hots(i, h):
                n = i * HS + h
                v.wait_ge(s(f"lr_in{h}"), i * 16 + 16)
                freed(v, s("lr_used"), n - HS + 1)
                v.tensor_scalar(lr_oh[h][:, 0:2 * LROW], lr_bc[h], iota_p[:], None, ALU.is_equal).then_inc(s("lr_oh"), 1)

            def body(i, more=True):
                one_hots(i, 2)
                select(i, 0)
                if more:
                    one_hots(i + 1, 0)
                select(i, 1)
                if more:
                    one_hots(i + 1, 1)
                select(i, 2)

            for h in range(HS):
                t.did(v.memset(lr_oh[h][:, 2 * LROW:], 0.0))
            t.settle()
            one_hots(0, 0)
            one_hots(0, 1)
            repeated(v, QS // HS - 1, body)
            body(QS // HS - 1, False)
            v.wait_ge(s("selected"), QS)

            def blocks_of(q):
                _, values = nc.values_load_multi_w_load_instructions(
                    blk_row[:, bass.ds(q * CS, CS)], engines=[mybir.EngineType.DVE], min_val=0, max_val=BLOCKS - 1,
                    skip_runtime_bounds_check_because="tab_i is clamped to BLOCKS - 1 and counts up from 0")
                return values

            def affine(own, z, mv_, rstd_, gain, bias, o, last_sem):
                for j in range(2):
                    own.did(v.tensor_scalar(z[:, j], z[:, j], mv_[:, j, 0:1], rstd_[:, j:j + 1], ALU.subtract, ALU.mult))
                own.settle()
                own.did(v.tensor_tensor(z, z, rv[:, gain:gain + 1, :].to_broadcast([R, 2, D]), ALU.mult))
                own.settle()
                v.tensor_tensor(o, z, rv[:, bias:bias + 1, :].to_broadcast([R, 2, D]), ALU.add).then_inc(s(last_sem), 1)

            def m_clip(g):
                v.wait_ge(s("m_q"), g + 1)
                freed(v, s("m_exp"), g)
                for o in range(2):
                    v.tensor_scalar(m_q[:, o], pt(0)[:, o], bq_c[:, o:o + 1], 0.0, ALU.add,
                                    ALU.min).then_inc(s("m_min"), 1)

            def m_sum(g):
                v.wait_ge(s("m_exp"), g + 1)
                v.wait_ge(s("m_qread"), 2 * g + 2)
                freed(v, s("m_nd"), g)
                v.tensor_tensor(m_n, m_e, m_r, ALU.add).then_inc(s("m_phi"), 1)

            def m_queries(g):
                m_clip(g)
                m_sum(g)

            def m_attention(g):
                own = Own(v, s("ma_own"), 2, g)
                v.wait_ge(s("m_nd"), g + 1)
                own.did(v.tensor_scalar(m_q, pt(1), 1e-6, None, ALU.add))
                own.settle()
                own.did(v.reciprocal(m_q, m_q))
                own.settle()
                freed(v, s("m_o_ps"), g)
                v.tensor_tensor(m_e, pt(2), m_q, ALU.mult).then_inc(s("m_att"), 1)
                own.end()

            def m_project(g):
                own = Own(v, s("mb_own"), 7, g)
                v.wait_ge(s("m_xn"), 16 * (g + 1))
                freed(v, s("m_T"), g)
                v.tensor_tensor(m_z, xn_in, rv[:, 0:1, :].to_broadcast([R, 2, D]), ALU.add).then_inc(s("m_xb"), 1)
                v.wait_ge(s("m_xb"), g + 1)
                v.wait_ge(s("m_o_ps"), g + 1)
                v.tensor_tensor(m_z, pr_(1), m_z, ALU.add).then_inc(s("m_z"), 1)
                v.wait_ge(s("m_z"), g + 1)
                statistics(own, m_z, st, mv).then_inc(s("var"), 1)
                v.wait_ge(s("rstd"), GROUPS + g + 1)
                affine(own, m_z, mv, rstd, 1, 2, m_y, "m_y")
                own.end()

            def m_keep(g):
                v.wait_ge(s("m_y"), g + 1)
                v.tensor_tensor(m_yb, m_y, rv[:, 3:4, :].to_broadcast([R, 2, D]), ALU.add).then_inc(s("m_yb"), 1)

            def m_last(g):
                own = Own(v, s("mc_own"), 7, g)
                v.wait_ge(s("m_d"), 2 * (g + 1))
                v.wait_ge(s("m_yb"), g + 1)
                v.tensor_tensor(m_z2, pr_(7), m_yb, ALU.add).then_inc(s("m_z2"), 1)
                v.wait_ge(s("m_z2"), g + 1)
                statistics(own, m_z2, st2, mv2).then_inc(s("m_var2"), 1)
                v.wait_ge(s("m_rstd2"), g + 1)
                v.wait_ge(s("m_stored"), 16 * (g + 1))
                affine(own, m_z2, mv2, rstd2, 4, 5, m_o, "m_out")
                own.end()

            x_ = t
            x_.did(v.tensor_scalar(t_l, rel_l, 0.0, None, ALU.is_ge))
            x_.settle()
            x_.did(v.scalar_tensor_tensor(valid, rel_l, float(R), t_l, ALU.is_lt, ALU.mult))
            x_.did(v.memset(reset[:, 0:1], 0.0))
            x_.did(v.memset(reset[:, LROW:LROW + 1], 0.0))
            x_.did(v.tensor_tensor(reset[:, 1:LROW], dst_f[:, 1:LROW], dst_f[:, 0:LROW - 1], ALU.not_equal))
            x_.settle()
            x_.did(v.tensor_scalar(reset[:, 1:LROW], reset[:, 1:LROW], -BIG, None, ALU.mult))
            v.wait_ge(s("soft_ps"), 1)
            v.wait_ge(s("ew_in"), 16 * CS)
            v.wait_ge(s("w2_in"), 16 * LOADS_MIX)
            for k in range(3):
                a, b = 4 * R * k, min(4 * R * (k + 1), LROW)
                ins = v.tensor_tensor(t_l[:, a:b], bank[k][0:QS, 0:b - a], ew_l[:, a:b], ALU.add)
                if k < 2:
                    x_.did(ins)
            ins.then_inc(s("soft_v"), 1)
            v.wait_ge(s("soft_v"), 1)
            x_.settle()
            x_.did(v.scalar_tensor_tensor(e_l, t_l, 0.01, t_l, ALU.mult, ALU.max))
            x_.settle()
            x_.did(v.tensor_tensor(e_l, e_l, valid, ALU.mult))
            x_.did(v.tensor_scalar(t_l, valid, BIG, -BIG, ALU.mult, ALU.add))
            x_.settle()
            x_.did(v.tensor_tensor(e_l, e_l, t_l, ALU.add))
            x_.settle()
            m_clip(0)

            def scans(first, last_, between=lambda: None):
                x_.did(v.tensor_tensor_scan(f_l, reset[:, 0:LROW], e_l, first, ALU.add, ALU.max))
                between()
                x_.settle()
                x_.did(v.tensor_tensor_scan(b_l[:, ::-1], reset[:, LROW:0:-1], f_l[:, ::-1], last_, ALU.add, ALU.max))
                x_.settle()

            scans(-BIG, -BIG, lambda: m_sum(0))
            v.tensor_copy(sm[:, 0:1], f_l[:, LROW - 1:LROW]).then_inc(s("summary"), 1)
            v.tensor_copy(sm[:, 1:2], b_l[:, 0:1]).then_inc(s("summary"), 1)
            v.tensor_tensor(sm[:, 2:3], dst_f[:, 0:1], dst_f[:, LROW - 1:LROW], ALU.is_equal).then_inc(s("summary"), 1)
            v.tensor_copy(sm[:, 3:4], dst_f[:, 0:1]).then_inc(s("summary"), 1)
            v.tensor_copy(sm[:, 4:5], dst_f[:, LROW - 1:LROW]).then_inc(s("summary"), 1)
            v.wait_ge(s("soft_ps"), 2)
            x_.did(v.tensor_copy(smr[:, 0:5, 0:QS], bank[3][0:1, 0:5 * QS].rearrange("p (k q) -> p k q", q=QS)))
            x_.did(v.memset(smr[:, 5:7, 0:QS], -BIG))
            x_.settle()
            row = lambda k, a, b: smr[:, k, a:b]
            x_.did(v.tensor_tensor(row(7, 1, QS), row(3, 1, QS), row(4, 0, QS - 1), ALU.is_equal))
            x_.settle()
            x_.did(v.tensor_scalar(row(8, 1, QS), row(7, 1, QS), BIG, -BIG, ALU.mult, ALU.add))
            x_.did(v.tensor_tensor(row(9, 1, QS), row(7, 1, QS), row(2, 0, QS - 1), ALU.mult))
            x_.did(v.tensor_tensor(row(10, 1, QS), row(7, 1, QS), row(2, 1, QS), ALU.mult))
            x_.settle()
            x_.did(v.tensor_scalar(row(9, 1, QS), row(9, 1, QS), BIG, -BIG, ALU.mult, ALU.add))
            x_.did(v.tensor_scalar(row(10, 1, QS), row(10, 1, QS), BIG, -BIG, ALU.mult, ALU.add))
            x_.did(v.tensor_tensor(row(0, 0, QS - 1), row(0, 0, QS - 1), row(8, 1, QS), ALU.add))
            x_.did(v.tensor_tensor(row(1, 1, QS), row(1, 1, QS), row(8, 1, QS), ALU.add))
            x_.settle()
            x_.did(v.tensor_tensor_scan(row(5, 1, QS), row(9, 1, QS), row(0, 0, QS - 1), -BIG, ALU.add, ALU.max))
            v.tensor_tensor_scan(smr[:, 6, QS - 2::-1], smr[:, 10, QS - 1:0:-1], smr[:, 1, QS - 1:0:-1], -BIG,
                                 ALU.add, ALU.max).then_inc(s("soft_v"), 1)
            m_attention(0)
            v.wait_ge(s("soft_ps"), 3)
            x_.did(v.tensor_copy(sm[:, 5:7], bank[4][0:QS, 0:2]))
            x_.settle()
            scans(sm[:, 5:6], sm[:, 6:7])
            v.tensor_tensor(e_l, e_l, b_l, ALU.subtract).then_inc(s("soft_v"), 1)
            m_project(0)
            v.wait_ge(s("p_exp"), 1)
            v.tensor_tensor(t_l, t_l, valid, ALU.mult).then_inc(s("soft_v"), 1)
            v.wait_ge(s("soft_ps"), 4)
            for a in range(2):
                x_.did(v.tensor_copy(a_p[:, :, CS * a:CS * a + CS].rearrange("p q j -> p j q"),
                                     bank[5 + a][0:R, 0:CS * QS].rearrange("p (j q) -> p j q", q=QS)))
            v.memset(mark[:], 0.0).then_inc(s("soft_v"), 1)
            x_.settle()

            def one_hot(i, z):
                q = i * HS + z // CS
                for k in range(2):
                    at = lambda a: a[:, bass.ds(q, 1), 2 * (z % CS) + k:2 * (z % CS) + k + 1].rearrange("p a b -> p (a b)")
                    v.tensor_scalar(onehot[:, 2 * (z % CS) + k, :], iota_r[:], at(a_rel), at(a_p), ALU.is_equal,
                                    ALU.mult).then_inc(s("onehot"), 1)

            def steps(i, h):
                at = blocks_of(i * HS + h)
                for c in range(CS):
                    z = h * CS + c
                    n = i * ZS + z
                    v.wait_ge(s("stepped"), n + 1)
                    freed(v, s("summed"), n)
                    to = accv[:, bass.ds(at[c], 1), :].rearrange("p b n -> p (b n)")
                    v.tensor_tensor(to, bank[3 + z % 2][0:R, 0:D + 1], to, ALU.add).then_inc(s("summed"), 1)
                    if h + 1 < HS:
                        one_hot(i, z + CS)
                    elif not (isinstance(i, int) and i == GROUPS - 1):
                        one_hot(i + 1, c)

            def body(i, more=True):
                if not (isinstance(i, int) and i == 0):
                    m_last(i - 1)
                m_keep(i)
                if more:
                    m_queries(i + 1)
                steps(i, 0)
                if more:
                    m_attention(i + 1)
                steps(i, 1)
                if more:
                    m_project(i + 1)
                steps(i, 2)

            v.wait_ge(s("soft_v"), 5)
            v.memset(mark[:], 0.0).then_inc(s("m_stored"), 16)
            v.wait_ge(s("blk_in"), 16)
            for z in range(CS):
                one_hot(0, z)
            x_.did(v.memset(acc[:, 2 * (LROW + 4):3 * (LROW + 4)], 0.0))
            x_.did(v.memset(acc[:, 5 * (LROW + 4):7 * (LROW + 4)], 0.0))
            x_.settle()
            v.wait_ge(s("soft_in"), 3)
            repeated(v, GROUPS - 1, body)
            body(GROUPS - 1, False)
            m_last(GROUPS - 1)
            v.wait_ge(s("summed"), STEPS)

            v.memset(lg[:], -BIG).then_inc(s("pads"), 1)
            v.memset(pr[:], -1.0).then_inc(s("pads"), 1)
            v.wait_ge(s("pads"), 2)

            def f_mean(g):
                own = Own(v, s("fa_own"), 4, g)
                den = acc[:].rearrange("p (g j n) -> p g j n", j=2, n=D + 1)[:, bass.ds(g, 1), :, D]
                den = den.rearrange("p g j -> p (g j)")
                freed(v, s("f_x1"), g)
                own.did(v.tensor_scalar(dn[:, 0, :], den, 0.5, None, ALU.max))
                own.did(v.tensor_scalar(dn[:, 1, :], den, 0.0, None, ALU.is_gt))
                own.settle()
                own.did(v.reciprocal(dn[:, 0, :], dn[:, 0, :]))
                own.did(v.tensor_scalar(dn[:, 2, :], dn[:, 1, :], -1.0, 1.0, ALU.mult, ALU.add))
                own.settle()
                freed(v, s("f_T"), g)
                for j in range(2):
                    a = acc[:].rearrange("p (g j n) -> p g j n", j=2, n=D + 1)[:, bass.ds(g, 1), j, 0:D]
                    v.tensor_scalar(f_an[:, j], a.rearrange("p g n -> p (g n)"), dn[:, 0, j:j + 1], None,
                                    ALU.mult).then_inc(s("f_an"), 1)
                own.end()

            def f_rows1(g):
                own = Own(v, s("fb_own"), 5, g)
                v.wait_ge(s("f_pre"), 7 * (g + 1))
                v.wait_ge(s("f_gnn"), g + 1)
                own.did(v.scalar_tensor_tensor(f_t[:, 0], pr_(2)[:, 0], dn[:, 1, 0:1], f_t[:, 0], ALU.mult, ALU.add))
                v.scalar_tensor_tensor(f_t[:, 1], pr_(2)[:, 1], dn[:, 1, 1:2], f_t[:, 1], ALU.mult,
                                       ALU.add).then_inc(s("f_r"), 1)
                v.wait_ge(s("f_r"), g + 1)
                own.settle()
                freed(v, s("f_start"), 2 * g)
                v.scalar_tensor_tensor(f_x1, f_t, 0.0, f_x, ALU.max, ALU.add).then_inc(s("f_x1"), 1)
                v.wait_ge(s("f_x1"), g + 1)
                statistics(own, f_x1, st, mv).then_inc(s("var"), 1)
                own.end()

            def f_rows2(g):
                v.wait_ge(s("rstd"), 2 * GROUPS + g + 1)
                for j in range(2):
                    v.tensor_scalar(f_t[:, j], f_x1[:, j], mv[:, j, 0:1], rstd[:, j:j + 1], ALU.subtract,
                                    ALU.mult).then_inc(s("f_xn1"), 1)

            def f_route1(g):
                own = Own(v, s("fc_own"), 2, g)
                v.wait_ge(s("f_lg_ps"), g + 1)
                own.did(v.tensor_tensor(lg[:, :, 0:EXPERTS],
                                        bank[3][0:R, 256:272].rearrange("p (j n) -> p j n", j=2)[:, :, 0:EXPERTS],
                                        rb2_bc[:, None, :].to_broadcast([R, 2, EXPERTS]), ALU.add))
                own.settle()
                own.did(v.tensor_reduce(rt[:, 2, :], lg[:], AX.X, ALU.max))
                own.settle()
                v.tensor_scalar(rt[:, 0, :], rt[:, 2, :], -1.0, None, ALU.mult).then_inc(s("f_nmx"), 1)
                own.end()

            def f_route2(g):
                own = Own(v, s("fd_own"), 8, g)
                v.wait_ge(s("f_sum"), 2 * (g + 1))
                own.did(v.reciprocal(rt[:, 2, :], rt[:, 1, :]))
                own.settle()
                for j in range(2):
                    own.did(v.tensor_scalar(pr[:, j, 0:EXPERTS], pr[:, j, 0:EXPERTS], rt[:, 2, j:j + 1], None, ALU.mult))
                own.settle()
                apart(v, "past")
                for j in range(2):
                    own.did(v.max(top[:, j, :], pr[:, j, :]))
                own.settle()
                apart(v, "past")
                for j in range(2):
                    own.did(v.max_index(topi[:, j, :], top[:, j, :], pr[:, j, :]))
                v.tensor_tensor(rt[:, 3, :], top[:, :, 1], top[:, :, 0], ALU.subtract).then_inc(s("f_dif"), 1)
                own.settle()
                own.did(v.tensor_copy(topf[:], topi[:, :, 0:2]))
                own.end()

            def f_route3(g):
                own = Own(v, s("fe_own"), 7, g)
                v.wait_ge(s("f_e2"), g + 1)
                own.did(v.tensor_scalar(rt[:, 5, :], rt[:, 4, :], 1.0, None, ALU.add))
                own.settle()
                own.did(v.reciprocal(rt[:, 6, :], rt[:, 5, :]))
                own.settle()
                own.did(v.tensor_tensor(rt[:, 7, :], rt[:, 6, :], rt[:, 4, :], ALU.mult))
                own.settle()
                for j in range(2):
                    own.did(v.tensor_scalar(wt1[:, j], iota_e[:], topf[:, j, 0:1], rt[:, 6, j:j + 1], ALU.is_equal, ALU.mult))
                    own.did(v.tensor_scalar(wt2[:, j], iota_e[:], topf[:, j, 1:2], rt[:, 7, j:j + 1], ALU.is_equal, ALU.mult))
                own.settle()
                v.tensor_tensor(wt[:], wt1[:], wt2[:], ALU.add).then_inc(s("f_wt"), 1)
                own.end()

            def low(sem_hi, sem_used, sem, full, hi_lo, n, used):
                v.wait_ge(s(sem_hi), n + 1)
                freed(v, s(sem_used), used)
                v.tensor_tensor(hi_lo[1][:], full, hi_lo[0][:].bitcast(F32), ALU.subtract).then_inc(s(sem), 1)

            def f_low0(g):
                low("f_xh", "f_h1_ps", "f_xl", f_xT, x_hl, g, 6 * g)

            def f_low1(g, e):
                low("f_hi1", "f_h2_ps", "f_lo1", f_h1[e % 2], h1_hl[e % 2], g * 6 + e, g * 6 + e - 1 if e else g * 6)

            def f_low2(g, e):
                low("f_hi2", "f_o", "f_lo2", f_h2[e % 2], h2_hl[e % 2], g * 6 + e, g * 6 + e - 1 if e else g * 6)

            def f_begin(g):
                v.wait_ge(s("f_bias"), g + 1)
                freed(v, s("f_stored"), 16 * g)
                for j in range(2):
                    v.tensor_tensor(f_x2[:, j], pr_(2)[:, j], f_x1[:, j], ALU.add).then_inc(s("f_start"), 1)
                v.wait_ge(s("f_start"), 2 * (g + 1))

            def f_add(g, e):
                v.wait_ge(s("f_o"), g * 6 + e + 1)
                if e:
                    v.wait_ge(s("f_x2"), g * 6 + e)
                for j in range(2):
                    ins = v.scalar_tensor_tensor(f_x2[:, j], pr_(6 + e % 2)[:, j], wt[:, j, e:e + 1], f_x2[:, j],
                                                 ALU.mult, ALU.add)
                ins.then_inc(s("f_x2"), 1)

            def f_experts(g, between):
                between(f_mean)
                f_route1(g)
                f_low1(g, 0)
                f_route2(g)
                f_low1(g, 1)
                f_route3(g)
                f_low2(g, 0)
                f_low1(g, 2)
                f_low2(g, 1)
                f_low1(g, 3)
                f_low2(g, 2)
                f_begin(g)
                f_add(g, 0)
                f_low1(g, 4)
                f_add(g, 1)
                between(f_rows1)
                f_low2(g, 3)
                f_low1(g, 5)
                between(f_rows2)
                f_low2(g, 4)
                f_add(g, 2)
                f_add(g, 3)
                f_low2(g, 5)
                between(f_low0)
                f_add(g, 4)
                f_add(g, 5)

            f_mean(0)
            for l in range(3):
                v.wait_ge(s("w_hi"), l + 1)
                v.tensor_tensor(w_lo[:, l], wexpv[:, l], w_hi[:, l].bitcast(F32), ALU.subtract).then_inc(s("w_lo"), 1)
            f_rows1(0)
            f_rows2(0)
            f_low0(0)
            def body(i):
                f_experts(i, lambda f: f(i + 1))

            repeated(v, GROUPS - 1, body)
            f_experts(GROUPS - 1, lambda f: None)


_INS = ["x", "src", "dst", "attr", "wselfT", "wfuncT", "wfunc", "att_nodes", "att_edge", "wq", "wk", "wv", "wo",
        "w1", "w2", "bq", "b1", "bkv", "rowvecs", "rw1", "rb1", "rw2", "rb2", "ew1", "ew2", "ew3", "eb1", "eb2", "eb3"]


def lay_out(i):
    import numpy as np

    a = {k: np.asarray(v) for k, v in i.items()}
    c = np.ascontiguousarray
    col = lambda b: c(b.reshape(-1, 128).T)
    return dict(
        x=a["x"], src=a["src"], dst=a["dst"], attr=a["edge_attr_64"],
        wselfT=c(a["L0_gnn_W_self"].T), wfuncT=c(a["L0_gnn_W_func"].T), wfunc=a["L0_gnn_W_func"],
        att_nodes=c(a["L0_gnn_W_att"][0, :2 * D].reshape(2, 2, 128).transpose(2, 1, 0)),
        att_edge=c(a["L0_gnn_W_att"][:, 2 * D:]),
        wq=a["L0_mix_Wq"], wk=a["L0_mix_Wk"], wv=a["L0_mix_Wv"], wo=a["L0_mix_Wo"], w1=a["L0_mix_W1"], w2=a["L0_mix_W2"],
        bq=col(a["L0_mix_bq"]), b1=col(a["L0_mix_b1"]),
        bkv=c(np.concatenate([a["L0_mix_bk"], a["L0_mix_bv"]])[None]),
        rowvecs=c(np.stack([a["L0_mix_" + k] for k in ("bo", "ln1_g", "ln1_b", "b2", "ln2_g", "ln2_b")])),
        rw1=a["L0_ffn_router_w1"], rb1=col(a["L0_ffn_router_b1"]), rw2=a["L0_ffn_router_w2"], rb2=a["L0_ffn_router_b2"][None],
        ew1=a["L0_ffn_expert_w1"], ew2=a["L0_ffn_expert_w2"], ew3=a["L0_ffn_expert_w3"],
        eb1=c(a["L0_ffn_expert_b1"].reshape(EXPERTS, 2, 128).transpose(2, 0, 1)),
        eb2=c(a["L0_ffn_expert_b2"].reshape(EXPERTS, 2, 128).transpose(2, 0, 1)), eb3=a["L0_ffn_expert_b3"],
    )


def kernel(**inputs):
    import concourse.bacc as bacc
    from concourse.bass_utils import run_bass_kernel_spmd as run

    arrays = lay_out(inputs)
    nc = bacc.Bacc("TRN2", target_bir_lowering=False, num_devices=1)
    args = [nc.dram_tensor(f"in_{n}", arrays[n].shape, mybir.dt.from_np(arrays[n].dtype), kind="ExternalInput").ap()
            for n in _INS]
    out = nc.dram_tensor("out_0", (N, D), F32, kind="ExternalOutput").ap()
    build(nc, *args, out)
    r = run(nc, [{f"in_{n}": arrays[n] for n in _INS}], core_ids=[0])
    return r.results[0]["out_0"]
```
